# Optimizing a Trainium2 kernel written in Bass

```python
import numpy as np
import jax
import jax.numpy as jnp

def _softmax(x, axis=-1):
    return jax.nn.softmax(x, axis=axis)

def _gelu(x):
    return jax.nn.gelu(x, approximate=True)

def _silu(x):
    return jax.nn.silu(x)

def _sigmoid(x):
    return jax.nn.sigmoid(x)

def _layernorm(x, axis=-1, eps=1e-05):
    m = jnp.mean(x, axis=axis, keepdims=True)
    v = jnp.var(x, axis=axis, keepdims=True)
    return (x - m) / jnp.sqrt(v + eps)

def _scatter_add(tgt, idx, src, axis=0):
    return tgt.at[idx].add(src)

def _segment_sum(src, seg, n):
    return jax.ops.segment_sum(src, seg, n)
kernel_name = 'mk_lm_tower_d1_tok_ids256_r4_7fa771'

def setup_inputs(seed: int=0):
    np.random.seed(seed)
    _w = jnp.asarray

    def _rec_inputs():
        import jax
        import jax.numpy as jnp
        _rk = jax.random.key(seed)
        x = jax.random.randint(jax.random.fold_in(_rk, 1), (64, 256), 0, 4360, jnp.int32)
        return x
    x = _rec_inputs()

    def _L0_tok_setup():
        import jax, jax.numpy as jnp
        import numpy as np
        VOCAB = 4360
        PROJ = 64
        PAD_IDX = 0
        key = jax.random.key(seed)
        k1, k2 = jax.random.split(key)
        x = jax.random.randint(k1, (64, 512), 0, VOCAB, dtype=jnp.int64)
        W = jax.random.normal(k2, (PROJ, VOCAB), dtype=jnp.float32) * 0.02
        return {'x': x, 'W': W}
    _L0_tok_all = _L0_tok_setup()
    _L0_tok_in = {k: v for k, v in _L0_tok_all.items() if k in ('W',)}
    del _L0_tok_all

    def _L0_attn_setup():
        import jax, jax.numpy as jnp
        import numpy as np
        key = jax.random.key(seed)
        k1, k2 = jax.random.split(key)
        B, N, D = (4, 1024, 64)
        inp = jax.random.normal(k1, (B, N, D), dtype=jnp.float32)
        q_weight = jax.random.normal(k2, (D, D), dtype=jnp.float32)
        return {'input': inp, 'q_weight': q_weight}
    _L0_attn_all = _L0_attn_setup()
    _L0_attn_in = {k: v for k, v in _L0_attn_all.items() if k in ('q_weight',)}
    del _L0_attn_all

    def _L0_ffn_setup():
        import jax, jax.numpy as jnp
        import numpy as np
        B, N, D = (16, 1024, 64)
        NUM_EXPERTS, TOP_K, HEADS = (4, 2, 4)
        N_EDGES = 262144
        LN_EPS = 1e-05

        def _layernorm(x, g, b):
            mu = x.mean(-1, keepdims=True)
            var = ((x - mu) ** 2).mean(-1, keepdims=True)
            return (x - mu) * jax.lax.rsqrt(var + LN_EPS) * g + b

        def _forward(x, edge_index, W_gat, att_src, att_dst, b_gat, ln_gamma, ln_beta, W1, b1, W2, b2):
            Bc, Nc, Dc = x.shape
            M = Bc * Nc
            x_flat = x.reshape(M, Dc)
            h = (x_flat @ W_gat).reshape(M, HEADS, NUM_EXPERTS)
            loops = jnp.arange(M, dtype=edge_index.dtype)
            src = jnp.concatenate([edge_index[0], loops])
            dst = jnp.concatenate([edge_index[1], loops])
            a_src = (h * att_src).sum(-1)
            a_dst = (h * att_dst).sum(-1)
            e = jax.nn.leaky_relu(a_src[src] + a_dst[dst], negative_slope=0.2)
            e_max = jax.ops.segment_max(e, dst, num_segments=M)
            ee = jnp.exp(e - e_max[dst])
            denom = jax.ops.segment_sum(ee, dst, num_segments=M)
            alpha = ee / (denom[dst] + 1e-16)
            msg = h[src] * alpha[:, :, None]
            agg = jax.ops.segment_sum(msg, dst, num_segments=M).reshape(M, HEADS * NUM_EXPERTS) + b_gat
            scores = _layernorm(agg, ln_gamma, ln_beta).reshape(M, HEADS, NUM_EXPERTS).mean(1)
            scores = scores.reshape(Bc, Nc, NUM_EXPERTS)
            topk_s, topk_i = jax.lax.top_k(scores, TOP_K)
            w = jax.nn.softmax(topk_s, axis=-1)
            out = jnp.zeros_like(x)
            for ei in range(NUM_EXPERTS):
                g = jnp.where(topk_i == ei, w, 0.0).sum(-1)
                hh = jax.nn.gelu(x @ W1[ei] + b1[ei], approximate=False)
                out = out + g[..., None] * (hh @ W2[ei] + b2[ei])
            return out
        key = jax.random.key(seed)
        ks = jax.random.split(key, 8)
        s = 0.05
        return {'x': jax.random.normal(ks[0], (B, N, D), jnp.float32), 'W_gat': jax.random.normal(ks[1], (D, HEADS * NUM_EXPERTS), jnp.float32) * s, 'att_src': jax.random.normal(ks[2], (HEADS, NUM_EXPERTS), jnp.float32) * s, 'att_dst': jax.random.normal(ks[3], (HEADS, NUM_EXPERTS), jnp.float32) * s, 'b_gat': jnp.zeros((HEADS * NUM_EXPERTS,), jnp.float32), 'ln_gamma': jnp.ones((HEADS * NUM_EXPERTS,), jnp.float32), 'ln_beta': jnp.zeros((HEADS * NUM_EXPERTS,), jnp.float32), 'W1': jax.random.normal(ks[4], (NUM_EXPERTS, D, 2 * D), jnp.float32) * s, 'b1': jnp.zeros((NUM_EXPERTS, 2 * D), jnp.float32), 'W2': jax.random.normal(ks[5], (NUM_EXPERTS, 2 * D, D), jnp.float32) * s, 'b2': jnp.zeros((NUM_EXPERTS, D), jnp.float32), 'edge_index': jax.random.randint(ks[6], (2, N_EDGES), 0, B * N, jnp.int32)}
    _L0_ffn_all = _L0_ffn_setup()
    _L0_ffn_in = {k: v for k, v in _L0_ffn_all.items() if k in ('W_gat', 'att_src', 'att_dst', 'b_gat', 'ln_gamma', 'ln_beta', 'W1', 'b1', 'W2', 'b2', 'edge_index')}
    del _L0_ffn_all
    return {'x': x, 'L0_tok_W': _L0_tok_in['W'], 'L0_attn_q_weight': _L0_attn_in['q_weight'], 'L0_ffn_W_gat': _L0_ffn_in['W_gat'], 'L0_ffn_att_src': _L0_ffn_in['att_src'], 'L0_ffn_att_dst': _L0_ffn_in['att_dst'], 'L0_ffn_b_gat': _L0_ffn_in['b_gat'], 'L0_ffn_ln_gamma': _L0_ffn_in['ln_gamma'], 'L0_ffn_ln_beta': _L0_ffn_in['ln_beta'], 'L0_ffn_W1': _L0_ffn_in['W1'], 'L0_ffn_b1': _L0_ffn_in['b1'], 'L0_ffn_W2': _L0_ffn_in['W2'], 'L0_ffn_b2': _L0_ffn_in['b2'], 'L0_ffn_edge_index': _L0_ffn_in['edge_index']}

def reference(x, L0_tok_W, L0_attn_q_weight, L0_ffn_W_gat, L0_ffn_att_src, L0_ffn_att_dst, L0_ffn_b_gat, L0_ffn_ln_gamma, L0_ffn_ln_beta, L0_ffn_W1, L0_ffn_b1, L0_ffn_W2, L0_ffn_b2, L0_ffn_edge_index):
    import jax
    import jax.numpy as jnp

    def _L0_tok_ref(x, W):
        import jax, jax.numpy as jnp
        import numpy as np
        VOCAB = 4360
        PROJ = 64
        PAD_IDX = 0
        out = jnp.take(W.T, x, axis=0)
        mask = (x != PAD_IDX)[..., None]
        return jnp.where(mask, out, jnp.zeros((), dtype=out.dtype))

    def _L0_attn_ref(input, q_weight):
        import jax, jax.numpy as jnp
        import numpy as np
        query = jnp.einsum('bnd,de->bne', input, q_weight)
        att = jax.nn.sigmoid(jnp.einsum('bnd,bmd->bnm', query, input))
        value = jnp.einsum('bnm,bmd->bnd', att, input)
        return value

    def _L0_ffn_ref(x, W_gat, att_src, att_dst, b_gat, ln_gamma, ln_beta, W1, b1, W2, b2, edge_index):
        import jax, jax.numpy as jnp
        import numpy as np
        B, N, D = (16, 1024, 64)
        NUM_EXPERTS, TOP_K, HEADS = (4, 2, 4)
        N_EDGES = 262144
        LN_EPS = 1e-05

        def _layernorm(x, g, b):
            mu = x.mean(-1, keepdims=True)
            var = ((x - mu) ** 2).mean(-1, keepdims=True)
            return (x - mu) * jax.lax.rsqrt(var + LN_EPS) * g + b

        def _forward(x, edge_index, W_gat, att_src, att_dst, b_gat, ln_gamma, ln_beta, W1, b1, W2, b2):
            Bc, Nc, Dc = x.shape
            M = Bc * Nc
            x_flat = x.reshape(M, Dc)
            h = (x_flat @ W_gat).reshape(M, HEADS, NUM_EXPERTS)
            loops = jnp.arange(M, dtype=edge_index.dtype)
            src = jnp.concatenate([edge_index[0], loops])
            dst = jnp.concatenate([edge_index[1], loops])
            a_src = (h * att_src).sum(-1)
            a_dst = (h * att_dst).sum(-1)
            e = jax.nn.leaky_relu(a_src[src] + a_dst[dst], negative_slope=0.2)
            e_max = jax.ops.segment_max(e, dst, num_segments=M)
            ee = jnp.exp(e - e_max[dst])
            denom = jax.ops.segment_sum(ee, dst, num_segments=M)
            alpha = ee / (denom[dst] + 1e-16)
            msg = h[src] * alpha[:, :, None]
            agg = jax.ops.segment_sum(msg, dst, num_segments=M).reshape(M, HEADS * NUM_EXPERTS) + b_gat
            scores = _layernorm(agg, ln_gamma, ln_beta).reshape(M, HEADS, NUM_EXPERTS).mean(1)
            scores = scores.reshape(Bc, Nc, NUM_EXPERTS)
            topk_s, topk_i = jax.lax.top_k(scores, TOP_K)
            w = jax.nn.softmax(topk_s, axis=-1)
            out = jnp.zeros_like(x)
            for ei in range(NUM_EXPERTS):
                g = jnp.where(topk_i == ei, w, 0.0).sum(-1)
                hh = jax.nn.gelu(x @ W1[ei] + b1[ei], approximate=False)
                out = out + g[..., None] * (hh @ W2[ei] + b2[ei])
            return out
        return _forward(x, edge_index, W_gat, att_src, att_dst, b_gat, ln_gamma, ln_beta, W1, b1, W2, b2)
    h = _L0_tok_ref(x, L0_tok_W)
    h = h + _L0_attn_ref(_layernorm(h, axis=-1), L0_attn_q_weight)
    h = h + _L0_ffn_ref(_layernorm(h, axis=-1), L0_ffn_W_gat, L0_ffn_att_src, L0_ffn_att_dst, L0_ffn_b_gat, L0_ffn_ln_gamma, L0_ffn_ln_beta, L0_ffn_W1, L0_ffn_b1, L0_ffn_W2, L0_ffn_b2, L0_ffn_edge_index)
    return h

_drawn_inputs = setup_inputs


def setup_inputs(seed=0):
    import zlib

    import numpy as np

    out = dict(_drawn_inputs(seed))
    spreads = {'L0_ffn_b_gat': (0.0, 0.8),
     'L0_ffn_ln_gamma': (1.0, 0.6),
     'L0_ffn_ln_beta': (0.0, 0.8),
     'L0_ffn_b1': (0.0, 0.8),
     'L0_ffn_b2': (0.0, 0.8)}
    factors = {'L0_ffn_W_gat': 8.0,
     'L0_ffn_att_src': 8.0,
     'L0_ffn_att_dst': 8.0,
     'L0_ffn_W1': 8.0,
     'L0_ffn_W2': 8.0}
    for name, (base, spread) in spreads.items():
        noise = np.random.default_rng([zlib.crc32(name.encode()), seed]).standard_normal(out[name].shape)
        drawn = base * np.exp(spread * noise) if base else spread * noise
        out[name] = jnp.asarray(drawn.astype(out[name].dtype))
    for name, factor in factors.items():
        out[name] = (out[name] * factor).astype(out[name].dtype)
    return out
```

```python
from contextlib import ExitStack

import concourse.bass as bass
from concourse import mybir
import numpy as np

ALU = mybir.AluOpType
ACT = mybir.ActivationFunctionType
AX = mybir.AxisListType
F32 = mybir.dt.float32
BF16 = mybir.dt.bfloat16
I32 = mybir.dt.int32
U32 = mybir.dt.uint32

P = 128
BIG = 1.0e38
LN_EPS = 1e-5
DEN_EPS = 1e-16
SLOPE = 0.2

TAB_W = 32
SUM_W = 20
ROW_W = 24


def build(nc, tok, emb, qw, wgat, att_src, att_dst, b_gat, gamma, beta, w1, b1, w2, b2, esrc, edst, out):
    NB = tok.shape[1]
    NTOK = P * NB
    D = emb.shape[1]
    HE = wgat.shape[1]
    EX, HID = w1.shape[1], w1.shape[2]
    HD = HE // EX
    EB = esrc.shape[1]
    NSLOT = P * (EB + NB)
    LANE = NSLOT // P
    FLAG = NTOK
    BATCHES = NB // 2
    GRP = 4
    STEPS = EB // BATCHES // GRP
    HALF = STEPS // 2 * GRP
    CH = LANE // P
    assert (D, HE, EX, HID) == (64, 16, 4, 128) and NB == P and STEPS == 8
    assert CH == HALF + 1 and CH * P == LANE and HD * (EX + 1) == SUM_W

    srt = nc.dram_tensor("sorted_sources", [NSLOT, 1], I32, kind="Internal").ap()
    table = nc.dram_tensor("node_table", [NTOK, TAB_W], F32, kind="Internal").ap()
    rows = nc.dram_tensor("slot_rows", [NSLOT + P, ROW_W], F32, kind="Internal").ap()
    yexp = nc.dram_tensor("expert_rows", [P, NB, EX * D], F32, kind="Internal").ap()

    with ExitStack() as ctx:
        def sb(name, shape, dt=F32):
            return ctx.enter_context(nc.sbuf_tensor(name, shape, dt))

        def ps(name, shape, dt=F32):
            return ctx.enter_context(nc.psum_tensor(name, shape, dt))

        def sem(name):
            return ctx.enter_context(nc.semaphore(name))

        iota2 = sb("iota2", [P, P, 2], BF16)
        ident_b = sb("ident_b", [P, P], BF16)
        ident_f = sb("ident_f", [P, P])
        before = sb("before", [P, P])
        zero_b = sb("zero_b", [P, P], BF16)
        ones_f = sb("ones_f", [P, P])
        node_id = sb("node_id", [P, NB], I32)
        lane_start = sb("lane_start", [P, P])
        slot_base = sb("slot_base", [P, 1])
        trash = sb("trash", [P, 1])
        flat_id = sb("flat_id", [P, P])
        col_no = sb("col_no", [P, LANE], mybir.dt.int16)

        qw_s = sb("qw_s", [D, D])
        wg_s = sb("wg_s", [D, HE])
        w1_s = sb("w1_s", [D, EX, HID])
        w2_s = sb("w2_s", [HID, EX, D])
        b1_s = sb("b1_s", [HID, EX])
        b2_s = sb("b2_s", [1, EX * D])
        att_s = sb("att_s", [P, 2, HE])
        gate_p = sb("gate_p", [P, 3, HE])

        ids = sb("ids", [P, NB + 4], I32)
        keep = sb("keep", [P, NB + 4])
        eidx = sb("eidx", [P, 2, 2], U32)
        erow = sb("erow", [P, 2, 2, D])
        X = sb("X", [P, NB, D])
        big = sb("big", [P, NTOK])
        xn2T = big[0:D, :]
        y_ring = big[:, 0:2 * 16 * EX * D].rearrange("p (s k f) -> p s k f", s=2, k=16)
        gated = big[:, 8192:8192 + 16 * EX * D].rearrange("p (k e d) -> p k e d", k=16, e=EX)
        o_ring = big[:, 12288:12288 + 2 * 16 * D].rearrange("p (s k d) -> p s k d", s=2, k=16)
        o_half = big[:, 14336:14336 + 2 * 16 * D].rearrange("p (s k d) -> p s k d", s=2, k=16)

        src = sb("src", [P, LANE], I32)
        key = src[:, :].bitcast(F32)
        dst = big[:, 0:EB].bitcast(I32)
        digit_i = big[:, EB:2 * EB].bitcast(I32)
        digit = sb("digit", [P, EB // 2 + 4, 2, 2], BF16)
        onehot = sb("onehot", [P, 2, 8, P, 2], BF16)
        hot_ring = onehot[:, :, :, :, :].rearrange("p s (q u) n b -> p (s q) u n b", q=2)
        hist = sb("hist", [P, P])
        incl = sb("incl", [P, P])
        rowsum = sb("rowsum", [P, 1])
        rowoff = sb("rowoff", [P, 1])
        off = sb("off", [P, P])
        off1 = sb("off1", [P, P])
        off2 = sb("off2", [P, P])
        hist_even = sb("hist_even", [P, P])
        end = sb("end", [P, P])
        offT = sb("offT", [P, P])
        endT = sb("endT", [P, NB + 32], U32)
        hiT = sb("hiT", [P, 2, GRP, P])
        hiT_b = sb("hiT_b", [P, GRP, P], BF16)
        same = sb("same", [P, 2, GRP, P], BF16)
        count = sb("count", [P, GRP, P])
        picked = sb("picked", [P, GRP, P])
        slotf = sb("slotf", [P, 2, HALF])
        sidx = sb("sidx", [P, 2, CH], U32)
        spay = sb("spay", [P, 2, CH], I32)

        stats = sb("stats", [P, 2, 2, 6])
        mv = sb("mv", [P, 2, 2, 2])
        vare = sb("vare", [P, 2, 2])
        std = sb("std", [P, 2, 2])
        rstd = sb("rstd", [P, 2, 2])
        xcur = sb("xcur", [P, 2, D])
        xn = sb("xn", [P, 2, D])
        xn2 = sb("xn2", [P, 2, D])
        xnT = sb("xnT", [D, 2 * P])
        xnT2 = sb("xnT2", [D, 2 * P])
        qT = sb("qT", [D, 2 * P])
        att = sb("att", [P, 2, 2 * P])
        tabt = sb("tabt", [P, 2, TAB_W])
        hatt = sb("hatt", [P, 2, 2, HE])

        srt_s = sb("srt_s", [P, LANE + 2 * CH], I32)
        cmp = onehot[:, :, :, :, :].rearrange("p s u n b -> p (s u n b)").rearrange("p (j n) -> p j n", n=P)
        cnt = sb("cnt", [P, P])
        first_f = sb("first_f", [P, 1])
        first_u = sb("first_u", [P, 1], U32)
        first_row = sb("first_row", [P, TAB_W])
        gidx = sb("gidx", [P, 2, CH], U32)
        grow = sb("grow", [P, 2, CH, TAB_W])
        keep4 = sb("keep4", [P, 2, HD, CH + 1])
        neg4 = sb("neg4", [P, 2, HD, CH + 1])
        ad_in = sb("ad_in", [P, 2, HD, CH + 1])
        ad = sb("ad", [P, 2, HD, CH + 1])
        e_raw = sb("e_raw", [P, 2, HD, CH])
        e_in = sb("e_in", [P, 2, HD, CH + 1])
        mx = sb("mx", [P, 2, HD, CH + 1])
        expo = sb("expo", [P, 2, 2 * HD, CH])
        ex = sb("ex", [P, 2, 2 * HD, CH])
        decay = sb("decay", [P, 2, SUM_W, CH + 1])
        add = sb("add", [P, 2, SUM_W, CH + 1])
        run = sb("run", [P, 2, SUM_W, CH + 1])
        orow = sb("orow", [P, 2, CH, ROW_W])
        hid = hiT[:, :, :, :].rearrange("p s b n -> p (s b n)").rearrange("p (e n) -> p e n", e=EX)
        y_out = sb("y_out", [P, 2, EX * D])

        lane_sum = sb("lane_sum", [P, 3, SUM_W])
        laneT = sb("laneT", [SUM_W, 3, P])
        lneg = sb("lneg", [SUM_W, P])
        lmax = sb("lmax", [SUM_W, P + 1])
        lexp = sb("lexp", [SUM_W, 2, P])
        lsum = sb("lsum", [SUM_W, P + 1])
        carry = sb("carry", [P, 2, SUM_W])
        fstart = sb("fstart", [P, 1])
        mendq = sb("mendq", [P, 4])
        mendu = sb("mendu", [P, 2], U32)
        mrow = sb("mrow", [P, ROW_W])
        mmax = sb("mmax", [P, HD])
        mexp = sb("mexp", [P, 2, HD])
        mtmp = sb("mtmp", [P, 2, SUM_W])
        mout = sb("mout", [P, ROW_W])

        TB = 16
        tidx = sb("tidx", [P, 2, TB], U32)
        trow = sb("trow", [P, 2, TB, ROW_W])
        den = sb("den", [P, TB, HD])
        agg = sb("agg", [P, TB, HD, EX])
        sq = sb("sq", [P, TB, HE])
        red = sb("red", [P, 6, TB])
        sc4 = sb("sc4", [P, TB, EX])
        dif = sb("dif", [P, TB, EX, EX])
        tie = sb("tie", [P, EX, EX])
        rank = sb("rank", [P, TB, EX])
        gate = sb("gate", [P, TB, EX])

        cnt_bank = [ps(f"ps_cnt{h}", [P, 512]) for h in range(2)]
        ps_cnt = [t[:, 0:P] for t in cnt_bank]
        ps_hiT = ps("ps_hiT", [P, 2, GRP, P], BF16)
        ps_same = ps("ps_same", [P, GRP, P])
        ps_slot = ps("ps_slot", [P, 2, GRP, P])
        ps_tr = ps("ps_tr", [P, 512])
        ps_sc = ps("ps_sc", [P, 2, 2 * P])
        ps_hid = [ps_slot[:, 0, 0:2, :].rearrange("p a b -> p (a b)"), ps_slot[:, 1, 0:2, :].rearrange("p a b -> p (a b)"),
                  ps_sc[:, 0, :], cnt_bank[0][:, 0:2 * P]]
        ps_y = ps_same[:, :, :].rearrange("p g n -> p (g n)").rearrange("p (a f) -> p a f", a=2)

        loaded = sem("loaded")
        waits_passed = sem("waits_passed")
        spare_rows = sem("spare_rows")
        edges_in = sem("edges_in")
        consts = sem("consts")
        consts2 = sem("consts2")
        prep = sem("prep")
        prep2 = sem("prep2")
        eidx_ready = sem("eidx_ready")
        emb_rows = [sem(f"emb_rows{s}") for s in range(2)]
        emb_kept = sem("emb_kept")
        hot_ready = sem("hot_ready")
        hist_done = sem("hist_done")
        off_mm = sem("off_mm")
        off_ready = sem("off_ready")
        oh_ready = sem("oh_ready")
        hiT_mm = sem("hiT_mm")
        hiT_ready = sem("hiT_ready")
        same_mm = sem("same_mm")
        same_ready = sem("same_ready")
        count_ready = sem("count_ready")
        counted = sem("counted")
        slot_mm = sem("slot_mm")
        slot_ready = sem("slot_ready")
        sidx_part = sem("sidx_part")
        sidx_ready = sem("sidx_ready")
        scattered = [sem(f"scattered{s}") for s in range(2)]
        var_ready = sem("var_ready")
        std_ready = sem("std_ready")
        norm_ready = sem("norm_ready")
        normT_mm = sem("normT_mm")
        normT_ready = sem("normT_ready")
        normT_kept = sem("normT_kept")
        q_mm = sem("q_mm")
        q_ready = sem("q_ready")
        score_mm = sem("score_mm")
        att_ready = sem("att_ready")
        value_mm = sem("value_mm")
        gat_mm = sem("gat_mm")
        table_ready = sem("table_ready")
        table_stored = sem("table_stored")
        dve_att = sem("dve_att")
        sorted_in = sem("sorted_in")
        lane_mm = sem("lane_mm")
        first_ready = sem("first_ready")
        first_in = sem("first_in")
        gidx_ready = sem("gidx_ready")
        gathered = [sem(f"gathered{s}") for s in range(2)]
        dve_str = sem("dve_str")
        expo_ready = sem("expo_ready")
        exp_ready = sem("exp_ready")
        run_ready = sem("run_ready")
        orow_ready = sem("orow_ready")
        orow_stored = [sem(f"orow_stored{s}") for s in range(2)]
        hid_mm = sem("hid_mm")
        hid_ready = sem("hid_ready")
        y_mm = sem("y_mm")
        y_ready = sem("y_ready")
        y_stored = sem("y_stored")
        dve_mend = sem("dve_mend")
        lane_ends = sem("lane_ends")
        lane_endsT = sem("lane_endsT")
        lane_expo = sem("lane_expo")
        lane_exp = sem("lane_exp")
        lane_carry = sem("lane_carry")
        lane_carryT = sem("lane_carryT")
        mend_idx = sem("mend_idx")
        mend_expo = sem("mend_expo")
        mend_exp = sem("mend_exp")
        mend_ready = sem("mend_ready")
        mend_in = sem("mend_in")
        mend_out = sem("mend_out")
        tidx_ready = sem("tidx_ready")
        tail_rows = [sem(f"tail_rows{s}") for s in range(2)]
        dve_tail = sem("dve_tail")
        y_loaded = [sem(f"y_loaded{s}") for s in range(2)]
        tail_var = sem("tail_var")
        tail_std = sem("tail_std")
        tail_sub = sem("tail_sub")
        tail_exp = sem("tail_exp")
        out_ready = sem("out_ready")
        out_stored = [sem(f"out_stored{s}") for s in range(2)]

        block = ctx.enter_context(nc.Block())

        TAIL = 29
        PREP2 = 8

        class Chain:

            def __init__(self, eng, s, base=0):
                self.eng, self.s, self.base, self.n, self.at = eng, s, base, 0, 0

            def turn(self, i, per_turn):
                self.at, self.per, self.n = i * per_turn, per_turn, 0

            def mark(self, ins):
                ins.then_inc(self.s, 1)
                self.n += 1
                return self.at + (self.base + self.n)

            def step(self, ins):
                self.eng.wait_ge(self.s, self.mark(ins))

            def end_turn(self, turns):
                assert self.n == self.per, (self.n, self.per)
                self.at, self.base, self.n = 0, self.base + turns * self.per, 0

        def lone_wait(eng, s, value):
            eng.wait_ge(s, value)
            eng.sem_inc(waits_passed, 1)

        def hot(s, b, d):
            return hot_ring[:, s, b // 2 * 2 + d, :, b % 2]

        @block.sync
        def _(sp):
            sp.dma_start(dst, edst).then_inc(edges_in, 16)
            sp.dma_start(ids[:, 0:NB], tok).then_inc(loaded, 16)
            sp.dma_start(src[:, 0:EB], esrc).then_inc(loaded, 16)
            for t, a in ((qw_s[:, :], qw), (wg_s[:, :], wgat), (w1_s[:, :, :], w1), (w2_s[:, :, :], w2),
                         (b1_s[:, :], b1), (b2_s[:, :], b2)):
                sp.dma_start(t, a).then_inc(loaded, 16)
            for t, a in ((att_s[:, 0, :], att_src), (att_s[:, 1, :], att_dst), (gate_p[:, 0, :], b_gat),
                         (gate_p[:, 1, :], gamma), (gate_p[:, 2, :], beta)):
                sp.dma_start(t, a.broadcast_to([P, HE])).then_inc(loaded, 16)

            sp.wait_ge(consts2, 3)
            sp.dma_start(rows[NSLOT:NSLOT + P, :], ones_f[:, 0:ROW_W]).then_inc(spare_rows, 16)
            tab_v = table.rearrange("(k p) f -> p k f", p=P)
            with sp.Fori(0, BATCHES) as i:
                sp.wait_ge(table_ready, i + 1)
                sp.dma_start(tab_v[:, bass.ds(i * 2, 2), :], tabt[:, :, :]).then_inc(table_stored, 16)

            for s in range(2):
                sp.wait_ge(scattered[s], BATCHES * CH * 16)
            sp.dma_start(srt_s[:, 0:LANE], srt[:, :].rearrange("(p t) o -> p (t o)", p=P)).then_inc(sorted_in, 16)

            rows_v = rows[0:NSLOT, :].rearrange("(p t) f -> p t f", p=P)
            with sp.Fori(0, BATCHES) as i:
                for s in range(2):
                    sp.wait_ge(orow_ready, i * 2 + (s + 1))
                    sp.dma_start(rows_v[:, bass.ds(i * (2 * CH) + s * CH, CH), :],
                                 orow[:, s, :, :]).then_inc(orow_stored[s], 16)
                sp.wait_ge(y_ready, i + 1)
                sp.dma_start(yexp[:, bass.ds(i * 2, 2), :], y_out[:, :, :]).then_inc(y_stored, 16)

            sp.wait_ge(y_stored, BATCHES * 16)
            with sp.Fori(0, NB // TB // 2) as i:
                for s in range(2):
                    sp.wait_ge(tidx_ready, i * 2 + (s + 1))
                    sp.dma_start(y_ring[:, s, :, :],
                                 yexp[:, bass.ds(i * (2 * TB) + s * TB, TB), :]).then_inc(y_loaded[s], 16)

        @block.gpsimd
        def _(pool):
            pool.iota(iota2[:, :, :], [[1, P], [0, 2]], base=0, channel_multiplier=0,
                      allow_small_or_imprecise_dtypes=True).then_inc(consts, 1)
            pool.memset(ident_b[:, :], 0.0).then_inc(consts2, 1)
            pool.memset(ident_f[:, :], 0.0).then_inc(consts2, 1)
            pool.memset(ones_f[:, :], 1.0).then_inc(consts2, 1)
            pool.memset(zero_b[:, :], 0.0).then_inc(consts, 1)
            pool.wait_ge(consts2, 3)
            pool.affine_select(out=ident_b[:, :], in_=ident_b[:, :], compare_op=ALU.not_equal, fill=1.0, base=0,
                               pattern=[[-1, P]], channel_multiplier=1).then_inc(consts, 1)
            pool.affine_select(out=ident_f[:, :], in_=ident_f[:, :], compare_op=ALU.not_equal, fill=1.0, base=0,
                               pattern=[[-1, P]], channel_multiplier=1).then_inc(consts, 1)
            pool.affine_select(out=before[:, :], in_=ones_f[:, :], compare_op=ALU.is_gt, fill=0.0, base=0,
                               pattern=[[1, P]], channel_multiplier=-1).then_inc(consts, 1)
            pool.iota(flat_id[:, :], [[1, P]], base=0, channel_multiplier=P,
                      allow_small_or_imprecise_dtypes=True).then_inc(consts, 1)
            with pool.Fori(0, NB // 4) as i:
                for s in range(2):
                    lone_wait(pool, eidx_ready, i * 2 + (s + 1))
                    for a in range(2):
                        pool.indirect_dma_start(erow[:, s, a, :], None, emb,
                                                bass.IndirectOffsetOnAxis(ap=eidx[:, s, a:a + 1], axis=0)
                                                ).then_inc(emb_rows[s], 16)
            pool.iota(node_id[:, :], [[P, NB]], base=FLAG, channel_multiplier=1).then_inc(consts, 1)
            pool.iota(lane_start[:, :], [[LANE, P]], base=0, channel_multiplier=0,
                      allow_small_or_imprecise_dtypes=True).then_inc(consts, 1)
            pool.iota(slot_base[:, :], [[0, 1]], base=-1, channel_multiplier=LANE,
                      allow_small_or_imprecise_dtypes=True).then_inc(consts, 1)
            pool.iota(trash[:, :], [[0, 1]], base=NSLOT, channel_multiplier=1,
                      allow_small_or_imprecise_dtypes=True).then_inc(consts, 1)
            pool.iota(col_no[:, :], [[1, LANE]], base=0, channel_multiplier=0,
                      allow_small_or_imprecise_dtypes=True).then_inc(consts, 1)
            pool.affine_select(out=tie[:, :, :], in_=ones_f[:, 0:EX * EX].rearrange("p (a b) -> p a b", a=EX),
                               compare_op=ALU.is_gt, fill=0.0, base=0, pattern=[[1, EX], [-1, EX]],
                               channel_multiplier=0).then_inc(consts, 1)

            with pool.Fori(0, BATCHES) as i:
                for s in range(2):
                    lone_wait(pool, sidx_ready, i * 2 + (s + 1))
                    for c in range(CH):
                        pool.indirect_dma_start(srt, bass.IndirectOffsetOnAxis(ap=sidx[:, s, c:c + 1], axis=0),
                                                spay[:, s, c:c + 1], None).then_inc(scattered[s], 16)

            pool.wait_ge(first_ready, 1)
            pool.wait_ge(table_stored, BATCHES * 16)
            pool.indirect_dma_start(first_row[:, :], None, table,
                                    bass.IndirectOffsetOnAxis(ap=first_u[:, 0:1], axis=0)).then_inc(first_in, 16)
            with pool.Fori(0, BATCHES) as i:
                for s in range(2):
                    lone_wait(pool, gidx_ready, i * 2 + (s + 1))
                    for c in range(CH):
                        pool.indirect_dma_start(grow[:, s, c, :], None, table,
                                                bass.IndirectOffsetOnAxis(ap=gidx[:, s, c:c + 1], axis=0)
                                                ).then_inc(gathered[s], 16)

            for s in range(2):
                pool.wait_ge(orow_stored[s], BATCHES * 16)
            pool.wait_ge(spare_rows, 16)
            pool.wait_ge(mend_idx, 1)
            pool.indirect_dma_start(mrow[:, :], None, rows,
                                    bass.IndirectOffsetOnAxis(ap=mendu[:, 0:1], axis=0)).then_inc(mend_in, 16)
            pool.wait_ge(mend_ready, 1)
            pool.indirect_dma_start(rows, bass.IndirectOffsetOnAxis(ap=mendu[:, 1:2], axis=0),
                                    mout[:, :], None).then_inc(mend_out, 16)
            pool.wait_ge(mend_out, 16)

            with pool.Fori(0, NB // TB // 2) as i:
                for s in range(2):
                    lone_wait(pool, tidx_ready, i * 2 + (s + 1))
                    for c in range(TB):
                        pool.indirect_dma_start(trow[:, s, c, :], None, rows,
                                                bass.IndirectOffsetOnAxis(ap=tidx[:, s, c:c + 1], axis=0)
                                                ).then_inc(tail_rows[s], 16)

        @block.tensor
        def _(pe):
            pe.wait_ge(consts, 6)
            for h in range(2):
                m = pe.matmul(ps_cnt[h], zero_b[:, :], zero_b[:, :], start=True, stop=True, skip_group_check=True)
            m.then_inc(hist_done, 1)
            with pe.Fori(0, EB // 64) as i:
                for j in range(8):
                    pe.wait_ge(hot_ready, i * 8 + (j + 1))
                    for b in range(8):
                        m = pe.matmul(ps_cnt[b % 2], onehot[:, j % 2, :, :, :][:, b // 2 * 2, :, b % 2],
                                      onehot[:, j % 2, :, :, :][:, b // 2 * 2 + 1, :, b % 2],
                                      start=False, stop=True, skip_group_check=True)
                    m.then_inc(hist_done, 1)
            pe.wait_ge(off_ready, 1)
            pe.matmul(ps_tr[:, 0:1], before[:, :], rowsum[:, :], start=True, stop=True).then_inc(off_mm, 1)
            pe.wait_ge(off_ready, 2)
            pe.transpose(ps_tr[:, 128:256], off[:, :], ident_f[:, :])
            pe.transpose(ps_tr[:, 256:384], end[:, :], ident_f[:, :]).then_inc(off_mm, 1)
            pe.matmul(ps_cnt[0], ident_f[:, :], off1[:, :], start=True, stop=True,
                      skip_group_check=True).then_inc(counted, 1)
            pe.matmul(ps_cnt[1], ident_f[:, :], off2[:, :], start=True, stop=True,
                      skip_group_check=True).then_inc(counted, 1)

            def hi_transposes(grp, s, slot):
                pe.wait_ge(oh_ready, grp + 1)
                for b in range(GRP):
                    m = pe.transpose(ps_hiT[:, s, b, :], hot(slot, b, 0), ident_b[:, :])
                m.then_inc(hiT_mm, 1)

            def same_high(grp, s):
                pe.wait_ge(hiT_ready, grp + 1)
                for b in range(GRP):
                    m = pe.matmul(ps_same[:, b, :], hiT_b[:, b, :], hiT_b[:, b, :], start=True, stop=True)
                m.then_inc(same_mm, 1)

            hi_transposes(0, 0, 0)
            same_high(0, 0)
            with pe.Fori(0, BATCHES) as i:
                for g in range(STEPS):
                    s = g % 2
                    pe.wait_ge(hiT_ready, i * STEPS + (g + 1))
                    hi_transposes(i * STEPS + (g + 1), 1 - s, (g + 1) % 4)
                    for b in range(GRP):
                        if b == 0:
                            pe.wait_ge(same_ready, i * STEPS + (g + 1))
                        pe.wait_ge(slot_ready, i * (STEPS * GRP) + (GRP * g + b + 1))
                        pe.matmul(ps_slot[:, b % 2, 0, :], same[:, s, b, :], hot(g % 4, b, 1), start=True, stop=False)
                        pe.wait_ge(count_ready, i * (STEPS * GRP) + (GRP * g + b + 1))
                        pe.matmul(ps_cnt[b % 2], hot(g % 4, b, 0), hot(g % 4, b, 1), start=False, stop=True,
                                  skip_group_check=True).then_inc(counted, 1)
                        pe.matmul(ps_slot[:, b % 2, 0, :], hiT[:, s, b, :], count[:, b, :],
                                  start=False, stop=True).then_inc(slot_mm, 1)
                        if b == 1:
                            pe.wait_ge(same_ready, i * STEPS + (g + 1))
                            same_high(i * STEPS + (g + 1), 1 - s)
                    if g == 1 or g == 5:
                        n = 0 if g == 1 else 1
                        x_ = (xn, xn2)[n]
                        lone_wait(pe, norm_ready, i * 2 + (n + 1))
                        pe.transpose(ps_tr[0:D, 0:P], x_[:, 0, :], ident_f[:, :])
                        pe.transpose(ps_tr[0:D, P:2 * P], x_[:, 1, :], ident_f[:, :]).then_inc(normT_mm, 1)
                    if g == 2:
                        lone_wait(pe, normT_ready, i * 2 + 1)
                        pe.matmul(ps_tr[0:D, 256:512], qw_s[:, :], xnT[:, :], start=True, stop=True).then_inc(q_mm, 1)
                    if g == 3:
                        pe.wait_ge(q_ready, i + 1)
                        for m in range(2):
                            last = pe.matmul(ps_sc[:, m, :], xnT[:, m * P:(m + 1) * P], qT[:, :], start=True, stop=True)
                        last.then_inc(score_mm, 1)
                    if g == 4:
                        pe.wait_ge(att_ready, i + 1)
                        for n in range(2):
                            for m in range(2):
                                last = pe.matmul(ps_tr[:, n * D:(n + 1) * D], att[:, m, n * P:(n + 1) * P],
                                                 xn[:, m, :], start=(m == 0), stop=(m == 1))
                        last.then_inc(value_mm, 1)
                    if g == 6:
                        pe.wait_ge(normT_ready, i * 2 + 2)
                        for n in range(2):
                            last = pe.matmul(ps_tr[:, 256 + n * HE:256 + (n + 1) * HE], xnT2[:, n * P:(n + 1) * P],
                                             wg_s[:, :], start=True, stop=True)
                        last.then_inc(gat_mm, 1)

            pe.wait_ge(prep2, PREP2)
            pe.matmul(ps_tr[:, 0:1], cnt[:, :], ones_f[:, 0:1], start=True, stop=True).then_inc(lane_mm, 1)

            with pe.Fori(0, BATCHES) as i:
                pe.wait_ge(hid_ready, i * EX)
                for e in range(EX):
                    pe.matmul(ps_hid[e], w1_s[:, e, :], xn2T[:, bass.ds(i * (2 * P), 2 * P)],
                              start=True, stop=True).then_inc(hid_mm, 1)
                pe.wait_ge(y_ready, i)
                for a in range(2):
                    for e in range(EX):
                        if a == 0:
                            pe.wait_ge(hid_ready, i * EX + (e + 1))
                        pe.matmul(ps_y[:, a, e * D:(e + 1) * D], hid[:, e, a * P:(a + 1) * P], w2_s[:, e, :],
                                  start=True, stop=False)
                        last = pe.matmul(ps_y[:, a, e * D:(e + 1) * D], ones_f[0:1, :], b2_s[0:1, e * D:(e + 1) * D],
                                         start=False, stop=True)
                last.then_inc(y_mm, 1)

            pe.wait_ge(lane_ends, 1)
            for n in range(3):
                last = pe.transpose(ps_tr[0:SUM_W, n * P:(n + 1) * P], lane_sum[:, n, :], ident_f[:, :])
            last.then_inc(lane_endsT, 1)
            pe.wait_ge(lane_carry, 1)
            pe.transpose(ps_sc[:, 0, 0:SUM_W], lsum[:, 0:P], ident_f[0:SUM_W, 0:SUM_W])
            pe.transpose(ps_sc[:, 0, 32:32 + SUM_W], lmax[:, 0:P], ident_f[0:SUM_W, 0:SUM_W]).then_inc(lane_carryT, 1)

        @block.scalar
        def _(act):
            act.wait_ge(loaded, 16 * 13)
            act.wait_ge(prep, 2)
            for s in range(2):
                act.activation(eidx[:, s, :], ids[:, 2 * s:2 * s + 2], ACT.Copy).then_inc(eidx_ready, 1)
            with act.Fori(0, NB // 4) as i:
                for s in range(2):
                    act.wait_ge(emb_rows[s], i * 32 + 32)
                    for a in range(2):
                        k = i * 4 + (2 * s + a)
                        act.activation(X[:, bass.ds(k, 1), :].rearrange("p o d -> p (o d)"), erow[:, s, a, :],
                                       ACT.Copy, scale=keep[:, bass.ds(k, 1)]).then_inc(emb_kept, 1)
                    act.activation(eidx[:, s, :], ids[:, bass.ds(i * 4 + (4 + 2 * s), 2)], ACT.Copy
                                   ).then_inc(eidx_ready, 1)

            def copy_hiT(grp, s):
                act.wait_ge(hiT_mm, grp + 1)
                act.activation(hiT_b[:, :, :], ps_hiT[:, s, :, :], ACT.Copy)
                act.activation(hiT[:, s, :, :], ps_hiT[:, s, :, :], ACT.Copy).then_inc(hiT_ready, 1)

            copy_hiT(0, 0)
            with act.Fori(0, BATCHES) as i:
                for g in range(STEPS):
                    s = g % 2
                    for b in range(GRP):
                        if b == 2:
                            act.wait_ge(slot_mm, i * (STEPS * GRP) + GRP * g)
                            copy_hiT(i * STEPS + (g + 1), 1 - s)
                        act.wait_ge(counted, i * (STEPS * GRP) + (GRP * g + b + 1))
                        act.activation(count[:, b, :], ps_cnt[b % 2], ACT.Copy).then_inc(count_ready, 1)
                    if g == 0 or g == 4:
                        n = g // 4
                        act.wait_ge(var_ready, i * 2 + (n + 1))
                        act.activation(std[:, n, :], vare[:, n, :], ACT.Sqrt).then_inc(std_ready, 1)
                    if g == 1:
                        act.wait_ge(normT_mm, i * 2 + 1)
                        act.activation(xnT[:, :], ps_tr[0:D, 0:2 * P], ACT.Copy).then_inc(normT_ready, 1)
                    if g == 5:
                        act.wait_ge(normT_mm, i * 2 + 2)
                        act.activation(xnT2[:, :], ps_tr[0:D, 0:2 * P], ACT.Copy).then_inc(normT_ready, 1)
                    if g == 2:
                        act.wait_ge(q_mm, i + 1)
                        act.activation(qT[:, :], ps_tr[0:D, 256:512], ACT.Copy).then_inc(q_ready, 1)
                    if g == 3:
                        act.wait_ge(score_mm, i + 1)
                        act.activation(att[:, :, :], ps_sc[:, :, :], ACT.Sigmoid).then_inc(att_ready, 1)
                    if g == 6:
                        act.wait_ge(normT_ready, i * 2 + 2)
                        act.activation(xn2T[:, bass.ds(i * (2 * P), 2 * P)], xnT2[:, :], ACT.Copy
                                       ).then_inc(normT_kept, 1)

            act.wait_ge(slot_mm, EB)
            with act.Fori(0, BATCHES) as i:
                for s in range(2):
                    act.wait_ge(expo_ready, i * 2 + (s + 1))
                    act.activation(ex[:, s, :, :], expo[:, s, :, :], ACT.Exp).then_inc(exp_ready, 1)
                    act.wait_ge(run_ready, i * 2 + (s + 1))
                    act.wait_ge(orow_stored[s], i * 16)
                    act.activation(orow[:, s, :, 0:SUM_W].rearrange("p t f -> p f t"),
                                   run[:, s, :, 1:CH + 1], ACT.Copy)
                    act.activation(orow[:, s, :, SUM_W:ROW_W].rearrange("p t f -> p f t"),
                                   mx[:, s, :, 1:CH + 1], ACT.Copy).then_inc(orow_ready, 1)
                act.wait_ge(y_mm, i)
                for e in range(EX):
                    act.wait_ge(hid_mm, i * EX + (e + 1))
                    act.activation(hid[:, e, :], ps_hid[e], ACT.Gelu, bias=b1_s[:, e:e + 1]).then_inc(hid_ready, 1)
                act.wait_ge(y_mm, i + 1)
                act.wait_ge(y_stored, i * 16)
                act.activation(y_out[:, :, :], ps_y, ACT.Copy).then_inc(y_ready, 1)

            act.wait_ge(lane_expo, 1)
            act.activation(lexp[:, :, :], lexp[:, :, :], ACT.Exp).then_inc(lane_exp, 1)
            act.wait_ge(mend_expo, 1)
            act.activation(mexp[:, :, :], mexp[:, :, :], ACT.Exp).then_inc(mend_exp, 1)

            out_v = out.rearrange("(k p) d -> p k d", p=P)
            with act.Fori(0, NB // TB // 2) as i:
                for s in range(2):
                    act.wait_ge(tail_var, i * 2 + (s + 1))
                    act.activation(red[:, 3, :], red[:, 2, :], ACT.Sqrt).then_inc(tail_std, 1)
                    act.wait_ge(tail_sub, i * 2 + (s + 1))
                    act.activation(gate[:, :, :], sc4[:, :, :], ACT.Exp).then_inc(tail_exp, 1)
                    act.wait_ge(out_ready, i * 2 + (s + 1))
                    act.dma_start(out_v[:, bass.ds(i * (2 * TB) + s * TB, TB), :], o_ring[:, s, :, :]
                                  ).then_inc(out_stored[s], 16)
            for s in range(2):
                act.wait_ge(out_stored[s], NB // TB // 2 * 16)

        @block.vector
        def _(dve):
            V = nc.vector
            c = Chain(dve, prep)
            c.mark(V.memset(ids[:, NB:NB + 4], 0))
            dve.wait_ge(loaded, 16 * 13)
            c.mark(V.tensor_scalar(keep[:, 0:NB], ids[:, 0:NB], 0, None, ALU.not_equal))
            c.mark(V.memset(digit[:, EB // 2:EB // 2 + 4, :, :], 0.0))
            dve.wait_ge(edges_in, 16)
            c.step(V.tensor_scalar(digit_i, dst, 7, None, ALU.logical_shift_right))
            c.step(V.tensor_copy(digit[:, 0:EB // 2, 0, :], digit_i.rearrange("p (a b) -> p a b", b=2)))
            c.step(V.tensor_scalar(digit_i, dst, P - 1, None, ALU.bitwise_and))
            c.step(V.tensor_copy(digit[:, 0:EB // 2, 1, :], digit_i.rearrange("p (a b) -> p a b", b=2)))
            dve.wait_ge(consts, 6)

            def one_hots(pair, to):
                units = to.shape[1]
                d = digit[:, bass.ds(pair, units // 2), :, :].rearrange("p a h b -> p (a h) b")
                return V.tensor_tensor(to,
                                       iota2[:, :, :].unsqueeze(1).broadcast_to([P, units, P, 2]),
                                       d.unsqueeze(2).broadcast_to([P, units, P, 2]), ALU.is_equal)

            with dve.Fori(0, EB // 64) as i:
                for j in range(8):
                    dve.wait_ge(hist_done, i * 8 + j)
                    one_hots(i * 32 + 4 * j, onehot[:, j % 2, :, :, :]).then_inc(hot_ready, 1)
            dve.wait_ge(hist_done, EB // 8 + 1)
            c.step(V.tensor_copy(hist_even[:, :], ps_cnt[0]))
            c.step(V.tensor_tensor(hist[:, :], hist_even[:, :], ps_cnt[1], ALU.add))
            c.step(V.tensor_tensor_scan(incl[:, :], ones_f[:, :], hist[:, :], 0.0, ALU.mult, ALU.add))
            V.tensor_copy(rowsum[:, :], incl[:, P - 1:P]).then_inc(off_ready, 1)
            dve.wait_ge(off_ready, 1)
            c.step(V.tensor_tensor(incl[:, :], incl[:, :], flat_id[:, :], ALU.add))
            dve.wait_ge(off_mm, 1)
            c.step(V.tensor_copy(rowoff[:, :], ps_tr[:, 0:1]))
            c.step(V.tensor_scalar(end[:, :], incl[:, :], rowoff[:, 0:1], None, ALU.add))
            c.step(V.tensor_tensor(off[:, :], end[:, :], hist[:, :], ALU.subtract))
            c.step(V.tensor_scalar(off1[:, :], off[:, :], 1.0, None, ALU.add))
            V.tensor_tensor(off2[:, :], off1[:, :], hist_even[:, :], ALU.add).then_inc(off_ready, 1)
            dve.wait_ge(off_mm, 2)
            c.mark(V.tensor_copy(offT[:, :], ps_tr[:, 128:256]))
            c.mark(V.memset(endT[:, NB:NB + 32], 0))
            c.mark(V.tensor_copy(endT[:, 0:NB], ps_tr[:, 256:384]))
            c.mark(V.memset(tabt[:, :, :], 1.0))
            c.step(V.memset(srt_s[:, LANE:LANE + 2 * CH], 0))

            def mask_same(grp, s):
                dve.wait_ge(same_mm, grp + 1)
                V.tensor_tensor(same[:, s, :, :], ps_same[:, :, :],
                                before[:, :].unsqueeze(1).broadcast_to([P, GRP, P]), ALU.mult
                                ).then_inc(same_ready, 1)

            one_hots(0, hot_ring[:, 0, :, :, :]).then_inc(oh_ready, 1)
            one_hots(2, hot_ring[:, 1, :, :, :]).then_inc(oh_ready, 1)
            mask_same(0, 0)
            V.memset(slotf[:, :, :], 0.0).then_inc(slot_ready, 2)
            dve.wait_ge(emb_kept, NB)
            dve.wait_ge(consts, 12)
            a = Chain(dve, dve_att)

            def layer_norm_stats(n):
                a.mark(V.bn_stats(stats[:, n, 0, :], xcur[:, 0, :]))
                lone_wait(dve, dve_att, a.mark(V.bn_stats(stats[:, n, 1, :], xcur[:, 1, :])))
                a.mark(V.bn_aggr(mv[:, n, 0, :], stats[:, n, 0, :]))
                a.step(V.bn_aggr(mv[:, n, 1, :], stats[:, n, 1, :]))
                V.tensor_scalar(vare[:, n, :], mv[:, n, :, 1], LN_EPS, None, ALU.add).then_inc(var_ready, 1)

            def layer_norm(i, n, to):
                dve.wait_ge(std_ready, i * 2 + (n + 1))
                a.step(V.reciprocal(rstd[:, n, :], std[:, n, :]))
                for t in range(2):
                    m = V.tensor_scalar(to[:, t, :], xcur[:, t, :], mv[:, n, t, 0:1], rstd[:, n, t:t + 1],
                                        ALU.subtract, ALU.mult)
                m.then_inc(norm_ready, 1)

            with dve.Fori(0, BATCHES) as i:
                a.turn(i, 16)
                for g in range(STEPS):
                    s = g % 2
                    grp = i * STEPS + g
                    dve.wait_ge(slot_ready, grp * GRP + 2)
                    one_hots(grp * 2 + 4, hot_ring[:, (g + 2) % 4, :, :, :]).then_inc(oh_ready, 1)
                    if g == 0:
                        dve.wait_ge(sidx_ready, i * 2)
                    for b in range(GRP):
                        if b == 3:
                            mask_same(grp + 1, 1 - s)
                        dve.wait_ge(slot_mm, grp * GRP + (b + 1))
                        n = GRP * g + b
                        V.tensor_tensor_reduce(out=picked[:, b, :], in0=ps_slot[:, b % 2, 0, :], in1=hot(g % 4, b, 1),
                                               scale=1.0, scalar=0.0, op0=ALU.mult, op1=ALU.add,
                                               accum_out=slotf[:, n // HALF, n % HALF:n % HALF + 1]
                                               ).then_inc(slot_ready, 1)
                    if g % 4 == 3:
                        h = g // 4
                        dve.wait_ge(scattered[h], i * (CH * 16))
                        V.tensor_copy(spay[:, h, 0:HALF], src[:, bass.ds(i * (2 * HALF) + h * HALF, HALF)])
                        V.tensor_copy(spay[:, h, HALF:CH], node_id[:, bass.ds(i * 2 + h, 1)])
                        V.tensor_copy(sidx[:, h, HALF:CH], offT[:, bass.ds(i * 2 + h, 1)])
                        dve.wait_ge(slot_ready, (grp + 1) * GRP + 2)
                        V.tensor_copy(sidx[:, h, 0:HALF], slotf[:, h, :]).then_inc(sidx_ready, 1)
                    if g == 0:
                        a.step(V.tensor_copy(xcur[:, :, :], X[:, bass.ds(i * 2, 2), :]))
                        layer_norm_stats(0)
                    if g == 1:
                        layer_norm(i, 0, xn)
                    if g == 4:
                        dve.wait_ge(value_mm, i + 1)
                        a.step(V.tensor_tensor(xcur[:, :, :], xcur[:, :, :],
                                               ps_tr[:, 0:2 * D].rearrange("p (t d) -> p t d", t=2), ALU.add))
                        layer_norm_stats(1)
                        a.mark(V.tensor_copy(X[:, bass.ds(i * 2, 2), :], xcur[:, :, :]))
                    if g == 5:
                        layer_norm(i, 1, xn2)
                    if g == 7:
                        dve.wait_ge(gat_mm, i + 1)
                        dve.wait_ge(table_stored, i * 16)
                        hv = ps_tr[:, 256:256 + 2 * HE].rearrange("p (t f) -> p t f", t=2)
                        a.mark(V.tensor_copy(tabt[:, :, 0:SUM_W].rearrange("p t (h e) -> p t h e", h=HD)[:, :, :, 0:EX],
                                             hv.rearrange("p t (h e) -> p t h e", h=HD)))
                        for n in range(2):
                            a.mark(V.tensor_tensor(hatt[:, n, :, :], hv,
                                                   att_s[:, n, :].unsqueeze(1).broadcast_to([P, 2, HE]), ALU.mult))
                        dve.wait_ge(dve_att, a.at + (a.base + a.n))
                        for n in range(2):
                            m = V.tensor_reduce(tabt[:, :, SUM_W + n * HD:SUM_W + (n + 1) * HD],
                                                hatt[:, n, :, :].rearrange("p t (h e) -> p t h e", h=HD),
                                                AX.X, ALU.add)
                        m.then_inc(table_ready, 1)
                a.end_turn(BATCHES)

            c2 = Chain(dve, prep2)
            dve.wait_ge(counted, EB + 2)
            for q in range(4):
                c2.step(V.tensor_tensor(cmp, offT[:, :].unsqueeze(1).broadcast_to([P, 32, P]),
                                        lane_start[:, 32 * q:32 * q + 32].unsqueeze(2).broadcast_to([P, 32, P]),
                                        ALU.is_le))
                c2.step(V.tensor_reduce(cnt[:, 32 * q:32 * q + 32], cmp, AX.X, ALU.add))
            assert c2.n == PREP2
            dve.wait_ge(lane_mm, 1)
            c2.step(V.tensor_scalar(first_f[:, :], ps_tr[:, 0:1], -1.0, None, ALU.add))
            V.tensor_copy(first_u[:, :], first_f[:, :]).then_inc(first_ready, 1)
            for s in range(2):
                c2.mark(V.memset(keep4[:, s, :, 0:1], 0.0))
                c2.mark(V.memset(neg4[:, s, :, 0:1], -BIG))
                c2.mark(V.memset(decay[:, s, :, 0:1], 0.0))
            c2.mark(V.memset(mx[:, 1, :, CH:CH + 1], -BIG))
            c2.mark(V.memset(run[:, 1, :, CH:CH + 1], 0.0))
            c2.step(V.memset(trow[:, 0, 0, 0:1], 0.0))
            dve.wait_ge(first_in, 16)
            c2.step(V.tensor_copy(ad[:, 1, :, CH], first_row[:, SUM_W + HD:SUM_W + 2 * HD]))

            def stream_index(s, at):
                V.tensor_scalar(gidx[:, s, :].bitcast(I32), srt_s[:, bass.ds(at, CH)], FLAG - 1, None,
                                ALU.bitwise_and).then_inc(gidx_ready, 1)

            dve.wait_ge(sorted_in, 16)
            stream_index(0, 0)
            stream_index(1, CH)
            st = Chain(dve, dve_str)
            with dve.Fori(0, BATCHES) as i:
                st.turn(i, 28)
                for s in range(2):
                    r = 1 - s
                    at = i * (2 * CH) + s * CH
                    sv = srt_s[:, bass.ds(at, CH)].unsqueeze(1).broadcast_to([P, HD, CH])
                    dve.wait_ge(orow_ready, i * 2 + s)
                    st.mark(V.tensor_scalar(keep4[:, s, :, 1:CH + 1], sv, FLAG, None, ALU.is_lt))
                    st.mark(V.tensor_scalar(neg4[:, s, :, 1:CH + 1], sv, FLAG, -BIG, ALU.is_ge, ALU.mult))
                    st.mark(V.tensor_copy(ad_in[:, s, :, 0], ad[:, r, :, CH]))
                    st.mark(V.tensor_copy(e_in[:, s, :, 0], mx[:, r, :, CH]))
                    st.mark(V.tensor_copy(add[:, s, :, 0], run[:, r, :, CH]))
                    dve.wait_ge(gathered[s], i * (CH * 16) + CH * 16)
                    g_t = grow[:, s, :, :].rearrange("p t f -> p f t")
                    st.step(V.scalar_tensor_tensor(ad_in[:, s, :, 1:CH + 1], sv, FLAG,
                                                   g_t[:, SUM_W + HD:SUM_W + 2 * HD, :], ALU.is_ge, ALU.mult))
                    flat = lambda t: t[:, s, :, :].rearrange("p f t -> p (f t)")
                    st.step(V.tensor_tensor_scan(flat(ad), flat(keep4), flat(ad_in), 0.0, ALU.mult, ALU.add))
                    st.step(V.tensor_tensor(e_raw[:, s, :, :], g_t[:, SUM_W:SUM_W + HD, :], ad[:, s, :, 1:CH + 1],
                                            ALU.add))
                    st.step(V.scalar_tensor_tensor(e_in[:, s, :, 1:CH + 1], e_raw[:, s, :, :], SLOPE,
                                                   e_raw[:, s, :, :], ALU.mult, ALU.max))
                    st.step(V.tensor_tensor_scan(flat(mx), flat(neg4), flat(e_in), 0.0, ALU.add, ALU.max))
                    st.mark(V.tensor_tensor(expo[:, s, HD:2 * HD, :], e_in[:, s, :, 1:CH + 1],
                                            mx[:, s, :, 1:CH + 1], ALU.subtract))
                    st.step(V.tensor_tensor(expo[:, s, 0:HD, :], mx[:, s, :, 0:CH], mx[:, s, :, 1:CH + 1],
                                            ALU.subtract))
                    V.tensor_scalar(expo[:, s, 0:HD, :], expo[:, s, 0:HD, :], 0.0, None, ALU.min
                                    ).then_inc(expo_ready, 1)
                    dve.wait_ge(exp_ready, i * 2 + (s + 1))
                    fan = [P, HD, EX + 1, CH]
                    st.mark(V.tensor_tensor(decay[:, s, :, 1:CH + 1].rearrange("p (h e) t -> p h e t", h=HD),
                                            ex[:, s, 0:HD, :].unsqueeze(2).broadcast_to(fan),
                                            keep4[:, s, :, 1:CH + 1].unsqueeze(2).broadcast_to(fan), ALU.mult))
                    st.step(V.tensor_tensor(add[:, s, :, 1:CH + 1].rearrange("p (h e) t -> p h e t", h=HD),
                                            g_t[:, 0:SUM_W, :].rearrange("p (h e) t -> p h e t", h=HD),
                                            ex[:, s, HD:2 * HD, :].unsqueeze(2).broadcast_to(fan), ALU.mult))
                    stream_index(s, at + 2 * CH)
                    V.tensor_tensor_scan(flat(run), flat(decay), flat(add), 0.0, ALU.mult, ALU.add
                                         ).then_inc(run_ready, 1)
                    dve.wait_ge(run_ready, i * 2 + (s + 1))
                st.end_turn(BATCHES)

            m_ = Chain(dve, dve_mend)
            m_.step(V.tensor_scalar(key, srt_s[:, 0:LANE], float(FLAG), float(LANE), ALU.is_lt, ALU.mult))
            m_.step(V.tensor_tensor(key, key, col_no[:, :], ALU.add))
            m_.step(V.tensor_reduce(fstart[:, :], key, AX.X, ALU.min))
            V.tensor_scalar(lane_sum[:, 2, :], fstart[:, 0:1].broadcast_to([P, SUM_W]), float(LANE), None, ALU.is_lt)
            V.tensor_copy(lane_sum[:, 1, :].rearrange("p (h e) -> p h e", h=HD),
                          mx[:, 1, :, CH:CH + 1].broadcast_to([P, HD, EX + 1]))
            V.tensor_copy(lane_sum[:, 0, :], run[:, 1, :, CH]).then_inc(lane_ends, 1)
            m_.step(V.tensor_tensor(mendq[:, 0:1], slot_base[:, :], fstart[:, :], ALU.add))
            m_.mark(V.tensor_tensor(mendq[:, 1:2], trash[:, :], mendq[:, 0:1], ALU.subtract))
            m_.step(V.tensor_scalar(mendq[:, 2:3], fstart[:, :], 0.0, None, ALU.is_equal))
            m_.mark(V.scalar_tensor_tensor(mendq[:, 3:4], mendq[:, 1:2], mendq[:, 2:3], mendq[:, 0:1],
                                           ALU.mult, ALU.add))
            m_.mark(V.tensor_scalar(mendu[:, 0:1], mendq[:, 0:1], 0.0, None, ALU.max))
            dve.wait_ge(dve_mend, m_.n)
            V.tensor_copy(mendu[:, 1:2], mendq[:, 3:4]).then_inc(mend_idx, 1)
            m_.mark(V.memset(lmax[:, 0:1], -BIG))
            m_.mark(V.memset(lsum[:, 0:1], 0.0))
            dve.wait_ge(lane_endsT, 1)
            m_.step(V.tensor_copy(laneT[:, :, :], ps_tr[0:SUM_W, 0:3 * P].rearrange("p (n l) -> p n l", n=3)))
            m_.step(V.tensor_scalar(lneg[:, :], laneT[:, 2, :], -BIG, None, ALU.mult))
            m_.step(V.tensor_tensor_scan(lmax[:, 1:P + 1], lneg[:, :], laneT[:, 1, :], -BIG, ALU.add, ALU.max))
            m_.mark(V.tensor_tensor(lexp[:, 1, :], laneT[:, 1, :], lmax[:, 1:P + 1], ALU.subtract))
            m_.step(V.tensor_tensor(lexp[:, 0, :], lmax[:, 0:P], lmax[:, 1:P + 1], ALU.subtract))
            V.tensor_scalar(lexp[:, 0, :], lexp[:, 0, :], 0.0, None, ALU.min).then_inc(lane_expo, 1)
            m_.step(V.tensor_scalar(lneg[:, :], laneT[:, 2, :], -1.0, 1.0, ALU.mult, ALU.add))
            dve.wait_ge(lane_exp, 1)
            m_.mark(V.tensor_tensor(lexp[:, 0, :], lexp[:, 0, :], lneg[:, :], ALU.mult))
            m_.step(V.tensor_tensor(lexp[:, 1, :], lexp[:, 1, :], laneT[:, 0, :], ALU.mult))
            V.tensor_tensor_scan(lsum[:, 1:P + 1], lexp[:, 0, :], lexp[:, 1, :], 0.0, ALU.mult, ALU.add
                                 ).then_inc(lane_carry, 1)
            dve.wait_ge(lane_carryT, 1)
            m_.step(V.tensor_copy(carry[:, :, :],
                                  ps_sc[:, 0, 0:64].rearrange("p (n f) -> p n f", n=2)[:, :, 0:SUM_W]))
            dve.wait_ge(mend_in, 16)
            cmax = carry[:, 1, :].rearrange("p (h e) -> p h e", h=HD)[:, :, 0]
            m_.step(V.tensor_tensor(mmax[:, :], cmax, mrow[:, SUM_W:ROW_W], ALU.max))
            V.tensor_copy(mout[:, SUM_W:ROW_W], mmax[:, :])
            V.tensor_tensor(mexp[:, 0, :], cmax, mmax[:, :], ALU.subtract)
            V.tensor_tensor(mexp[:, 1, :], mrow[:, SUM_W:ROW_W], mmax[:, :], ALU.subtract).then_inc(mend_expo, 1)
            dve.wait_ge(mend_exp, 1)
            for n, part in ((0, carry[:, 0, :]), (1, mrow[:, 0:SUM_W])):
                m_.mark(V.tensor_tensor(mtmp[:, n, :].rearrange("p (h e) -> p h e", h=HD),
                                        part.rearrange("p (h e) -> p h e", h=HD),
                                        mexp[:, n, :].unsqueeze(2).broadcast_to([P, HD, EX + 1]), ALU.mult))
            dve.wait_ge(dve_mend, m_.n)
            V.tensor_tensor(mout[:, 0:SUM_W], mtmp[:, 0, :], mtmp[:, 1, :], ALU.add).then_inc(mend_ready, 1)

            for s in range(2):
                V.tensor_copy(tidx[:, s, :], endT[:, s * TB:(s + 1) * TB]).then_inc(tidx_ready, 1)
            t_ = Chain(dve, dve_tail)
            hs = lambda t: t.rearrange("p k (h e) -> p k h e", h=HD)
            with dve.Fori(0, NB // TB // 2) as i:
                t_.turn(i, 2 * TAIL)
                for s in range(2):
                    n0 = t_.n
                    dve.wait_ge(tail_rows[s], i * (TB * 16) + TB * 16)
                    sums = hs(trow[:, s, :, 0:SUM_W])
                    t_.step(V.tensor_scalar(den[:, :, :], sums[:, :, :, EX], DEN_EPS, None, ALU.add))
                    t_.step(V.reciprocal(den[:, :, :], den[:, :, :]))
                    t_.step(V.tensor_tensor(agg[:, :, :, :], sums[:, :, :, 0:EX],
                                            den[:, :, :].unsqueeze(3).broadcast_to([P, TB, HD, EX]), ALU.mult))
                    ag = agg[:, :, :, :].rearrange("p k h e -> p k (h e)")
                    over_k = lambda v: v.unsqueeze(1).broadcast_to([P, TB, HE])
                    over_f = lambda v: v.unsqueeze(2).broadcast_to([P, TB, HE])
                    t_.step(V.tensor_tensor(ag, ag, over_k(gate_p[:, 0, :]), ALU.add))
                    t_.step(V.tensor_reduce(red[:, 0, :], ag, AX.X, ALU.add))
                    t_.step(V.tensor_scalar(red[:, 1, :], red[:, 0, :], 1.0 / HE, None, ALU.mult))
                    t_.step(V.tensor_tensor(ag, ag, over_f(red[:, 1, :]), ALU.subtract))
                    t_.step(V.tensor_tensor(sq[:, :, :], ag, ag, ALU.mult))
                    t_.step(V.tensor_reduce(red[:, 0, :], sq[:, :, :], AX.X, ALU.add))
                    V.tensor_scalar(red[:, 2, :], red[:, 0, :], 1.0 / HE, LN_EPS, ALU.mult, ALU.add
                                    ).then_inc(tail_var, 1)
                    dve.wait_ge(tail_std, i * 2 + (s + 1))
                    t_.step(V.reciprocal(red[:, 4, :], red[:, 3, :]))
                    t_.step(V.tensor_tensor(ag, ag, over_f(red[:, 4, :]), ALU.mult))
                    t_.step(V.tensor_tensor(ag, ag, over_k(gate_p[:, 1, :]), ALU.mult))
                    t_.step(V.tensor_tensor(ag, ag, over_k(gate_p[:, 2, :]), ALU.add))
                    t_.step(V.tensor_reduce(sc4[:, :, :], agg[:, :, :, :].rearrange("p k h e -> p k e h"), AX.X, ALU.add))
                    t_.step(V.tensor_scalar(sc4[:, :, :], sc4[:, :, :], 1.0 / HD, None, ALU.mult))
                    pair = [P, TB, EX, EX]
                    other = sc4[:, :, :].unsqueeze(2).broadcast_to(pair)
                    own = sc4[:, :, :].unsqueeze(3).broadcast_to(pair)
                    t_.mark(V.tensor_tensor(dif[:, :, :, :], other, own, ALU.is_equal))
                    t_.step(V.tensor_reduce(red[:, 5, :], sc4[:, :, :], AX.X, ALU.max))
                    dif_f = dif[:, :, :, :].rearrange("p k e o -> p k (e o)")
                    t_.mark(V.tensor_tensor(dif_f, dif_f, over_k(tie[:, :, :].rearrange("p e o -> p (e o)")), ALU.mult))
                    t_.step(V.tensor_tensor(agg[:, :, :, :], other, own, ALU.is_gt))
                    V.tensor_tensor(sc4[:, :, :], sc4[:, :, :], red[:, 5, :].unsqueeze(2).broadcast_to([P, TB, EX]),
                                    ALU.subtract).then_inc(tail_sub, 1)
                    t_.step(V.tensor_tensor(dif_f, dif_f, ag, ALU.add))
                    t_.step(V.tensor_reduce(rank[:, :, :], dif[:, :, :, :], AX.X, ALU.add))
                    dve.wait_ge(tail_exp, i * 2 + (s + 1))
                    t_.step(V.scalar_tensor_tensor(gate[:, :, :], rank[:, :, :], 1.5, gate[:, :, :], ALU.is_lt, ALU.mult))
                    t_.step(V.tensor_reduce(red[:, 0, :], gate[:, :, :], AX.X, ALU.add))
                    t_.step(V.reciprocal(red[:, 1, :], red[:, 0, :]))
                    t_.step(V.tensor_tensor(gate[:, :, :], gate[:, :, :],
                                            red[:, 1, :].unsqueeze(2).broadcast_to([P, TB, EX]), ALU.mult))
                    dve.wait_ge(y_loaded[s], i * 16 + 16)
                    t_.step(V.tensor_tensor(gated.rearrange("p k e d -> p (k e) d"),
                                            y_ring[:, s, :, :].rearrange("p k (e d) -> p (k e) d", e=EX),
                                            gate[:, :, :].rearrange("p k e -> p (k e)").unsqueeze(2
                                            ).broadcast_to([P, TB * EX, D]), ALU.mult))
                    V.tensor_copy(tidx[:, s, :], endT[:, bass.ds(i * (2 * TB) + (2 + s) * TB, TB)]).then_inc(tidx_ready, 1)
                    dve.wait_ge(out_stored[s], i * 16)
                    t_.mark(V.tensor_tensor(o_half[:, 0, :, :], gated[:, :, 0, :], gated[:, :, 1, :], ALU.add))
                    t_.step(V.tensor_tensor(o_half[:, 1, :, :], gated[:, :, 2, :], gated[:, :, 3, :], ALU.add))
                    t_.step(V.tensor_tensor(o_half[:, 0, :, :], o_half[:, 0, :, :], o_half[:, 1, :, :], ALU.add))
                    V.tensor_tensor(o_ring[:, s, :, :], o_half[:, 0, :, :],
                                    X[:, bass.ds(i * (2 * TB) + s * TB, TB), :], ALU.add).then_inc(out_ready, 1)
                    assert t_.n - n0 == TAIL, t_.n - n0
                t_.end_turn(NB // TB // 2)


NAMES = ["x", "L0_tok_W", "L0_attn_q_weight", "L0_ffn_W_gat", "L0_ffn_att_src", "L0_ffn_att_dst", "L0_ffn_b_gat",
         "L0_ffn_ln_gamma", "L0_ffn_ln_beta", "L0_ffn_W1", "L0_ffn_b1", "L0_ffn_W2", "L0_ffn_b2"]


def kernel(**inputs):
    import concourse.bacc as bacc
    from concourse.bass_utils import run_bass_kernel_spmd

    x, emb, qw, wgat, asrc, adst, bgat, gamma, beta, w1, b1, w2, b2 = (np.asarray(inputs[n]) for n in NAMES)
    edges = np.asarray(inputs["L0_ffn_edge_index"])
    he = wgat.shape[1]
    arrays = {
        "tok": x.reshape(-1, P).T,
        "emb": emb.T,
        "qw": qw,
        "wgat": wgat,
        "att_src": asrc.reshape(1, he),
        "att_dst": adst.reshape(1, he),
        "b_gat": bgat.reshape(1, he),
        "gamma": gamma.reshape(1, he),
        "beta": beta.reshape(1, he),
        "w1": w1.transpose(1, 0, 2),
        "b1": b1.T,
        "w2": w2.transpose(1, 0, 2),
        "b2": b2.reshape(1, -1),
        "esrc": edges[0].reshape(P, -1),
        "edst": edges[1].reshape(P, -1),
    }
    arrays = {k: np.ascontiguousarray(v) for k, v in arrays.items()}
    nc = bacc.Bacc("TRN2", target_bir_lowering=False, num_devices=1)
    args = [nc.dram_tensor("in_" + k, v.shape, mybir.dt.from_np(v.dtype), kind="ExternalInput").ap()
            for k, v in arrays.items()]
    shape = (x.size, emb.shape[0])
    args.append(nc.dram_tensor("result", shape, F32, kind="ExternalOutput").ap())
    build(nc, *args)
    r = run_bass_kernel_spmd(nc, [{"in_" + k: v for k, v in arrays.items()}], core_ids=[0])
    return r.results[0]["result"].reshape(*x.shape, emb.shape[0])
```

```python
from contextlib import ExitStack

import concourse.bass as bass
from concourse import mybir
import numpy as np

ALU = mybir.AluOpType
ACT = mybir.ActivationFunctionType
AX = mybir.AxisListType
F32 = mybir.dt.float32
BF16 = mybir.dt.bfloat16
I32 = mybir.dt.int32
U32 = mybir.dt.uint32

P = 128
BIG = 1.0e38
LN_EPS = 1e-5
DEN_EPS = 1e-16
SLOPE = 0.2

TAB_W = 32
SUM_W = 20
ROW_W = 24


def build(nc, tok, emb, qw, wgat, att_src, att_dst, b_gat, gamma, beta, w1, b1, w2, b2, esrc, edst, out):
    NB = tok.shape[1]
    NTOK = P * NB
    D = emb.shape[1]
    HE = wgat.shape[1]
    EX, HID = w1.shape[1], w1.shape[2]
    HD = HE // EX
    EB = esrc.shape[1]
    NSLOT = P * (EB + NB)
    LANE = NSLOT // P
    FLAG = NTOK
    BATCHES = NB // 2
    GRP = 4
    STEPS = EB // BATCHES // GRP
    HALF = STEPS // 2 * GRP
    CH = LANE // P
    assert (D, HE, EX, HID) == (64, 16, 4, 128) and NB == P and STEPS == 8
    assert CH == HALF + 1 and CH * P == LANE and HD * (EX + 1) == SUM_W

    srt = nc.dram_tensor("sorted_sources", [NSLOT, 1], I32, kind="Internal").ap()
    table = nc.dram_tensor("node_table", [NTOK, TAB_W], F32, kind="Internal").ap()
    rows = nc.dram_tensor("slot_rows", [NSLOT + P, ROW_W], F32, kind="Internal").ap()
    yexp = nc.dram_tensor("expert_rows", [P, NB, EX * D], F32, kind="Internal").ap()

    with ExitStack() as ctx:
        def sb(name, shape, dt=F32):
            return ctx.enter_context(nc.sbuf_tensor(name, shape, dt))

        def ps(name, shape, dt=F32):
            return ctx.enter_context(nc.psum_tensor(name, shape, dt))

        def sem(name):
            return ctx.enter_context(nc.semaphore(name))

        iota2 = sb("iota2", [P, P, 2], BF16)
        ident_b = sb("ident_b", [P, P], BF16)
        ident_f = sb("ident_f", [P, P])
        before = sb("before", [P, P])
        zero_b = sb("zero_b", [P, P], BF16)
        ones_f = sb("ones_f", [P, P])
        lane_start = sb("lane_start", [P, P])
        slot_base = sb("slot_base", [P, 1])
        trash = sb("trash", [P, 1])
        flat_id = sb("flat_id", [P, P])
        col_no = sb("col_no", [P, LANE], mybir.dt.int16)

        qw_s = sb("qw_s", [D, D])
        wg_s = sb("wg_s", [D, HE])
        w1_s = sb("w1_s", [D, EX, HID])
        w2_s = sb("w2_s", [HID, EX, D])
        b1_s = sb("b1_s", [HID, EX])
        b2_s = sb("b2_s", [1, EX * D])
        att_s = sb("att_s", [P, 2, HE])
        gate_p = sb("gate_p", [P, 3, HE])

        ids = sb("ids", [P, NB + 4], I32)
        keep = sb("keep", [P, NB + 4])
        eidx = sb("eidx", [P, 2, 2], U32)
        erow = sb("erow", [P, 2, 2, D])
        X = sb("X", [P, NB + 2, D])
        big = sb("big", [P, NTOK])
        xn2T = big[0:D, :]
        y_ring = big[:, 0:2 * 16 * EX * D].rearrange("p (s k f) -> p s k f", s=2, k=16)
        gated = big[:, 8192:8192 + 16 * EX * D].rearrange("p (k e d) -> p k e d", k=16, e=EX)
        o_ring = big[:, 12288:12288 + 2 * 16 * D].rearrange("p (s k d) -> p s k d", s=2, k=16)
        o_half = big[:, 14336:14336 + 2 * 16 * D].rearrange("p (s k d) -> p s k d", s=2, k=16)

        src = sb("src", [P, LANE], I32)
        key = src[:, :].bitcast(F32)
        dst = big[:, 0:EB].bitcast(I32)
        digit_i = big[:, EB:2 * EB].bitcast(I32)
        digit = sb("digit", [P, EB // 2 + 4, 2, 2], BF16)
        onehot = sb("onehot", [P, 2, 8, P, 2], BF16)
        hot_ring = onehot[:, :, :, :, :].rearrange("p s (q u) n b -> p (s q) u n b", q=2)
        hist = sb("hist", [P, P])
        incl = sb("incl", [P, P])
        rowsum = sb("rowsum", [P, 1])
        rowoff = sb("rowoff", [P, 1])
        off = sb("off", [P, P])
        off1 = sb("off1", [P, P])
        off2 = sb("off2", [P, P])
        hist_even = sb("hist_even", [P, P])
        end = sb("end", [P, P])
        offT = sb("offT", [P, P])
        endT = sb("endT", [P, NB + 32], U32)
        hiT = sb("hiT", [P, 2, GRP, P])
        hiT_b = sb("hiT_b", [P, GRP, P], BF16)
        same = sb("same", [P, 2, GRP, P], BF16)
        count = sb("count", [P, GRP, P])
        picked = sb("picked", [P, GRP, P])
        slotf = sb("slotf", [P, 2, HALF])
        sidx = sb("sidx", [P, 2, HALF], U32)
        spay = sb("spay", [P, 2, HALF], I32)

        stats = sb("stats", [P, 2, 2, 6])
        mv = sb("mv", [P, 2, 2, 2])
        vare = sb("vare", [P, 2, 2])
        std = sb("std", [P, 2, 2])
        rstd = sb("rstd", [P, 2, 2])
        xcur = sb("xcur", [P, 2, D])
        xn = sb("xn", [P, 2, D])
        xn2 = sb("xn2", [P, 2, D])
        xnT = sb("xnT", [D, 2 * P])
        xnT2 = sb("xnT2", [D, 2 * P])
        qT = sb("qT", [D, 2 * P])
        att = sb("att", [P, 2, 2 * P])
        tabt = sb("tabt", [P, 2, TAB_W])
        hatt = sb("hatt", [P, 2, 2, HE])

        srt_s = sb("srt_s", [P, LANE + 2 * CH], I32)
        cmp = onehot[:, :, :, :, :].rearrange("p s u n b -> p (s u n b)").rearrange("p (j n) -> p j n", n=P)
        cnt = sb("cnt", [P, P])
        start = sb("start", [P, 2, CH + 1])
        node = sb("node", [P, 2, CH + 1])
        self_id = sb("self_id", [P, 2, CH])
        first_u = sb("first_u", [P, 1], U32)
        first_row = sb("first_row", [P, TAB_W])
        gidx = sb("gidx", [P, 2, CH], U32)
        grow = sb("grow", [P, 2, CH, TAB_W])
        keep4 = sb("keep4", [P, 2, HD, CH + 1])
        neg4 = sb("neg4", [P, 2, HD, CH + 1])
        ad_in = sb("ad_in", [P, 2, HD, CH + 1])
        ad = sb("ad", [P, 2, HD, CH + 1])
        e_raw = sb("e_raw", [P, 2, HD, CH])
        e_in = sb("e_in", [P, 2, HD, CH + 1])
        mx = sb("mx", [P, 2, HD, CH + 1])
        expo = sb("expo", [P, 2, 2 * HD, CH])
        ex = sb("ex", [P, 2, 2 * HD, CH])
        decay = sb("decay", [P, 2, SUM_W, CH + 1])
        add = sb("add", [P, 2, SUM_W, CH + 1])
        run = sb("run", [P, 2, SUM_W, CH + 1])
        orow = sb("orow", [P, 2, CH, ROW_W])
        hid = hiT[:, :, :, :].rearrange("p s b n -> p (s b n)").rearrange("p (e n) -> p e n", e=EX)
        y_out = sb("y_out", [P, 2, EX * D])

        lane_sum = sb("lane_sum", [P, 3, SUM_W])
        laneT = sb("laneT", [SUM_W, 3, P])
        lneg = sb("lneg", [SUM_W, P])
        lmax = sb("lmax", [SUM_W, P + 1])
        lexp = sb("lexp", [SUM_W, 2, P])
        lsum = sb("lsum", [SUM_W, P + 1])
        carry = sb("carry", [P, 2, SUM_W])
        fstart = sb("fstart", [P, 1])
        mendq = sb("mendq", [P, 4])
        mendu = sb("mendu", [P, 2], U32)
        mrow = sb("mrow", [P, ROW_W])
        mmax = sb("mmax", [P, HD])
        mexp = sb("mexp", [P, 2, HD])
        mtmp = sb("mtmp", [P, 2, SUM_W])
        mout = sb("mout", [P, ROW_W])

        TB = 16
        tidx = sb("tidx", [P, 2, TB], U32)
        trow = sb("trow", [P, 2, TB, ROW_W])
        den = sb("den", [P, TB, HD])
        agg = sb("agg", [P, TB, HD, EX])
        sq = sb("sq", [P, TB, HE])
        red = sb("red", [P, 6, TB])
        sc4 = sb("sc4", [P, TB, EX])
        dif = sb("dif", [P, TB, EX, EX])
        tie = sb("tie", [P, EX, EX])
        rank = sb("rank", [P, TB, EX])
        gate = sb("gate", [P, TB, EX])

        cnt_bank = [ps(f"ps_cnt{h}", [P, 512]) for h in range(2)]
        ps_cnt = [t[:, 0:P] for t in cnt_bank]
        ps_hiT = ps("ps_hiT", [P, 2, GRP, P], BF16)
        ps_same = ps("ps_same", [P, GRP, P])
        ps_slot = ps("ps_slot", [P, 2, GRP, P])
        ps_tr = ps("ps_tr", [P, 512])
        ps_sc = ps("ps_sc", [P, 2, 2 * P])
        ps_hid = [ps_slot[:, 0, 0:2, :].rearrange("p a b -> p (a b)"), ps_slot[:, 1, 0:2, :].rearrange("p a b -> p (a b)"),
                  ps_sc[:, 0, :], cnt_bank[0][:, 0:2 * P]]
        ps_y = ps_same[:, :, :].rearrange("p g n -> p (g n)").rearrange("p (a f) -> p a f", a=2)

        loaded = sem("loaded")
        waits_passed = sem("waits_passed")
        spare_rows = sem("spare_rows")
        blank_ready = sem("blank_ready")
        list_blank = sem("list_blank")
        edges_in = sem("edges_in")
        consts = sem("consts")
        consts2 = sem("consts2")
        prep = sem("prep")
        prep2 = sem("prep2")
        eidx_ready = sem("eidx_ready")
        emb_rows = [sem(f"emb_rows{s}") for s in range(2)]
        emb_kept = sem("emb_kept")
        hot_ready = sem("hot_ready")
        hist_done = sem("hist_done")
        off_mm = sem("off_mm")
        off_ready = sem("off_ready")
        oh_ready = sem("oh_ready")
        hiT_mm = sem("hiT_mm")
        hiT_ready = sem("hiT_ready")
        same_mm = sem("same_mm")
        same_ready = sem("same_ready")
        count_ready = sem("count_ready")
        counted = sem("counted")
        slot_mm = sem("slot_mm")
        slot_ready = sem("slot_ready")
        sidx_part = sem("sidx_part")
        sidx_ready = sem("sidx_ready")
        scattered = [sem(f"scattered{s}") for s in range(2)]
        var_ready = sem("var_ready")
        std_ready = sem("std_ready")
        norm_ready = sem("norm_ready")
        normT_mm = sem("normT_mm")
        normT_ready = sem("normT_ready")
        normT_kept = sem("normT_kept")
        q_mm = sem("q_mm")
        q_ready = sem("q_ready")
        score_mm = sem("score_mm")
        att_ready = sem("att_ready")
        value_mm = sem("value_mm")
        gat_mm = sem("gat_mm")
        table_ready = sem("table_ready")
        table_stored = sem("table_stored")
        dve_att = sem("dve_att")
        sorted_in = sem("sorted_in")
        lane_mm = sem("lane_mm")
        first_ready = sem("first_ready")
        first_in = sem("first_in")
        gidx_ready = sem("gidx_ready")
        gathered = [sem(f"gathered{s}") for s in range(2)]
        dve_str = sem("dve_str")
        expo_ready = sem("expo_ready")
        exp_ready = sem("exp_ready")
        run_ready = sem("run_ready")
        orow_ready = sem("orow_ready")
        orow_stored = [sem(f"orow_stored{s}") for s in range(2)]
        hid_mm = sem("hid_mm")
        hid_ready = sem("hid_ready")
        y_mm = sem("y_mm")
        y_ready = sem("y_ready")
        y_stored = sem("y_stored")
        dve_mend = sem("dve_mend")
        lane_ends = sem("lane_ends")
        lane_endsT = sem("lane_endsT")
        lane_expo = sem("lane_expo")
        lane_exp = sem("lane_exp")
        lane_carry = sem("lane_carry")
        lane_carryT = sem("lane_carryT")
        mend_idx = sem("mend_idx")
        mend_expo = sem("mend_expo")
        mend_exp = sem("mend_exp")
        mend_ready = sem("mend_ready")
        mend_in = sem("mend_in")
        mend_out = sem("mend_out")
        tidx_ready = sem("tidx_ready")
        tail_rows = [sem(f"tail_rows{s}") for s in range(2)]
        dve_tail = sem("dve_tail")
        y_loaded = [sem(f"y_loaded{s}") for s in range(2)]
        tail_var = sem("tail_var")
        tail_std = sem("tail_std")
        tail_sub = sem("tail_sub")
        tail_exp = sem("tail_exp")
        out_ready = sem("out_ready")
        out_stored = [sem(f"out_stored{s}") for s in range(2)]

        block = ctx.enter_context(nc.Block())

        TAIL = 29
        PREP2 = 8

        class Chain:

            def __init__(self, eng, s, base=0):
                self.eng, self.s, self.base, self.n, self.at = eng, s, base, 0, 0

            def turn(self, i, per_turn):
                self.at, self.per, self.n = i * per_turn, per_turn, 0

            def mark(self, ins):
                ins.then_inc(self.s, 1)
                self.n += 1
                return self.at + (self.base + self.n)

            def step(self, ins):
                self.eng.wait_ge(self.s, self.mark(ins))

            def end_turn(self, turns):
                assert self.n == self.per, (self.n, self.per)
                self.at, self.base, self.n = 0, self.base + turns * self.per, 0

        def lone_wait(eng, s, value):
            eng.wait_ge(s, value)
            eng.sem_inc(waits_passed, 1)

        def hot(s, b, d):
            return hot_ring[:, s, b // 2 * 2 + d, :, b % 2]

        @block.sync
        def _(sp):
            sp.dma_start(dst, edst).then_inc(edges_in, 16)
            sp.dma_start(ids[:, 0:NB], tok).then_inc(loaded, 16)
            sp.dma_start(w1_s[:, :, :], w1).then_inc(table_stored, 16)
            sp.dma_start(w2_s[:, :, :], w2).then_inc(orow_stored[0], 16)
            sp.dma_start(b1_s[:, :], b1).then_inc(orow_stored[1], 16)
            sp.dma_start(b2_s[:, :], b2).then_inc(y_stored, 16)
            for t, a in ((att_s[:, 0, :], att_src), (att_s[:, 1, :], att_dst), (gate_p[:, 0, :], b_gat),
                         (gate_p[:, 1, :], gamma), (gate_p[:, 2, :], beta)):
                sp.dma_start(t, a.broadcast_to([P, HE])).then_inc(loaded, 16)

            sp.wait_ge(consts2, 3)
            sp.dma_start(rows[NSLOT:NSLOT + P, :], ones_f[:, 0:ROW_W]).then_inc(spare_rows, 16)
            sp.wait_ge(blank_ready, 1)
            sp.dma_start(srt[:, :].rearrange("(p t) o -> p (t o)", p=P), srt_s[:, 0:LANE]).then_inc(list_blank, 16)
            tab_v = table.rearrange("(k p) f -> p k f", p=P)
            with sp.Fori(0, BATCHES) as i:
                sp.wait_ge(table_ready, i + 1)
                sp.dma_start(tab_v[:, bass.ds(i * 2, 2), :], tabt[:, :, :]).then_inc(table_stored, 16)

            for s in range(2):
                sp.wait_ge(scattered[s], 16 + BATCHES * HALF * 16)
            sp.dma_start(srt_s[:, 0:LANE], srt[:, :].rearrange("(p t) o -> p (t o)", p=P)).then_inc(sorted_in, 16)

            rows_v = rows[0:NSLOT, :].rearrange("(p t) f -> p t f", p=P)
            with sp.Fori(0, BATCHES) as i:
                for s in range(2):
                    sp.wait_ge(orow_ready, i * 2 + (s + 2))
                    sp.dma_start(rows_v[:, bass.ds(i * (2 * CH) + s * CH, CH), :],
                                 orow[:, s, :, :]).then_inc(orow_stored[s], 16)
                sp.wait_ge(y_ready, i + 2)
                sp.dma_start(yexp[:, bass.ds(i * 2, 2), :], y_out[:, :, :]).then_inc(y_stored, 16)

            sp.wait_ge(y_stored, 16 + BATCHES * 16)
            with sp.Fori(0, NB // TB // 2) as i:
                for s in range(2):
                    sp.wait_ge(tidx_ready, i * 2 + (s + 1))
                    sp.dma_start(y_ring[:, s, :, :],
                                 yexp[:, bass.ds(i * (2 * TB) + s * TB, TB), :]).then_inc(y_loaded[s], 16)

        @block.gpsimd
        def _(pool):
            pool.iota(iota2[:, :, :], [[1, P], [0, 2]], base=0, channel_multiplier=0,
                      allow_small_or_imprecise_dtypes=True).then_inc(consts, 1)
            for s in range(2):
                pool.dma_start(src[:, s * (EB // 2):(s + 1) * (EB // 2)], esrc[:, s * (EB // 2):(s + 1) * (EB // 2)]
                               ).then_inc(scattered[s], 16)
            pool.memset(ident_b[:, :], 0.0).then_inc(consts2, 1)
            pool.memset(ident_f[:, :], 0.0).then_inc(consts2, 1)
            pool.memset(ones_f[:, :], 1.0).then_inc(consts2, 1)
            pool.memset(zero_b[:, :], 0.0).then_inc(consts, 1)
            pool.wait_ge(consts2, 3)
            pool.affine_select(out=ident_b[:, :], in_=ident_b[:, :], compare_op=ALU.not_equal, fill=1.0, base=0,
                               pattern=[[-1, P]], channel_multiplier=1).then_inc(consts, 1)
            pool.affine_select(out=ident_f[:, :], in_=ident_f[:, :], compare_op=ALU.not_equal, fill=1.0, base=0,
                               pattern=[[-1, P]], channel_multiplier=1).then_inc(consts, 1)
            pool.affine_select(out=before[:, :], in_=ones_f[:, :], compare_op=ALU.is_gt, fill=0.0, base=0,
                               pattern=[[1, P]], channel_multiplier=-1).then_inc(consts, 1)
            pool.iota(flat_id[:, :], [[1, P]], base=0, channel_multiplier=P,
                      allow_small_or_imprecise_dtypes=True).then_inc(consts, 1)
            pool.memset(srt_s[:, :], FLAG).then_inc(blank_ready, 1)
            with pool.Fori(0, NB // 4) as i:
                for s in range(2):
                    lone_wait(pool, eidx_ready, i * 2 + (s + 1))
                    for a in range(2):
                        pool.indirect_dma_start(erow[:, s, a, :], None, emb,
                                                bass.IndirectOffsetOnAxis(ap=eidx[:, s, a:a + 1], axis=0)
                                                ).then_inc(emb_rows[s], 16)
            pool.iota(lane_start[:, :], [[LANE, P]], base=0, channel_multiplier=0,
                      allow_small_or_imprecise_dtypes=True).then_inc(consts, 1)
            pool.iota(slot_base[:, :], [[0, 1]], base=-1, channel_multiplier=LANE,
                      allow_small_or_imprecise_dtypes=True).then_inc(consts, 1)
            pool.iota(trash[:, :], [[0, 1]], base=NSLOT, channel_multiplier=1,
                      allow_small_or_imprecise_dtypes=True).then_inc(consts, 1)
            pool.iota(col_no[:, :], [[1, LANE]], base=0, channel_multiplier=0,
                      allow_small_or_imprecise_dtypes=True).then_inc(consts, 1)
            pool.affine_select(out=tie[:, :, :], in_=ones_f[:, 0:EX * EX].rearrange("p (a b) -> p a b", a=EX),
                               compare_op=ALU.is_gt, fill=0.0, base=0, pattern=[[1, EX], [-1, EX]],
                               channel_multiplier=0).then_inc(consts, 1)

            pool.wait_ge(list_blank, 16)
            with pool.Fori(0, BATCHES) as i:
                for s in range(2):
                    lone_wait(pool, sidx_ready, i * 2 + (s + 2))
                    for c in range(HALF):
                        pool.indirect_dma_start(srt, bass.IndirectOffsetOnAxis(ap=sidx[:, s, c:c + 1], axis=0),
                                                spay[:, s, c:c + 1], None).then_inc(scattered[s], 16)

            pool.wait_ge(first_ready, 1)
            pool.wait_ge(table_stored, 16 + BATCHES * 16)
            pool.indirect_dma_start(first_row[:, :], None, table,
                                    bass.IndirectOffsetOnAxis(ap=first_u[:, 0:1], axis=0)).then_inc(first_in, 16)
            with pool.Fori(0, BATCHES) as i:
                for s in range(2):
                    lone_wait(pool, gidx_ready, i * 2 + (s + 1))
                    for c in range(CH):
                        pool.indirect_dma_start(grow[:, s, c, :], None, table,
                                                bass.IndirectOffsetOnAxis(ap=gidx[:, s, c:c + 1], axis=0)
                                                ).then_inc(gathered[s], 16)

            for s in range(2):
                pool.wait_ge(orow_stored[s], 16 + BATCHES * 16)
            pool.wait_ge(spare_rows, 16)
            pool.wait_ge(mend_idx, 1)
            pool.indirect_dma_start(mrow[:, :], None, rows,
                                    bass.IndirectOffsetOnAxis(ap=mendu[:, 0:1], axis=0)).then_inc(mend_in, 16)
            pool.wait_ge(mend_ready, 1)
            pool.indirect_dma_start(rows, bass.IndirectOffsetOnAxis(ap=mendu[:, 1:2], axis=0),
                                    mout[:, :], None).then_inc(mend_out, 16)
            pool.wait_ge(mend_out, 16)

            with pool.Fori(0, NB // TB // 2) as i:
                for s in range(2):
                    lone_wait(pool, tidx_ready, i * 2 + (s + 1))
                    for c in range(TB):
                        pool.indirect_dma_start(trow[:, s, c, :], None, rows,
                                                bass.IndirectOffsetOnAxis(ap=tidx[:, s, c:c + 1], axis=0)
                                                ).then_inc(tail_rows[s], 16)

        @block.tensor
        def _(pe):
            pe.wait_ge(consts, 6)
            for h in range(2):
                m = pe.matmul(ps_cnt[h], zero_b[:, :], zero_b[:, :], start=True, stop=True, skip_group_check=True)
            m.then_inc(hist_done, 2)
            with pe.Fori(0, EB // 64) as i:
                for j in range(8):
                    pe.wait_ge(hot_ready, i * 8 + (j + 1))
                    for b in range(8):
                        m = pe.matmul(ps_cnt[b % 2], onehot[:, j % 2, :, :, :][:, b // 2 * 2, :, b % 2],
                                      onehot[:, j % 2, :, :, :][:, b // 2 * 2 + 1, :, b % 2],
                                      start=False, stop=True, skip_group_check=True)
                    m.then_inc(hist_done, 1)
            pe.wait_ge(off_ready, 1)
            pe.matmul(ps_tr[:, 0:1], before[:, :], rowsum[:, :], start=True, stop=True).then_inc(off_mm, 1)
            pe.wait_ge(off_ready, 2)
            pe.transpose(ps_tr[:, 128:256], off[:, :], ident_f[:, :])
            pe.transpose(ps_tr[:, 256:384], end[:, :], ident_f[:, :]).then_inc(off_mm, 1)
            pe.matmul(ps_cnt[0], ident_f[:, :], off1[:, :], start=True, stop=True,
                      skip_group_check=True).then_inc(counted, 1)
            pe.matmul(ps_cnt[1], ident_f[:, :], off2[:, :], start=True, stop=True,
                      skip_group_check=True).then_inc(counted, 1)

            def hi_transposes(grp, s, slot):
                pe.wait_ge(oh_ready, grp + 1)
                for b in range(GRP):
                    m = pe.transpose(ps_hiT[:, s, b, :], hot(slot, b, 0), ident_b[:, :])
                m.then_inc(hiT_mm, 1)

            def same_high(grp, s):
                pe.wait_ge(hiT_ready, grp + 1)
                for b in range(GRP):
                    m = pe.matmul(ps_same[:, b, :], hiT_b[:, b, :], hiT_b[:, b, :], start=True, stop=True)
                m.then_inc(same_mm, 1)

            def attend(i, t):
                if t == 4 or t == 24:
                    n = t // 24
                    x_ = (xn, xn2)[n]
                    lone_wait(pe, norm_ready, i * 2 + (n + 1))
                    pe.transpose(ps_tr[0:D, 0:P], x_[:, 0, :], ident_f[:, :])
                    pe.transpose(ps_tr[0:D, P:2 * P], x_[:, 1, :], ident_f[:, :]).then_inc(normT_mm, 1)
                if t == 8:
                    lone_wait(pe, normT_ready, i * 2 + 1)
                    pe.matmul(ps_tr[0:D, 256:512], qw_s[:, :], xnT[:, :], start=True, stop=True).then_inc(q_mm, 1)
                if t == 12:
                    pe.wait_ge(q_ready, i + 1)
                    for m in range(2):
                        last = pe.matmul(ps_sc[:, m, :], xnT[:, m * P:(m + 1) * P], qT[:, :], start=True, stop=True)
                    last.then_inc(score_mm, 1)
                if t == 17:
                    pe.wait_ge(att_ready, i + 1)
                    for n in range(2):
                        for m in range(2):
                            last = pe.matmul(ps_tr[:, n * D:(n + 1) * D], att[:, m, n * P:(n + 1) * P],
                                             xn[:, m, :], start=(m == 0), stop=(m == 1))
                    last.then_inc(value_mm, 1)
                if t == 28:
                    pe.wait_ge(normT_ready, i * 2 + 2)
                    for n in range(2):
                        last = pe.matmul(ps_tr[:, 256 + n * HE:256 + (n + 1) * HE], xnT2[:, n * P:(n + 1) * P],
                                         wg_s[:, :], start=True, stop=True)
                    last.then_inc(gat_mm, 1)

            hi_transposes(0, 0, 0)
            same_high(0, 0)
            pe.matmul(ps_slot[:, 0, 0, :], zero_b[:, :], zero_b[:, :], start=True, stop=True,
                      skip_group_check=True).then_inc(slot_mm, 1)
            with pe.Fori(0, BATCHES) as i:
                for g in range(STEPS):
                    s = g % 2
                    pe.wait_ge(hiT_ready, i * STEPS + (g + 1))
                    hi_transposes(i * STEPS + (g + 1), 1 - s, (g + 1) % 4)
                    for b in range(GRP):
                        if b == 0:
                            pe.wait_ge(same_ready, i * STEPS + (g + 1))
                        pe.wait_ge(slot_ready, i * (STEPS * GRP) + (GRP * g + b + 1))
                        pe.matmul(ps_slot[:, b % 2, 0, :], same[:, s, b, :], hot(g % 4, b, 1), start=True, stop=False)
                        pe.wait_ge(count_ready, i * (STEPS * GRP) + (GRP * g + b + 1))
                        pe.matmul(ps_cnt[b % 2], hot(g % 4, b, 0), hot(g % 4, b, 1), start=False, stop=True,
                                  skip_group_check=True).then_inc(counted, 1)
                        pe.matmul(ps_slot[:, b % 2, 0, :], hiT[:, s, b, :], count[:, b, :],
                                  start=False, stop=True).then_inc(slot_mm, 1)
                        if b == 1:
                            pe.wait_ge(same_ready, i * STEPS + (g + 1))
                            same_high(i * STEPS + (g + 1), 1 - s)
                        attend(i, GRP * g + b)

            pe.wait_ge(prep2, PREP2)
            pe.matmul(ps_tr[:, 0:1], cnt[:, :], ones_f[:, 0:1], start=True, stop=True).then_inc(lane_mm, 1)

            pe.matmul(ps_y[:, 0, 0:P], zero_b[:, :], zero_b[:, :], start=True, stop=True,
                      skip_group_check=True).then_inc(y_mm, 1)
            with pe.Fori(0, BATCHES) as i:
                pe.wait_ge(hid_ready, i * EX + 1)
                for e in range(EX):
                    pe.matmul(ps_hid[e], w1_s[:, e, :], xn2T[:, bass.ds(i * (2 * P), 2 * P)],
                              start=True, stop=True).then_inc(hid_mm, 1)
                pe.wait_ge(y_ready, i + 1)
                for a in range(2):
                    for e in range(EX):
                        if a == 0:
                            pe.wait_ge(hid_ready, i * EX + (e + 2))
                        pe.matmul(ps_y[:, a, e * D:(e + 1) * D], hid[:, e, a * P:(a + 1) * P], w2_s[:, e, :],
                                  start=True, stop=False)
                        last = pe.matmul(ps_y[:, a, e * D:(e + 1) * D], ones_f[0:1, :], b2_s[0:1, e * D:(e + 1) * D],
                                         start=False, stop=True)
                last.then_inc(y_mm, 1)

            pe.wait_ge(lane_ends, 1)
            for n in range(3):
                last = pe.transpose(ps_tr[0:SUM_W, n * P:(n + 1) * P], lane_sum[:, n, :], ident_f[:, :])
            last.then_inc(lane_endsT, 1)
            pe.wait_ge(lane_carry, 1)
            pe.transpose(ps_sc[:, 0, 0:SUM_W], lsum[:, 0:P], ident_f[0:SUM_W, 0:SUM_W])
            pe.transpose(ps_sc[:, 0, 32:32 + SUM_W], lmax[:, 0:P], ident_f[0:SUM_W, 0:SUM_W]).then_inc(lane_carryT, 1)

        @block.scalar
        def _(act):
            act.dma_start(qw_s[:, :], qw).then_inc(out_stored[0], 16)
            act.dma_start(wg_s[:, :], wgat).then_inc(out_stored[1], 16)
            act.wait_ge(loaded, 16 * 6)
            for s_ in (table_stored, orow_stored[0], orow_stored[1], y_stored, out_stored[0], out_stored[1]):
                act.wait_ge(s_, 16)
            act.wait_ge(prep, 2)
            for s in range(2):
                act.activation(eidx[:, s, :], ids[:, 2 * s:2 * s + 2], ACT.Copy).then_inc(eidx_ready, 1)
            with act.Fori(0, NB // 4) as i:
                for s in range(2):
                    act.wait_ge(emb_rows[s], i * 32 + 32)
                    for a in range(2):
                        k = i * 4 + (2 * s + a)
                        act.activation(X[:, bass.ds(k, 1), :].rearrange("p o d -> p (o d)"), erow[:, s, a, :],
                                       ACT.Copy, scale=keep[:, bass.ds(k, 1)]).then_inc(emb_kept, 1)
                    act.activation(eidx[:, s, :], ids[:, bass.ds(i * 4 + (4 + 2 * s), 2)], ACT.Copy
                                   ).then_inc(eidx_ready, 1)

            def copy_hiT(grp, s):
                act.wait_ge(hiT_mm, grp + 1)
                act.activation(hiT_b[:, :, :], ps_hiT[:, s, :, :], ACT.Copy)
                act.activation(hiT[:, s, :, :], ps_hiT[:, s, :, :], ACT.Copy).then_inc(hiT_ready, 1)

            def std_of(i, n):
                act.wait_ge(var_ready, i * 2 + (n + 1))
                act.activation(std[:, n, :], vare[:, n, :], ACT.Sqrt).then_inc(std_ready, 1)

            def attend(i, t):
                if t == 7:
                    act.wait_ge(normT_mm, i * 2 + 1)
                    act.activation(xnT[:, :], ps_tr[0:D, 0:2 * P], ACT.Copy).then_inc(normT_ready, 1)
                if t == 11:
                    act.wait_ge(q_mm, i + 1)
                    act.activation(qT[:, :], ps_tr[0:D, 256:512], ACT.Copy).then_inc(q_ready, 1)
                if t == 15:
                    act.wait_ge(score_mm, i + 1)
                    act.activation(att[:, :, :], ps_sc[:, :, :], ACT.Sigmoid).then_inc(att_ready, 1)
                if t == 20:
                    std_of(i, 1)
                if t == 27:
                    act.wait_ge(normT_mm, i * 2 + 2)
                    act.activation(xnT2[:, :], ps_tr[0:D, 0:2 * P], ACT.Copy).then_inc(normT_ready, 1)
                if t == 29:
                    act.wait_ge(normT_ready, i * 2 + 2)
                    act.activation(xn2T[:, bass.ds(i * (2 * P), 2 * P)], xnT2[:, :], ACT.Copy
                                   ).then_inc(normT_kept, 1)

            copy_hiT(0, 0)
            with act.Fori(0, BATCHES) as i:
                std_of(i, 0)
                for g in range(STEPS):
                    s = g % 2
                    for b in range(GRP):
                        if b == 2:
                            act.wait_ge(slot_mm, i * (STEPS * GRP) + (GRP * g + 1))
                            copy_hiT(i * STEPS + (g + 1), 1 - s)
                        act.wait_ge(counted, i * (STEPS * GRP) + (GRP * g + b + 1))
                        act.activation(count[:, b, :], ps_cnt[b % 2], ACT.Copy).then_inc(count_ready, 1)
                        attend(i, GRP * g + b)

            act.wait_ge(slot_mm, EB + 1)
            act.activation(hid[:, 0, 0:EX], b1_s[:, :], ACT.Copy).then_inc(hid_ready, 1)
            act.activation(y_out[:, 0, 0:EX], b1_s[:, :], ACT.Copy).then_inc(y_ready, 1)
            act.activation(orow[:, 0, 0, 0:EX], b1_s[:, :], ACT.Copy).then_inc(orow_ready, 1)
            with act.Fori(0, BATCHES) as i:
                for s in range(2):
                    act.wait_ge(expo_ready, i * 2 + (s + 1))
                    act.activation(ex[:, s, :, :], expo[:, s, :, :], ACT.Exp).then_inc(exp_ready, 1)
                    act.wait_ge(run_ready, i * 2 + (s + 1))
                    act.wait_ge(orow_stored[s], i * 16 + 16)
                    act.activation(orow[:, s, :, 0:SUM_W].rearrange("p t f -> p f t"),
                                   run[:, s, :, 1:CH + 1], ACT.Copy)
                    act.activation(orow[:, s, :, SUM_W:ROW_W].rearrange("p t f -> p f t"),
                                   mx[:, s, :, 1:CH + 1], ACT.Copy).then_inc(orow_ready, 1)
                act.wait_ge(y_mm, i + 1)
                for e in range(EX):
                    act.wait_ge(hid_mm, i * EX + (e + 1))
                    act.activation(hid[:, e, :], ps_hid[e], ACT.Gelu, bias=b1_s[:, e:e + 1]).then_inc(hid_ready, 1)
                act.wait_ge(y_mm, i + 2)
                act.wait_ge(y_stored, i * 16 + 16)
                act.activation(y_out[:, :, :], ps_y, ACT.Copy).then_inc(y_ready, 1)

            act.wait_ge(lane_expo, 1)
            act.activation(lexp[:, :, :], lexp[:, :, :], ACT.Exp).then_inc(lane_exp, 1)
            act.wait_ge(mend_expo, 1)
            act.activation(mexp[:, :, :], mexp[:, :, :], ACT.Exp).then_inc(mend_exp, 1)

            out_v = out.rearrange("(k p) d -> p k d", p=P)
            with act.Fori(0, NB // TB // 2) as i:
                for s in range(2):
                    act.wait_ge(tail_var, i * 2 + (s + 1))
                    act.activation(red[:, 3, :], red[:, 2, :], ACT.Sqrt).then_inc(tail_std, 1)
                    act.wait_ge(tail_sub, i * 2 + (s + 1))
                    act.activation(gate[:, :, :], sc4[:, :, :], ACT.Exp).then_inc(tail_exp, 1)
                    act.wait_ge(out_ready, i * 2 + (s + 1))
                    act.dma_start(out_v[:, bass.ds(i * (2 * TB) + s * TB, TB), :], o_ring[:, s, :, :]
                                  ).then_inc(out_stored[s], 16)
            for s in range(2):
                act.wait_ge(out_stored[s], 16 + NB // TB // 2 * 16)

        @block.vector
        def _(dve):
            V = nc.vector
            c = Chain(dve, prep)
            c.mark(V.memset(ids[:, NB:NB + 4], 0))
            dve.wait_ge(loaded, 16 * 6)
            c.mark(V.tensor_scalar(keep[:, 0:NB], ids[:, 0:NB], 0, None, ALU.not_equal))
            c.mark(V.memset(digit[:, EB // 2:EB // 2 + 4, :, :], 0.0))
            dve.wait_ge(edges_in, 16)
            c.step(V.tensor_scalar(digit_i, dst, 7, None, ALU.logical_shift_right))
            c.step(V.tensor_copy(digit[:, 0:EB // 2, 0, :], digit_i.rearrange("p (a b) -> p a b", b=2)))
            c.step(V.tensor_scalar(digit_i, dst, P - 1, None, ALU.bitwise_and))
            c.step(V.tensor_copy(digit[:, 0:EB // 2, 1, :], digit_i.rearrange("p (a b) -> p a b", b=2)))
            dve.wait_ge(consts, 6)

            def one_hots(pair, to):
                units = to.shape[1]
                d = digit[:, bass.ds(pair, units // 2), :, :].rearrange("p a h b -> p (a h) b")
                return V.tensor_tensor(to,
                                       iota2[:, :, :].unsqueeze(1).broadcast_to([P, units, P, 2]),
                                       d.unsqueeze(2).broadcast_to([P, units, P, 2]), ALU.is_equal)

            with dve.Fori(0, EB // 64) as i:
                for j in range(8):
                    dve.wait_ge(hist_done, i * 8 + (j + 1))
                    one_hots(i * 32 + 4 * j, onehot[:, j % 2, :, :, :]).then_inc(hot_ready, 1)
            dve.wait_ge(hist_done, EB // 8 + 2)
            c.step(V.tensor_copy(hist_even[:, :], ps_cnt[0]))
            c.step(V.tensor_tensor(hist[:, :], hist_even[:, :], ps_cnt[1], ALU.add))
            c.step(V.tensor_tensor_scan(incl[:, :], ones_f[:, :], hist[:, :], 0.0, ALU.mult, ALU.add))
            V.tensor_copy(rowsum[:, :], incl[:, P - 1:P]).then_inc(off_ready, 1)
            dve.wait_ge(off_ready, 1)
            c.step(V.tensor_tensor(incl[:, :], incl[:, :], flat_id[:, :], ALU.add))
            dve.wait_ge(off_mm, 1)
            c.step(V.tensor_copy(rowoff[:, :], ps_tr[:, 0:1]))
            c.step(V.tensor_scalar(end[:, :], incl[:, :], rowoff[:, 0:1], None, ALU.add))
            c.step(V.tensor_tensor(off[:, :], end[:, :], hist[:, :], ALU.subtract))
            c.step(V.tensor_scalar(off1[:, :], off[:, :], 1.0, None, ALU.add))
            V.tensor_tensor(off2[:, :], off1[:, :], hist_even[:, :], ALU.add).then_inc(off_ready, 1)
            dve.wait_ge(off_mm, 2)
            c.mark(V.tensor_copy(offT[:, :], ps_tr[:, 128:256]))
            c.mark(V.memset(endT[:, NB:NB + 32], 0))
            c.mark(V.tensor_copy(endT[:, 0:NB], ps_tr[:, 256:384]))
            c.mark(V.memset(tabt[:, :, :], 1.0))
            c.step(V.memset(X[:, NB:NB + 2, :], 0.0))

            def mask_same(grp, s):
                dve.wait_ge(same_mm, grp + 1)
                V.tensor_tensor(same[:, s, :, :], ps_same[:, :, :],
                                before[:, :].unsqueeze(1).broadcast_to([P, GRP, P]), ALU.mult
                                ).then_inc(same_ready, 1)

            one_hots(0, hot_ring[:, 0, :, :, :]).then_inc(oh_ready, 1)
            one_hots(2, hot_ring[:, 1, :, :, :]).then_inc(oh_ready, 1)
            mask_same(0, 0)
            V.memset(slotf[:, :, :], 0.0).then_inc(slot_ready, 2)
            V.memset(picked[:, :, :], 0.0).then_inc(sidx_ready, 1)
            dve.wait_ge(emb_kept, NB)
            dve.wait_ge(consts, 11)
            a = Chain(dve, dve_att)

            def layer_norm_stats(chain, n):
                chain.mark(V.bn_stats(stats[:, n, 0, :], xcur[:, 0, :]))
                lone_wait(dve, chain.s, chain.mark(V.bn_stats(stats[:, n, 1, :], xcur[:, 1, :])))
                chain.mark(V.bn_aggr(mv[:, n, 0, :], stats[:, n, 0, :]))
                chain.step(V.bn_aggr(mv[:, n, 1, :], stats[:, n, 1, :]))
                V.tensor_scalar(vare[:, n, :], mv[:, n, :, 1], LN_EPS, None, ALU.add).then_inc(var_ready, 1)

            def layer_norm(i, n, to):
                dve.wait_ge(std_ready, i * 2 + (n + 1))
                a.step(V.reciprocal(rstd[:, n, :], std[:, n, :]))
                for t in range(2):
                    m = V.tensor_scalar(to[:, t, :], xcur[:, t, :], mv[:, n, t, 0:1], rstd[:, n, t:t + 1],
                                        ALU.subtract, ALU.mult)
                m.then_inc(norm_ready, 1)

            def attend(i, t):
                if t == 1:
                    layer_norm(i, 0, xn)
                if t == 18:
                    dve.wait_ge(value_mm, i + 1)
                    a.step(V.tensor_tensor(xcur[:, :, :], xcur[:, :, :],
                                           ps_tr[:, 0:2 * D].rearrange("p (t d) -> p t d", t=2), ALU.add))
                    layer_norm_stats(a, 1)
                    a.mark(V.tensor_copy(X[:, bass.ds(i * 2, 2), :], xcur[:, :, :]))
                if t == 22:
                    layer_norm(i, 1, xn2)
                if t == 29:
                    dve.wait_ge(gat_mm, i + 1)
                    dve.wait_ge(table_stored, i * 16 + 16)
                    hv = ps_tr[:, 256:256 + 2 * HE].rearrange("p (t f) -> p t f", t=2)
                    a.mark(V.tensor_copy(tabt[:, :, 0:SUM_W].rearrange("p t (h e) -> p t h e", h=HD)[:, :, :, 0:EX],
                                         hv.rearrange("p t (h e) -> p t h e", h=HD)))
                    for n in range(2):
                        a.mark(V.tensor_tensor(hatt[:, n, :, :], hv,
                                               att_s[:, n, :].unsqueeze(1).broadcast_to([P, 2, HE]), ALU.mult))
                    dve.wait_ge(dve_att, a.at + (a.base + a.n))
                    for n in range(2):
                        m = V.tensor_reduce(tabt[:, :, SUM_W + n * HD:SUM_W + (n + 1) * HD],
                                            hatt[:, n, :, :].rearrange("p t (h e) -> p t h e", h=HD),
                                            AX.X, ALU.add)
                    m.then_inc(table_ready, 1)
                if t == 30:
                    a.step(V.tensor_copy(xcur[:, :, :], X[:, bass.ds(i * 2 + 2, 2), :]))
                    layer_norm_stats(a, 0)

            c.step(V.tensor_copy(xcur[:, :, :], X[:, 0:2, :]))
            layer_norm_stats(c, 0)
            with dve.Fori(0, BATCHES) as i:
                a.turn(i, 16)
                for g in range(STEPS):
                    s = g % 2
                    grp = i * STEPS + g
                    dve.wait_ge(slot_ready, grp * GRP + 2)
                    one_hots(grp * 2 + 4, hot_ring[:, (g + 2) % 4, :, :, :]).then_inc(oh_ready, 1)
                    if g == 0:
                        dve.wait_ge(sidx_ready, i * 2 + 1)
                    for b in range(GRP):
                        if b == 3:
                            mask_same(grp + 1, 1 - s)
                        dve.wait_ge(slot_mm, grp * GRP + (b + 2))
                        n = GRP * g + b
                        V.tensor_tensor_reduce(out=picked[:, b, :], in0=ps_slot[:, b % 2, 0, :], in1=hot(g % 4, b, 1),
                                               scale=1.0, scalar=0.0, op0=ALU.mult, op1=ALU.add,
                                               accum_out=slotf[:, n // HALF, n % HALF:n % HALF + 1]
                                               ).then_inc(slot_ready, 1)
                        attend(i, n)
                    if g % 4 == 3:
                        h = g // 4
                        dve.wait_ge(scattered[h], i * (HALF * 16) + 16)
                        V.tensor_copy(spay[:, h, :], src[:, bass.ds(i * (2 * HALF) + h * HALF, HALF)])
                        dve.wait_ge(slot_ready, (grp + 1) * GRP + 2)
                        V.tensor_copy(sidx[:, h, :], slotf[:, h, :]).then_inc(sidx_ready, 1)
                a.end_turn(BATCHES)

            c2 = Chain(dve, prep2)
            dve.wait_ge(counted, EB + 2)
            for q in range(4):
                c2.step(V.tensor_tensor(cmp, offT[:, :].unsqueeze(1).broadcast_to([P, 32, P]),
                                        lane_start[:, 32 * q:32 * q + 32].unsqueeze(2).broadcast_to([P, 32, P]),
                                        ALU.is_lt))
                c2.step(V.tensor_reduce(cnt[:, 32 * q:32 * q + 32], cmp, AX.X, ALU.add))
            assert c2.n == PREP2
            dve.wait_ge(lane_mm, 1)
            c2.step(V.tensor_scalar(node[:, 1, CH:CH + 1], ps_tr[:, 0:1], -1.0, None, ALU.add))
            V.tensor_scalar(first_u[:, :], node[:, 1, CH:CH + 1], 0.0, None, ALU.max).then_inc(first_ready, 1)
            for s in range(2):
                c2.mark(V.memset(keep4[:, s, :, 0:1], 0.0))
                c2.mark(V.memset(neg4[:, s, :, 0:1], -BIG))
                c2.mark(V.memset(decay[:, s, :, 0:1], 0.0))
            c2.mark(V.memset(mx[:, 1, :, CH:CH + 1], -BIG))
            c2.mark(V.memset(run[:, 1, :, CH:CH + 1], 0.0))
            c2.step(V.memset(trow[:, 0, 0, 0:1], 0.0))
            dve.wait_ge(first_in, 16)
            c2.step(V.tensor_copy(ad[:, 1, :, CH], first_row[:, SUM_W + HD:SUM_W + 2 * HD]))

            def stream_index(chain, s, at):
                sv = srt_s[:, bass.ds(at, CH)]
                chain.mark(V.tensor_copy(start[:, s, 0:1], node[:, 1 - s, CH:CH + 1]))
                chain.step(V.tensor_scalar(start[:, s, 1:CH + 1], sv, FLAG, None, ALU.is_ge))
                chain.step(V.tensor_tensor_scan(node[:, s, :], ones_f[:, 0:CH + 1], start[:, s, :], 0.0,
                                                ALU.mult, ALU.add))
                chain.step(V.scalar_tensor_tensor(self_id[:, s, :], node[:, s, 1:CH + 1], -float(FLAG),
                                                  start[:, s, 1:CH + 1], ALU.add, ALU.mult))
                V.tensor_tensor(gidx[:, s, :], self_id[:, s, :], sv, ALU.add).then_inc(gidx_ready, 1)

            dve.wait_ge(sorted_in, 16)
            stream_index(c2, 0, 0)
            stream_index(c2, 1, CH)
            st = Chain(dve, dve_str)
            with dve.Fori(0, BATCHES) as i:
                st.turn(i, 36)
                for s in range(2):
                    r = 1 - s
                    at = i * (2 * CH) + s * CH
                    sv = srt_s[:, bass.ds(at, CH)].unsqueeze(1).broadcast_to([P, HD, CH])
                    dve.wait_ge(orow_ready, i * 2 + (s + 1))
                    st.mark(V.tensor_scalar(keep4[:, s, :, 1:CH + 1], sv, FLAG, None, ALU.is_lt))
                    st.mark(V.tensor_scalar(neg4[:, s, :, 1:CH + 1], sv, FLAG, -BIG, ALU.is_ge, ALU.mult))
                    st.mark(V.tensor_copy(ad_in[:, s, :, 0], ad[:, r, :, CH]))
                    st.mark(V.tensor_copy(e_in[:, s, :, 0], mx[:, r, :, CH]))
                    st.mark(V.tensor_copy(add[:, s, :, 0], run[:, r, :, CH]))
                    dve.wait_ge(gathered[s], i * (CH * 16) + CH * 16)
                    g_t = grow[:, s, :, :].rearrange("p t f -> p f t")
                    st.step(V.scalar_tensor_tensor(ad_in[:, s, :, 1:CH + 1], sv, FLAG,
                                                   g_t[:, SUM_W + HD:SUM_W + 2 * HD, :], ALU.is_ge, ALU.mult))
                    flat = lambda t: t[:, s, :, :].rearrange("p f t -> p (f t)")
                    st.step(V.tensor_tensor_scan(flat(ad), flat(keep4), flat(ad_in), 0.0, ALU.mult, ALU.add))
                    st.step(V.tensor_tensor(e_raw[:, s, :, :], g_t[:, SUM_W:SUM_W + HD, :], ad[:, s, :, 1:CH + 1],
                                            ALU.add))
                    st.step(V.scalar_tensor_tensor(e_in[:, s, :, 1:CH + 1], e_raw[:, s, :, :], SLOPE,
                                                   e_raw[:, s, :, :], ALU.mult, ALU.max))
                    st.step(V.tensor_tensor_scan(flat(mx), flat(neg4), flat(e_in), 0.0, ALU.add, ALU.max))
                    st.mark(V.tensor_tensor(expo[:, s, HD:2 * HD, :], e_in[:, s, :, 1:CH + 1],
                                            mx[:, s, :, 1:CH + 1], ALU.subtract))
                    st.step(V.tensor_tensor(expo[:, s, 0:HD, :], mx[:, s, :, 0:CH], mx[:, s, :, 1:CH + 1],
                                            ALU.subtract))
                    V.tensor_scalar(expo[:, s, 0:HD, :], expo[:, s, 0:HD, :], 0.0, None, ALU.min
                                    ).then_inc(expo_ready, 1)
                    dve.wait_ge(exp_ready, i * 2 + (s + 1))
                    fan = [P, HD, EX + 1, CH]
                    st.mark(V.tensor_tensor(decay[:, s, :, 1:CH + 1].rearrange("p (h e) t -> p h e t", h=HD),
                                            ex[:, s, 0:HD, :].unsqueeze(2).broadcast_to(fan),
                                            keep4[:, s, :, 1:CH + 1].unsqueeze(2).broadcast_to(fan), ALU.mult))
                    st.step(V.tensor_tensor(add[:, s, :, 1:CH + 1].rearrange("p (h e) t -> p h e t", h=HD),
                                            g_t[:, 0:SUM_W, :].rearrange("p (h e) t -> p h e t", h=HD),
                                            ex[:, s, HD:2 * HD, :].unsqueeze(2).broadcast_to(fan), ALU.mult))
                    stream_index(st, s, at + 2 * CH)
                    V.tensor_tensor_scan(flat(run), flat(decay), flat(add), 0.0, ALU.mult, ALU.add
                                         ).then_inc(run_ready, 1)
                    dve.wait_ge(run_ready, i * 2 + (s + 1))
                st.end_turn(BATCHES)

            m_ = Chain(dve, dve_mend)
            m_.step(V.tensor_scalar(key, srt_s[:, 0:LANE], float(FLAG), float(LANE), ALU.is_lt, ALU.mult))
            m_.step(V.tensor_tensor(key, key, col_no[:, :], ALU.add))
            m_.step(V.tensor_reduce(fstart[:, :], key, AX.X, ALU.min))
            V.tensor_scalar(lane_sum[:, 2, :], fstart[:, 0:1].broadcast_to([P, SUM_W]), float(LANE), None, ALU.is_lt)
            V.tensor_copy(lane_sum[:, 1, :].rearrange("p (h e) -> p h e", h=HD),
                          mx[:, 1, :, CH:CH + 1].broadcast_to([P, HD, EX + 1]))
            V.tensor_copy(lane_sum[:, 0, :], run[:, 1, :, CH]).then_inc(lane_ends, 1)
            m_.step(V.tensor_tensor(mendq[:, 0:1], slot_base[:, :], fstart[:, :], ALU.add))
            m_.mark(V.tensor_tensor(mendq[:, 1:2], trash[:, :], mendq[:, 0:1], ALU.subtract))
            m_.step(V.tensor_scalar(mendq[:, 2:3], fstart[:, :], 0.0, None, ALU.is_equal))
            m_.mark(V.scalar_tensor_tensor(mendq[:, 3:4], mendq[:, 1:2], mendq[:, 2:3], mendq[:, 0:1],
                                           ALU.mult, ALU.add))
            m_.mark(V.tensor_scalar(mendu[:, 0:1], mendq[:, 0:1], 0.0, None, ALU.max))
            dve.wait_ge(dve_mend, m_.n)
            V.tensor_copy(mendu[:, 1:2], mendq[:, 3:4]).then_inc(mend_idx, 1)
            m_.mark(V.memset(lmax[:, 0:1], -BIG))
            m_.mark(V.memset(lsum[:, 0:1], 0.0))
            dve.wait_ge(lane_endsT, 1)
            m_.step(V.tensor_copy(laneT[:, :, :], ps_tr[0:SUM_W, 0:3 * P].rearrange("p (n l) -> p n l", n=3)))
            m_.step(V.tensor_scalar(lneg[:, :], laneT[:, 2, :], -BIG, None, ALU.mult))
            m_.step(V.tensor_tensor_scan(lmax[:, 1:P + 1], lneg[:, :], laneT[:, 1, :], -BIG, ALU.add, ALU.max))
            m_.mark(V.tensor_tensor(lexp[:, 1, :], laneT[:, 1, :], lmax[:, 1:P + 1], ALU.subtract))
            m_.step(V.tensor_tensor(lexp[:, 0, :], lmax[:, 0:P], lmax[:, 1:P + 1], ALU.subtract))
            V.tensor_scalar(lexp[:, 0, :], lexp[:, 0, :], 0.0, None, ALU.min).then_inc(lane_expo, 1)
            m_.step(V.tensor_scalar(lneg[:, :], laneT[:, 2, :], -1.0, 1.0, ALU.mult, ALU.add))
            dve.wait_ge(lane_exp, 1)
            m_.mark(V.tensor_tensor(lexp[:, 0, :], lexp[:, 0, :], lneg[:, :], ALU.mult))
            m_.step(V.tensor_tensor(lexp[:, 1, :], lexp[:, 1, :], laneT[:, 0, :], ALU.mult))
            V.tensor_tensor_scan(lsum[:, 1:P + 1], lexp[:, 0, :], lexp[:, 1, :], 0.0, ALU.mult, ALU.add
                                 ).then_inc(lane_carry, 1)
            dve.wait_ge(lane_carryT, 1)
            m_.step(V.tensor_copy(carry[:, :, :],
                                  ps_sc[:, 0, 0:64].rearrange("p (n f) -> p n f", n=2)[:, :, 0:SUM_W]))
            dve.wait_ge(mend_in, 16)
            cmax = carry[:, 1, :].rearrange("p (h e) -> p h e", h=HD)[:, :, 0]
            m_.step(V.tensor_tensor(mmax[:, :], cmax, mrow[:, SUM_W:ROW_W], ALU.max))
            V.tensor_copy(mout[:, SUM_W:ROW_W], mmax[:, :])
            V.tensor_tensor(mexp[:, 0, :], cmax, mmax[:, :], ALU.subtract)
            V.tensor_tensor(mexp[:, 1, :], mrow[:, SUM_W:ROW_W], mmax[:, :], ALU.subtract).then_inc(mend_expo, 1)
            dve.wait_ge(mend_exp, 1)
            for n, part in ((0, carry[:, 0, :]), (1, mrow[:, 0:SUM_W])):
                m_.mark(V.tensor_tensor(mtmp[:, n, :].rearrange("p (h e) -> p h e", h=HD),
                                        part.rearrange("p (h e) -> p h e", h=HD),
                                        mexp[:, n, :].unsqueeze(2).broadcast_to([P, HD, EX + 1]), ALU.mult))
            dve.wait_ge(dve_mend, m_.n)
            V.tensor_tensor(mout[:, 0:SUM_W], mtmp[:, 0, :], mtmp[:, 1, :], ALU.add).then_inc(mend_ready, 1)

            for s in range(2):
                V.tensor_copy(tidx[:, s, :], endT[:, s * TB:(s + 1) * TB]).then_inc(tidx_ready, 1)
            t_ = Chain(dve, dve_tail)
            hs = lambda t: t.rearrange("p k (h e) -> p k h e", h=HD)
            with dve.Fori(0, NB // TB // 2) as i:
                t_.turn(i, 2 * TAIL)
                for s in range(2):
                    n0 = t_.n
                    dve.wait_ge(tail_rows[s], i * (TB * 16) + TB * 16)
                    sums = hs(trow[:, s, :, 0:SUM_W])
                    t_.step(V.tensor_scalar(den[:, :, :], sums[:, :, :, EX], DEN_EPS, None, ALU.add))
                    t_.step(V.reciprocal(den[:, :, :], den[:, :, :]))
                    t_.step(V.tensor_tensor(agg[:, :, :, :], sums[:, :, :, 0:EX],
                                            den[:, :, :].unsqueeze(3).broadcast_to([P, TB, HD, EX]), ALU.mult))
                    ag = agg[:, :, :, :].rearrange("p k h e -> p k (h e)")
                    over_k = lambda v: v.unsqueeze(1).broadcast_to([P, TB, HE])
                    over_f = lambda v: v.unsqueeze(2).broadcast_to([P, TB, HE])
                    t_.step(V.tensor_tensor(ag, ag, over_k(gate_p[:, 0, :]), ALU.add))
                    t_.step(V.tensor_reduce(red[:, 0, :], ag, AX.X, ALU.add))
                    t_.step(V.tensor_scalar(red[:, 1, :], red[:, 0, :], 1.0 / HE, None, ALU.mult))
                    t_.step(V.tensor_tensor(ag, ag, over_f(red[:, 1, :]), ALU.subtract))
                    t_.step(V.tensor_tensor(sq[:, :, :], ag, ag, ALU.mult))
                    t_.step(V.tensor_reduce(red[:, 0, :], sq[:, :, :], AX.X, ALU.add))
                    V.tensor_scalar(red[:, 2, :], red[:, 0, :], 1.0 / HE, LN_EPS, ALU.mult, ALU.add
                                    ).then_inc(tail_var, 1)
                    dve.wait_ge(tail_std, i * 2 + (s + 1))
                    t_.step(V.reciprocal(red[:, 4, :], red[:, 3, :]))
                    t_.step(V.tensor_tensor(ag, ag, over_f(red[:, 4, :]), ALU.mult))
                    t_.step(V.tensor_tensor(ag, ag, over_k(gate_p[:, 1, :]), ALU.mult))
                    t_.step(V.tensor_tensor(ag, ag, over_k(gate_p[:, 2, :]), ALU.add))
                    t_.step(V.tensor_reduce(sc4[:, :, :], agg[:, :, :, :].rearrange("p k h e -> p k e h"), AX.X, ALU.add))
                    t_.step(V.tensor_scalar(sc4[:, :, :], sc4[:, :, :], 1.0 / HD, None, ALU.mult))
                    pair = [P, TB, EX, EX]
                    other = sc4[:, :, :].unsqueeze(2).broadcast_to(pair)
                    own = sc4[:, :, :].unsqueeze(3).broadcast_to(pair)
                    t_.mark(V.tensor_tensor(dif[:, :, :, :], other, own, ALU.is_equal))
                    t_.step(V.tensor_reduce(red[:, 5, :], sc4[:, :, :], AX.X, ALU.max))
                    dif_f = dif[:, :, :, :].rearrange("p k e o -> p k (e o)")
                    t_.mark(V.tensor_tensor(dif_f, dif_f, over_k(tie[:, :, :].rearrange("p e o -> p (e o)")), ALU.mult))
                    t_.step(V.tensor_tensor(agg[:, :, :, :], other, own, ALU.is_gt))
                    V.tensor_tensor(sc4[:, :, :], sc4[:, :, :], red[:, 5, :].unsqueeze(2).broadcast_to([P, TB, EX]),
                                    ALU.subtract).then_inc(tail_sub, 1)
                    t_.step(V.tensor_tensor(dif_f, dif_f, ag, ALU.add))
                    t_.step(V.tensor_reduce(rank[:, :, :], dif[:, :, :, :], AX.X, ALU.add))
                    dve.wait_ge(tail_exp, i * 2 + (s + 1))
                    t_.step(V.scalar_tensor_tensor(gate[:, :, :], rank[:, :, :], 1.5, gate[:, :, :], ALU.is_lt, ALU.mult))
                    t_.step(V.tensor_reduce(red[:, 0, :], gate[:, :, :], AX.X, ALU.add))
                    t_.step(V.reciprocal(red[:, 1, :], red[:, 0, :]))
                    t_.step(V.tensor_tensor(gate[:, :, :], gate[:, :, :],
                                            red[:, 1, :].unsqueeze(2).broadcast_to([P, TB, EX]), ALU.mult))
                    dve.wait_ge(y_loaded[s], i * 16 + 16)
                    t_.step(V.tensor_tensor(gated.rearrange("p k e d -> p (k e) d"),
                                            y_ring[:, s, :, :].rearrange("p k (e d) -> p (k e) d", e=EX),
                                            gate[:, :, :].rearrange("p k e -> p (k e)").unsqueeze(2
                                            ).broadcast_to([P, TB * EX, D]), ALU.mult))
                    V.tensor_copy(tidx[:, s, :], endT[:, bass.ds(i * (2 * TB) + (2 + s) * TB, TB)]).then_inc(tidx_ready, 1)
                    dve.wait_ge(out_stored[s], i * 16 + 16)
                    t_.mark(V.tensor_tensor(o_half[:, 0, :, :], gated[:, :, 0, :], gated[:, :, 1, :], ALU.add))
                    t_.step(V.tensor_tensor(o_half[:, 1, :, :], gated[:, :, 2, :], gated[:, :, 3, :], ALU.add))
                    t_.step(V.tensor_tensor(o_half[:, 0, :, :], o_half[:, 0, :, :], o_half[:, 1, :, :], ALU.add))
                    V.tensor_tensor(o_ring[:, s, :, :], o_half[:, 0, :, :],
                                    X[:, bass.ds(i * (2 * TB) + s * TB, TB), :], ALU.add).then_inc(out_ready, 1)
                    assert t_.n - n0 == TAIL, t_.n - n0
                t_.end_turn(NB // TB // 2)


NAMES = ["x", "L0_tok_W", "L0_attn_q_weight", "L0_ffn_W_gat", "L0_ffn_att_src", "L0_ffn_att_dst", "L0_ffn_b_gat",
         "L0_ffn_ln_gamma", "L0_ffn_ln_beta", "L0_ffn_W1", "L0_ffn_b1", "L0_ffn_W2", "L0_ffn_b2"]


def kernel(**inputs):
    import concourse.bacc as bacc
    from concourse.bass_utils import run_bass_kernel_spmd

    x, emb, qw, wgat, asrc, adst, bgat, gamma, beta, w1, b1, w2, b2 = (np.asarray(inputs[n]) for n in NAMES)
    edges = np.asarray(inputs["L0_ffn_edge_index"])
    he = wgat.shape[1]
    arrays = {
        "tok": x.reshape(-1, P).T,
        "emb": emb.T,
        "qw": qw,
        "wgat": wgat,
        "att_src": asrc.reshape(1, he),
        "att_dst": adst.reshape(1, he),
        "b_gat": bgat.reshape(1, he),
        "gamma": gamma.reshape(1, he),
        "beta": beta.reshape(1, he),
        "w1": w1.transpose(1, 0, 2),
        "b1": b1.T,
        "w2": w2.transpose(1, 0, 2),
        "b2": b2.reshape(1, -1),
        "esrc": edges[0].reshape(P, -1),
        "edst": edges[1].reshape(P, -1),
    }
    arrays = {k: np.ascontiguousarray(v) for k, v in arrays.items()}
    nc = bacc.Bacc("TRN2", target_bir_lowering=False, num_devices=1)
    args = [nc.dram_tensor("in_" + k, v.shape, mybir.dt.from_np(v.dtype), kind="ExternalInput").ap()
            for k, v in arrays.items()]
    shape = (x.size, emb.shape[0])
    args.append(nc.dram_tensor("result", shape, F32, kind="ExternalOutput").ap())
    build(nc, *args)
    r = run_bass_kernel_spmd(nc, [{"in_" + k: v for k, v in arrays.items()}], core_ids=[0])
    return r.results[0]["result"].reshape(*x.shape, emb.shape[0])
```

```python
from contextlib import ExitStack

import concourse.bass as bass
from concourse import mybir
import numpy as np

ALU = mybir.AluOpType
ACT = mybir.ActivationFunctionType
AX = mybir.AxisListType
F32 = mybir.dt.float32
BF16 = mybir.dt.bfloat16
I32 = mybir.dt.int32
U32 = mybir.dt.uint32

P = 128
BIG = 1.0e38
LN_EPS = 1e-5
DEN_EPS = 1e-16
SLOPE = 0.2

TAB_W = 32
SUM_W = 20
ROW_W = 24


def build(nc, tok, emb, qw, wgat, att_src, att_dst, b_gat, gamma, beta, w1, b1, w2, b2, esrc, edst, out):
    NB = tok.shape[1]
    NTOK = P * NB
    D = emb.shape[1]
    HE = wgat.shape[1]
    EX, HID = w1.shape[1], w1.shape[2]
    HD = HE // EX
    EB = esrc.shape[1]
    NSLOT = P * (EB + NB)
    LANE = NSLOT // P
    FLAG = NTOK
    BATCHES = NB // 2
    GRP = 4
    STEPS = EB // BATCHES // GRP
    HALF = STEPS // 2 * GRP
    HPAIR, CODED = 8, 3
    CH = LANE // P
    assert (D, HE, EX, HID) == (64, 16, 4, 128) and NB == P and STEPS == 8
    assert CH == HALF + 1 and CH * P == LANE and HD * (EX + 1) == SUM_W

    srt = nc.dram_tensor("sorted_sources", [NSLOT, 1], I32, kind="Internal").ap()
    table = nc.dram_tensor("node_table", [NTOK, TAB_W], F32, kind="Internal").ap()
    rows = nc.dram_tensor("slot_rows", [NSLOT + P, ROW_W], F32, kind="Internal").ap()
    yexp = nc.dram_tensor("expert_rows", [P, NB, EX * D], F32, kind="Internal").ap()

    with ExitStack() as ctx:
        def sb(name, shape, dt=F32):
            return ctx.enter_context(nc.sbuf_tensor(name, shape, dt))

        def ps(name, shape, dt=F32):
            return ctx.enter_context(nc.psum_tensor(name, shape, dt))

        def sem(name):
            return ctx.enter_context(nc.semaphore(name))

        iota2 = sb("iota2", [P, P, 2], BF16)
        ident_b = sb("ident_b", [P, P], BF16)
        ident_f = sb("ident_f", [P, P])
        before = sb("before", [P, P])
        zero_b = sb("zero_b", [P, P], BF16)
        ones_f = sb("ones_f", [P, P])
        lane_start = sb("lane_start", [P, P])
        slot_base = sb("slot_base", [P, 1])
        trash = sb("trash", [P, 1])
        flat_id = sb("flat_id", [P, P])
        col_no = sb("col_no", [P, LANE], mybir.dt.int16)

        qw_s = sb("qw_s", [D, D])
        wg_s = sb("wg_s", [D, HE])
        w1_s = sb("w1_s", [D, EX, HID])
        w2_s = sb("w2_s", [HID, EX, D])
        b1_s = sb("b1_s", [HID, EX])
        b2_s = sb("b2_s", [1, EX * D])
        att_s = sb("att_s", [P, 2, HE])
        gate_p = sb("gate_p", [P, 3, HE])

        ids = sb("ids", [P, NB + 4], I32)
        keep = sb("keep", [P, NB + 4])
        eidx = sb("eidx", [P, 2, 2], U32)
        erow = sb("erow", [P, 2, 2, D])
        X = sb("X", [P, NB + 2, D])
        big = sb("big", [P, NTOK])
        xn2T = big[0:D, :]
        y_ring = big[:, 0:2 * 16 * EX * D].rearrange("p (s k f) -> p s k f", s=2, k=16)
        gated = big[:, 8192:8192 + 16 * EX * D].rearrange("p (k e d) -> p k e d", k=16, e=EX)
        o_ring = big[:, 12288:12288 + 2 * 16 * D].rearrange("p (s k d) -> p s k d", s=2, k=16)
        o_half = big[:, 14336:14336 + 2 * 16 * D].rearrange("p (s k d) -> p s k d", s=2, k=16)

        src = sb("src", [P, LANE], I32)
        key = src[:, :].bitcast(F32)
        dst = big[:, 0:EB].bitcast(I32)
        digit_i = big[:, EB:2 * EB].bitcast(I32)
        low_i = dst
        minus_hi = big[:, 2 * EB:3 * EB]
        hot16 = big[:, 3 * EB:3 * EB + 2 * HPAIR * 2 * P].bitcast(BF16).rearrange(
            "p (s a h n b) -> p s a h n b", s=2, a=HPAIR, h=2, b=2)
        digit = sb("digit", [P, EB // 2 + 4, 2, 2], BF16)
        onehot = sb("onehot", [P, 2, 8, P, 2], BF16)
        hot_ring = onehot[:, :, :, :, :].rearrange("p s (q u) n b -> p (s q) u n b", q=2)
        hist = sb("hist", [P, P])
        incl = sb("incl", [P, P])
        rowsum = sb("rowsum", [P, 1])
        rowoff = sb("rowoff", [P, 1])
        off = sb("off", [P, P])
        off1 = sb("off1", [P, P])
        off2 = sb("off2", [P, P])
        hist_even = sb("hist_even", [P, P])
        end = sb("end", [P, P])
        offT = sb("offT", [P, P])
        endT = sb("endT", [P, NB + 32], U32)
        hiT = sb("hiT", [P, 2, GRP, P])
        hiT_b = sb("hiT_b", [P, GRP, P], BF16)
        same = sb("same", [P, 2, GRP, P], BF16)
        count = sb("count", [P, GRP, P])
        picked = sb("picked", [P, GRP, P])
        diff = picked[:, 0, :]
        code_sum = picked[:, 1:3, :]
        slotf = sb("slotf", [P, 2, HALF])
        sidx = sb("sidx", [P, 2, HALF], U32)
        spay = sb("spay", [P, 2, HALF], I32)

        stats = sb("stats", [P, 2, 2, 6])
        mv = sb("mv", [P, 2, 2, 2])
        vare = sb("vare", [P, 2, 2])
        std = sb("std", [P, 2, 2])
        rstd = sb("rstd", [P, 2, 2])
        xcur = sb("xcur", [P, 2, D])
        xn = sb("xn", [P, 2, D])
        xn2 = sb("xn2", [P, 2, D])
        xnT = sb("xnT", [D, 2 * P])
        xnT2 = sb("xnT2", [D, 2 * P])
        qT = sb("qT", [D, 2 * P])
        att = sb("att", [P, 2, 2 * P])
        tabt = sb("tabt", [P, 2, TAB_W])
        hatt = sb("hatt", [P, 2, 2, HE])

        srt_s = sb("srt_s", [P, LANE + 2 * CH], I32)
        cmp = onehot[:, :, :, :, :].rearrange("p s u n b -> p (s u n b)").rearrange("p (j n) -> p j n", n=P)
        cnt = sb("cnt", [P, P])
        start = sb("start", [P, 2, CH + 1])
        node = sb("node", [P, 2, CH + 1])
        self_id = sb("self_id", [P, 2, CH])
        first_u = sb("first_u", [P, 1], U32)
        first_row = sb("first_row", [P, TAB_W])
        gidx = sb("gidx", [P, 2, CH], U32)
        grow = sb("grow", [P, 2, CH, TAB_W])
        keep4 = sb("keep4", [P, 2, HD, CH + 1])
        neg4 = sb("neg4", [P, 2, HD, CH + 1])
        ad_in = sb("ad_in", [P, 2, HD, CH + 1])
        ad = sb("ad", [P, 2, HD, CH + 1])
        e_raw = sb("e_raw", [P, 2, HD, CH])
        e_in = sb("e_in", [P, 2, HD, CH + 1])
        mx = sb("mx", [P, 2, HD, CH + 1])
        expo = sb("expo", [P, 2, 2 * HD, CH])
        ex = sb("ex", [P, 2, 2 * HD, CH])
        decay = sb("decay", [P, 2, SUM_W, CH + 1])
        add = sb("add", [P, 2, SUM_W, CH + 1])
        run = sb("run", [P, 2, SUM_W, CH + 1])
        orow = sb("orow", [P, 2, CH, ROW_W])
        hid = hiT[:, :, :, :].rearrange("p s b n -> p (s b n)").rearrange("p (e n) -> p e n", e=EX)
        y_out = sb("y_out", [P, 2, EX * D])

        lane_sum = sb("lane_sum", [P, 3, SUM_W])
        laneT = sb("laneT", [SUM_W, 3, P])
        lneg = sb("lneg", [SUM_W, P])
        lmax = sb("lmax", [SUM_W, P + 1])
        lexp = sb("lexp", [SUM_W, 2, P])
        lsum = sb("lsum", [SUM_W, P + 1])
        carry = sb("carry", [P, 2, SUM_W])
        fstart = sb("fstart", [P, 1])
        mendq = sb("mendq", [P, 4])
        mendu = sb("mendu", [P, 2], U32)
        mrow = sb("mrow", [P, ROW_W])
        mmax = sb("mmax", [P, HD])
        mexp = sb("mexp", [P, 2, HD])
        mtmp = sb("mtmp", [P, 2, SUM_W])
        mout = sb("mout", [P, ROW_W])

        TB = 16
        tidx = sb("tidx", [P, 2, TB], U32)
        trow = sb("trow", [P, 2, TB, ROW_W])
        den = sb("den", [P, TB, HD])
        agg = sb("agg", [P, TB, HD, EX])
        sq = sb("sq", [P, TB, HE])
        red = sb("red", [P, 6, TB])
        sc4 = sb("sc4", [P, TB, EX])
        dif = sb("dif", [P, TB, EX, EX])
        tie = sb("tie", [P, EX, EX])
        rank = sb("rank", [P, TB, EX])
        gate = sb("gate", [P, TB, EX])

        cnt_bank = [ps(f"ps_cnt{h}", [P, 512]) for h in range(2)]
        ps_cnt = [t[:, 0:P] for t in cnt_bank]
        ps_hiT = ps("ps_hiT", [P, 2, GRP, P], BF16)
        ps_same = ps("ps_same", [P, GRP, P])
        ps_slot = ps("ps_slot", [P, 2, GRP, P])
        ps_tr = ps("ps_tr", [P, 512])
        ps_sc = ps("ps_sc", [P, 2, 2 * P])
        ps_code = [ps_same[:, 0, :], ps_slot[:, 0, 0, :]]
        ps_iota = ps_sc[:, 0, 0:P]
        ps_hid = [ps_slot[:, 0, 0:2, :].rearrange("p a b -> p (a b)"), ps_slot[:, 1, 0:2, :].rearrange("p a b -> p (a b)"),
                  ps_sc[:, 0, :], cnt_bank[0][:, 0:2 * P]]
        ps_y = ps_same[:, :, :].rearrange("p g n -> p (g n)").rearrange("p (a f) -> p a f", a=2)

        loaded = sem("loaded")
        waits_passed = sem("waits_passed")
        spare_rows = sem("spare_rows")
        blank_ready = sem("blank_ready")
        list_blank = sem("list_blank")
        edges_in = sem("edges_in")
        consts = sem("consts")
        consts2 = sem("consts2")
        prep = sem("prep")
        prep2 = sem("prep2")
        eidx_ready = sem("eidx_ready")
        emb_rows = [sem(f"emb_rows{s}") for s in range(2)]
        emb_kept = sem("emb_kept")
        hot_ready = sem("hot_ready")
        code_steps = sem("code_steps")
        code_ready = sem("code_ready")
        iota_ready = sem("iota_ready")
        diff_made = sem("diff_made")
        hist_done = sem("hist_done")
        off_mm = sem("off_mm")
        off_ready = sem("off_ready")
        oh_ready = sem("oh_ready")
        hiT_mm = sem("hiT_mm")
        hiT_ready = sem("hiT_ready")
        same_mm = sem("same_mm")
        same_ready = sem("same_ready")
        count_ready = sem("count_ready")
        counted = sem("counted")
        slot_mm = sem("slot_mm")
        slot_ready = sem("slot_ready")
        sidx_ready = sem("sidx_ready")
        scattered = [sem(f"scattered{s}") for s in range(2)]
        var_ready = sem("var_ready")
        std_ready = sem("std_ready")
        norm_ready = sem("norm_ready")
        normT_mm = sem("normT_mm")
        normT_ready = sem("normT_ready")
        normT_kept = sem("normT_kept")
        q_mm = sem("q_mm")
        q_ready = sem("q_ready")
        score_mm = sem("score_mm")
        att_ready = sem("att_ready")
        value_mm = sem("value_mm")
        gat_mm = sem("gat_mm")
        table_ready = sem("table_ready")
        table_stored = sem("table_stored")
        dve_att = sem("dve_att")
        sorted_in = sem("sorted_in")
        lane_mm = sem("lane_mm")
        first_ready = sem("first_ready")
        first_in = sem("first_in")
        gidx_ready = sem("gidx_ready")
        gathered = [sem(f"gathered{s}") for s in range(2)]
        dve_str = sem("dve_str")
        expo_ready = sem("expo_ready")
        exp_ready = sem("exp_ready")
        run_ready = sem("run_ready")
        orow_ready = sem("orow_ready")
        orow_stored = [sem(f"orow_stored{s}") for s in range(2)]
        hid_mm = sem("hid_mm")
        hid_ready = sem("hid_ready")
        y_mm = sem("y_mm")
        y_ready = sem("y_ready")
        y_stored = sem("y_stored")
        dve_mend = sem("dve_mend")
        lane_ends = sem("lane_ends")
        lane_endsT = sem("lane_endsT")
        lane_expo = sem("lane_expo")
        lane_exp = sem("lane_exp")
        lane_carry = sem("lane_carry")
        lane_carryT = sem("lane_carryT")
        mend_idx = sem("mend_idx")
        mend_expo = sem("mend_expo")
        mend_exp = sem("mend_exp")
        mend_ready = sem("mend_ready")
        mend_in = sem("mend_in")
        mend_out = sem("mend_out")
        tidx_ready = sem("tidx_ready")
        tail_rows = [sem(f"tail_rows{s}") for s in range(2)]
        dve_tail = sem("dve_tail")
        y_loaded = [sem(f"y_loaded{s}") for s in range(2)]
        tail_var = sem("tail_var")
        tail_std = sem("tail_std")
        tail_sub = sem("tail_sub")
        tail_exp = sem("tail_exp")
        gate_ready = sem("gate_ready")
        last_gated = sem("last_gated")
        out_ready = sem("out_ready")
        out_stored = [sem(f"out_stored{s}") for s in range(2)]

        block = ctx.enter_context(nc.Block())

        TAIL = 28
        PREP2 = 8

        class Chain:

            def __init__(self, eng, s, base=0):
                self.eng, self.s, self.base, self.n, self.at = eng, s, base, 0, 0

            def turn(self, i, per_turn):
                self.at, self.per, self.n = i * per_turn, per_turn, 0

            def mark(self, ins):
                ins.then_inc(self.s, 1)
                self.n += 1
                return self.at + (self.base + self.n)

            def step(self, ins):
                self.eng.wait_ge(self.s, self.mark(ins))

            def end_turn(self, turns):
                assert self.n == self.per, (self.n, self.per)
                self.at, self.base, self.n = 0, self.base + turns * self.per, 0

        def lone_wait(eng, s, value):
            eng.wait_ge(s, value)
            eng.sem_inc(waits_passed, 1)

        def hot(s, b, d):
            return hot_ring[:, s, b // 2 * 2 + d, :, b % 2]

        @block.sync
        def _(sp):
            sp.dma_start(dst, edst).then_inc(edges_in, 16)
            sp.dma_start(ids[:, 0:NB], tok).then_inc(loaded, 16)
            sp.dma_start(w1_s[:, :, :], w1).then_inc(table_stored, 16)
            sp.dma_start(w2_s[:, :, :], w2).then_inc(orow_stored[0], 16)
            sp.dma_start(b1_s[:, :], b1).then_inc(orow_stored[1], 16)
            sp.dma_start(b2_s[:, :], b2).then_inc(y_stored, 16)
            for t, a in ((att_s[:, 0, :], att_src), (att_s[:, 1, :], att_dst), (gate_p[:, 0, :], b_gat),
                         (gate_p[:, 1, :], gamma), (gate_p[:, 2, :], beta)):
                sp.dma_start(t, a.broadcast_to([P, HE])).then_inc(loaded, 16)

            sp.wait_ge(consts2, 3)
            sp.dma_start(rows[NSLOT:NSLOT + P, :], ones_f[:, 0:ROW_W]).then_inc(spare_rows, 16)
            sp.wait_ge(blank_ready, 1)
            sp.dma_start(srt[:, :].rearrange("(p t) o -> p (t o)", p=P), srt_s[:, 0:LANE]).then_inc(list_blank, 16)
            tab_v = table.rearrange("(k p) f -> p k f", p=P)
            with sp.Fori(0, BATCHES) as i:
                sp.wait_ge(table_ready, i + 1)
                sp.dma_start(tab_v[:, bass.ds(i * 2, 2), :], tabt[:, :, :]).then_inc(table_stored, 16)

            for s in range(2):
                sp.wait_ge(scattered[s], 16 + BATCHES * HALF * 16)
            sp.dma_start(srt_s[:, 0:LANE], srt[:, :].rearrange("(p t) o -> p (t o)", p=P)).then_inc(sorted_in, 16)

            rows_v = rows[0:NSLOT, :].rearrange("(p t) f -> p t f", p=P)
            with sp.Fori(0, BATCHES) as i:
                for s in range(2):
                    sp.wait_ge(orow_ready, i * 2 + (s + 2))
                    sp.dma_start(rows_v[:, bass.ds(i * (2 * CH) + s * CH, CH), :],
                                 orow[:, s, :, :]).then_inc(orow_stored[s], 16)
                    if s == 0:
                        sp.wait_ge(y_ready, i + 2)
                        sp.dma_start(yexp[:, bass.ds(i * 2, 2), :], y_out[:, :, :]).then_inc(y_stored, 16)

            sp.wait_ge(y_stored, 16 + BATCHES * 16)
            sp.wait_ge(mend_out, 16)
            with sp.Fori(0, NB // TB // 2) as i:
                for s in range(2):
                    sp.wait_ge(tidx_ready, i * 2 + (s + 1))
                    sp.dma_start(y_ring[:, s, :, :],
                                 yexp[:, bass.ds(i * (2 * TB) + s * TB, TB), :]).then_inc(y_loaded[s], 16)

        @block.gpsimd
        def _(pool):
            pool.iota(iota2[:, :, :], [[1, P], [0, 2]], base=0, channel_multiplier=0,
                      allow_small_or_imprecise_dtypes=True).then_inc(consts, 1)
            for s in range(2):
                pool.dma_start(src[:, s * (EB // 2):(s + 1) * (EB // 2)], esrc[:, s * (EB // 2):(s + 1) * (EB // 2)]
                               ).then_inc(scattered[s], 16)
            pool.memset(ident_b[:, :], 0.0).then_inc(consts2, 1)
            pool.memset(ident_f[:, :], 0.0).then_inc(consts2, 1)
            pool.memset(ones_f[:, :], 1.0).then_inc(consts2, 1)
            pool.memset(zero_b[:, :], 0.0).then_inc(consts, 1)
            pool.wait_ge(consts2, 3)
            pool.affine_select(out=ident_b[:, :], in_=ident_b[:, :], compare_op=ALU.not_equal, fill=1.0, base=0,
                               pattern=[[-1, P]], channel_multiplier=1).then_inc(consts, 1)
            pool.affine_select(out=ident_f[:, :], in_=ident_f[:, :], compare_op=ALU.not_equal, fill=1.0, base=0,
                               pattern=[[-1, P]], channel_multiplier=1).then_inc(consts, 1)
            pool.affine_select(out=before[:, :], in_=ones_f[:, :], compare_op=ALU.is_gt, fill=0.0, base=0,
                               pattern=[[1, P]], channel_multiplier=-1).then_inc(consts, 1)
            pool.iota(flat_id[:, :], [[1, P]], base=0, channel_multiplier=P,
                      allow_small_or_imprecise_dtypes=True).then_inc(consts, 1)
            pool.memset(srt_s[:, :], FLAG).then_inc(blank_ready, 1)
            pool.memset(diff, 0.0).then_inc(diff_made, 1)
            for n, (base, half) in enumerate(((0, 0.5), (1, -0.5), (1 - P, 0.5))):
                pool.wait_ge(diff_made, n + 1)
                pool.affine_select(out=diff, in_=diff, compare_op=ALU.not_equal, fill=half, base=base,
                                   pattern=[[-1, P]], channel_multiplier=1).then_inc(diff_made, 1)
            with pool.Fori(0, NB // 4) as i:
                for s in range(2):
                    lone_wait(pool, eidx_ready, i * 2 + (s + 1))
                    for a in range(2):
                        pool.indirect_dma_start(erow[:, s, a, :], None, emb,
                                                bass.IndirectOffsetOnAxis(ap=eidx[:, s, a:a + 1], axis=0)
                                                ).then_inc(emb_rows[s], 16)
            pool.iota(lane_start[:, :], [[LANE, P]], base=0, channel_multiplier=0,
                      allow_small_or_imprecise_dtypes=True).then_inc(consts, 1)
            pool.iota(slot_base[:, :], [[0, 1]], base=-1, channel_multiplier=LANE,
                      allow_small_or_imprecise_dtypes=True).then_inc(consts, 1)
            pool.iota(trash[:, :], [[0, 1]], base=NSLOT, channel_multiplier=1,
                      allow_small_or_imprecise_dtypes=True).then_inc(consts, 1)
            pool.iota(col_no[:, :], [[1, LANE]], base=0, channel_multiplier=0,
                      allow_small_or_imprecise_dtypes=True).then_inc(consts, 1)
            pool.affine_select(out=tie[:, :, :], in_=ones_f[:, 0:EX * EX].rearrange("p (a b) -> p a b", a=EX),
                               compare_op=ALU.is_gt, fill=0.0, base=0, pattern=[[1, EX], [-1, EX]],
                               channel_multiplier=0).then_inc(consts, 1)

            pool.wait_ge(list_blank, 16)
            with pool.Fori(0, BATCHES) as i:
                for s in range(2):
                    lone_wait(pool, sidx_ready, i * 2 + (s + 2))
                    for c in range(HALF):
                        pool.indirect_dma_start(srt, bass.IndirectOffsetOnAxis(ap=sidx[:, s, c:c + 1], axis=0),
                                                spay[:, s, c:c + 1], None).then_inc(scattered[s], 16)

            pool.wait_ge(first_ready, 1)
            pool.wait_ge(table_stored, 16 + BATCHES * 16)
            pool.indirect_dma_start(first_row[:, :], None, table,
                                    bass.IndirectOffsetOnAxis(ap=first_u[:, 0:1], axis=0)).then_inc(first_in, 16)
            with pool.Fori(0, BATCHES) as i:
                for s in range(2):
                    lone_wait(pool, gidx_ready, i * 2 + (s + 1))
                    for c in range(CH):
                        pool.indirect_dma_start(grow[:, s, c, :], None, table,
                                                bass.IndirectOffsetOnAxis(ap=gidx[:, s, c:c + 1], axis=0)
                                                ).then_inc(gathered[s], 16)

            for s in range(2):
                pool.wait_ge(orow_stored[s], 16 + BATCHES * 16)
            pool.wait_ge(spare_rows, 16)
            pool.wait_ge(mend_idx, 1)
            pool.indirect_dma_start(mrow[:, :], None, rows,
                                    bass.IndirectOffsetOnAxis(ap=mendu[:, 0:1], axis=0)).then_inc(mend_in, 16)
            pool.wait_ge(mend_ready, 1)
            pool.indirect_dma_start(rows, bass.IndirectOffsetOnAxis(ap=mendu[:, 1:2], axis=0),
                                    mout[:, :], None).then_inc(mend_out, 16)
            pool.wait_ge(mend_out, 16)

            with pool.Fori(0, NB // TB // 2) as i:
                for s in range(2):
                    lone_wait(pool, tidx_ready, i * 2 + (s + 1))
                    for c in range(TB):
                        pool.indirect_dma_start(trow[:, s, c, :], None, rows,
                                                bass.IndirectOffsetOnAxis(ap=tidx[:, s, c:c + 1], axis=0)
                                                ).then_inc(tail_rows[s], 16)

        @block.tensor
        def _(pe):
            pe.wait_ge(consts, 6)
            for to in ps_cnt + ps_code:
                m = pe.matmul(to, zero_b[:, :], zero_b[:, :], start=True, stop=True, skip_group_check=True)
            m.then_inc(hist_done, 2)
            with pe.Fori(0, EB // 64) as i:
                for j in range(4):
                    pe.wait_ge(hot_ready, i * 4 + (j + 1))
                    for a in range(HPAIR):
                        if a == HPAIR - CODED:
                            pe.wait_ge(code_ready, i * 4 + (j + 1))
                        for b in range(2):
                            m = pe.matmul((ps_cnt if a < HPAIR - CODED else ps_code)[b],
                                          hot16[:, j % 2, a, 0, :, b], hot16[:, j % 2, a, 1, :, b],
                                          start=False, stop=True, skip_group_check=True)
                    m.then_inc(hist_done, 1)
            pe.wait_ge(diff_made, 4)
            pe.wait_ge(hot_ready, EB // 16 + 1)
            pe.wait_ge(code_ready, EB // 16 + 1)
            for h in range(2):
                m = pe.matmul(ps_cnt[h], diff, code_sum[:, h, :], start=False, stop=True, skip_group_check=True)
            m.then_inc(hist_done, 1)
            pe.wait_ge(off_ready, 1)
            pe.matmul(ps_tr[:, 0:1], before[:, :], rowsum[:, :], start=True, stop=True).then_inc(off_mm, 1)
            pe.wait_ge(off_ready, 2)
            pe.transpose(ps_tr[:, 128:256], off[:, :], ident_f[:, :])
            pe.transpose(ps_tr[:, 256:384], end[:, :], ident_f[:, :]).then_inc(off_mm, 1)
            pe.matmul(ps_cnt[0], ident_f[:, :], off1[:, :], start=True, stop=True,
                      skip_group_check=True).then_inc(counted, 1)
            pe.matmul(ps_cnt[1], ident_f[:, :], off2[:, :], start=True, stop=True,
                      skip_group_check=True).then_inc(counted, 1)

            def hi_transposes(grp, s, slot):
                pe.wait_ge(oh_ready, grp + 1)
                for b in range(GRP):
                    m = pe.transpose(ps_hiT[:, s, b, :], hot(slot, b, 0), ident_b[:, :])
                m.then_inc(hiT_mm, 1)

            def same_high(grp, s):
                pe.wait_ge(hiT_ready, grp + 1)
                for b in range(GRP):
                    m = pe.matmul(ps_same[:, b, :], hiT_b[:, b, :], hiT_b[:, b, :], start=True, stop=True)
                m.then_inc(same_mm, 1)

            def attend(i, t):
                if t == 4 or t == 24:
                    n = t // 24
                    normed = (xn, xn2)[n]
                    lone_wait(pe, norm_ready, i * 2 + (n + 1))
                    pe.transpose(ps_tr[0:D, 0:P], normed[:, 0, :], ident_f[:, :])
                    pe.transpose(ps_tr[0:D, P:2 * P], normed[:, 1, :], ident_f[:, :]).then_inc(normT_mm, 1)
                if t == 8:
                    lone_wait(pe, normT_ready, i * 2 + 1)
                    pe.matmul(ps_tr[0:D, 256:512], qw_s[:, :], xnT[:, :], start=True, stop=True).then_inc(q_mm, 1)
                if t == 12:
                    pe.wait_ge(q_ready, i + 1)
                    for m in range(2):
                        last = pe.matmul(ps_sc[:, m, :], xnT[:, m * P:(m + 1) * P], qT[:, :], start=True, stop=True)
                    last.then_inc(score_mm, 1)
                if t == 17:
                    pe.wait_ge(att_ready, i + 1)
                    for n in range(2):
                        for m in range(2):
                            last = pe.matmul(ps_tr[:, n * D:(n + 1) * D], att[:, m, n * P:(n + 1) * P],
                                             xn[:, m, :], start=(m == 0), stop=(m == 1))
                    last.then_inc(value_mm, 1)
                if t == 28:
                    pe.wait_ge(normT_ready, i * 2 + 2)
                    for n in range(2):
                        last = pe.matmul(ps_tr[:, 256 + n * HE:256 + (n + 1) * HE], xnT2[:, n * P:(n + 1) * P],
                                         wg_s[:, :], start=True, stop=True)
                    last.then_inc(gat_mm, 1)

            hi_transposes(0, 0, 0)
            same_high(0, 0)
            pe.matmul(ps_slot[:, 0, 0, :], zero_b[:, :], zero_b[:, :], start=True, stop=True,
                      skip_group_check=True).then_inc(slot_mm, 1)
            with pe.Fori(0, BATCHES) as i:
                for g in range(STEPS):
                    s = g % 2
                    pe.wait_ge(hiT_ready, i * STEPS + (g + 1))
                    hi_transposes(i * STEPS + (g + 1), 1 - s, (g + 1) % 4)
                    for b in range(GRP):
                        if b == 0:
                            pe.wait_ge(same_ready, i * STEPS + (g + 1))
                        pe.wait_ge(slot_ready, i * (STEPS * GRP) + (GRP * g + b + 1))
                        pe.matmul(ps_slot[:, b % 2, 0, :], same[:, s, b, :], hot(g % 4, b, 1), start=True, stop=False)
                        pe.wait_ge(count_ready, i * (STEPS * GRP) + (GRP * g + b + 1))
                        pe.matmul(ps_cnt[b % 2], hot(g % 4, b, 0), hot(g % 4, b, 1), start=False, stop=True,
                                  skip_group_check=True).then_inc(counted, 1)
                        pe.matmul(ps_slot[:, b % 2, 0, :], hiT[:, s, b, :], count[:, b, :],
                                  start=False, stop=True).then_inc(slot_mm, 1)
                        if b == 1:
                            pe.wait_ge(same_ready, i * STEPS + (g + 1))
                            same_high(i * STEPS + (g + 1), 1 - s)
                        attend(i, GRP * g + b)

            pe.wait_ge(prep2, PREP2)
            pe.matmul(ps_tr[:, 0:1], cnt[:, :], ones_f[:, 0:1], start=True, stop=True).then_inc(lane_mm, 1)

            pe.matmul(ps_y[:, 0, 0:P], zero_b[:, :], zero_b[:, :], start=True, stop=True,
                      skip_group_check=True).then_inc(y_mm, 1)
            with pe.Fori(0, BATCHES) as i:
                pe.wait_ge(hid_ready, i * EX + 1)
                for e in range(EX):
                    pe.matmul(ps_hid[e], w1_s[:, e, :], xn2T[:, bass.ds(i * (2 * P), 2 * P)],
                              start=True, stop=True).then_inc(hid_mm, 1)
                pe.wait_ge(y_ready, i + 1)
                for a in range(2):
                    for e in range(EX):
                        if a == 0:
                            pe.wait_ge(hid_ready, i * EX + (e + 2))
                        pe.matmul(ps_y[:, a, e * D:(e + 1) * D], hid[:, e, a * P:(a + 1) * P], w2_s[:, e, :],
                                  start=True, stop=False)
                        last = pe.matmul(ps_y[:, a, e * D:(e + 1) * D], ones_f[0:1, :], b2_s[0:1, e * D:(e + 1) * D],
                                         start=False, stop=True)
                last.then_inc(y_mm, 1)

            pe.wait_ge(lane_ends, 1)
            for n in range(3):
                last = pe.transpose(ps_tr[0:SUM_W, n * P:(n + 1) * P], lane_sum[:, n, :], ident_f[:, :])
            last.then_inc(lane_endsT, 1)
            pe.wait_ge(lane_carry, 1)
            pe.transpose(ps_sc[:, 0, 0:SUM_W], lsum[:, 0:P], ident_f[0:SUM_W, 0:SUM_W])
            pe.transpose(ps_sc[:, 0, 32:32 + SUM_W], lmax[:, 0:P], ident_f[0:SUM_W, 0:SUM_W]).then_inc(lane_carryT, 1)

        @block.scalar
        def _(act):
            act.dma_start(qw_s[:, :], qw).then_inc(out_stored[0], 16)
            act.dma_start(wg_s[:, :], wgat).then_inc(out_stored[1], 16)
            act.wait_ge(loaded, 16 * 6)
            for arrived in (table_stored, orow_stored[0], orow_stored[1], y_stored, out_stored[0], out_stored[1]):
                act.wait_ge(arrived, 16)
            act.wait_ge(prep, 2)
            for s in range(2):
                act.activation(eidx[:, s, :], ids[:, 2 * s:2 * s + 2], ACT.Copy).then_inc(eidx_ready, 1)
            act.wait_ge(prep, 4)
            act.activation(minus_hi, digit_i, ACT.Copy, bias=0.5, scale=-1.0).then_inc(code_steps, 1)
            act.wait_ge(code_steps, 1)
            act.wait_ge(iota_ready, 1)
            with act.Fori(0, NB // 4) as i:
                for s in range(2):
                    act.wait_ge(emb_rows[s], i * 32 + 32)
                    for a in range(2):
                        k = i * 4 + (2 * s + a)
                        act.activation(X[:, bass.ds(k, 1), :].rearrange("p o d -> p (o d)"), erow[:, s, a, :],
                                       ACT.Copy, scale=keep[:, bass.ds(k, 1)]).then_inc(emb_kept, 1)
                    act.activation(eidx[:, s, :], ids[:, bass.ds(i * 4 + (4 + 2 * s), 2)], ACT.Copy
                                   ).then_inc(eidx_ready, 1)
                    for j in (2 * s, 2 * s + 1):
                        act.wait_ge(hist_done, i * 4 + (j + 1))
                        for q in range(2 * CODED):
                            a, b = HPAIR - CODED + q // 2, q % 2
                            m = act.activation(hot16[:, j % 2, a, 0, :, b], ps_iota, ACT.Sign,
                                               bias=minus_hi[:, bass.ds(i * 64 + (j * 16 + 2 * a + b), 1)])
                        m.then_inc(code_ready, 1)
            act.wait_ge(hist_done, EB // 16 + 2)
            act.activation(code_sum[:, 1, :], ps_code[1], ACT.Copy).then_inc(code_ready, 1)

            def copy_hiT(grp, s):
                act.wait_ge(hiT_mm, grp + 1)
                act.activation(hiT_b[:, :, :], ps_hiT[:, s, :, :], ACT.Copy)
                act.activation(hiT[:, s, :, :], ps_hiT[:, s, :, :], ACT.Copy).then_inc(hiT_ready, 1)

            def std_of(i, n):
                act.wait_ge(var_ready, i * 2 + (n + 1))
                act.activation(std[:, n, :], vare[:, n, :], ACT.Sqrt).then_inc(std_ready, 1)

            def attend(i, t):
                if t == 7:
                    act.wait_ge(normT_mm, i * 2 + 1)
                    act.activation(xnT[:, :], ps_tr[0:D, 0:2 * P], ACT.Copy).then_inc(normT_ready, 1)
                if t == 11:
                    act.wait_ge(q_mm, i + 1)
                    act.activation(qT[:, :], ps_tr[0:D, 256:512], ACT.Copy).then_inc(q_ready, 1)
                if t == 15:
                    act.wait_ge(score_mm, i + 1)
                    act.activation(att[:, :, :], ps_sc[:, :, :], ACT.Sigmoid).then_inc(att_ready, 1)
                if t == 20:
                    std_of(i, 1)
                if t == 27:
                    act.wait_ge(normT_mm, i * 2 + 2)
                    act.activation(xnT2[:, :], ps_tr[0:D, 0:2 * P], ACT.Copy).then_inc(normT_ready, 1)
                if t == 29:
                    act.wait_ge(normT_ready, i * 2 + 2)
                    act.activation(xn2T[:, bass.ds(i * (2 * P), 2 * P)], xnT2[:, :], ACT.Copy
                                   ).then_inc(normT_kept, 1)

            copy_hiT(0, 0)
            with act.Fori(0, BATCHES) as i:
                std_of(i, 0)
                for g in range(STEPS):
                    s = g % 2
                    for b in range(GRP):
                        if b == 2:
                            act.wait_ge(slot_mm, i * (STEPS * GRP) + (GRP * g + 1))
                            copy_hiT(i * STEPS + (g + 1), 1 - s)
                        act.wait_ge(counted, i * (STEPS * GRP) + (GRP * g + b + 1))
                        act.activation(count[:, b, :], ps_cnt[b % 2], ACT.Copy).then_inc(count_ready, 1)
                        attend(i, GRP * g + b)

            act.wait_ge(slot_mm, EB + 1)
            act.activation(hid[:, 0, 0:EX], b1_s[:, :], ACT.Copy).then_inc(hid_ready, 1)
            act.activation(y_out[:, 0, 0:EX], b1_s[:, :], ACT.Copy).then_inc(y_ready, 1)
            act.activation(orow[:, 0, 0, 0:EX], b1_s[:, :], ACT.Copy).then_inc(orow_ready, 1)
            with act.Fori(0, BATCHES) as i:
                for s in range(2):
                    act.wait_ge(expo_ready, i * 2 + (s + 1))
                    act.activation(ex[:, s, :, :], expo[:, s, :, :], ACT.Exp).then_inc(exp_ready, 1)
                    act.wait_ge(run_ready, i * 2 + (s + 1))
                    act.wait_ge(orow_stored[s], i * 16 + 16)
                    act.activation(orow[:, s, :, 0:SUM_W].rearrange("p t f -> p f t"),
                                   run[:, s, :, 1:CH + 1], ACT.Copy)
                    act.activation(orow[:, s, :, SUM_W:ROW_W].rearrange("p t f -> p f t"),
                                   mx[:, s, :, 1:CH + 1], ACT.Copy).then_inc(orow_ready, 1)
                    if s == 0:
                        act.wait_ge(y_mm, i + 1)
                        for e in range(EX):
                            act.wait_ge(hid_mm, i * EX + (e + 1))
                            act.activation(hid[:, e, :], ps_hid[e], ACT.Gelu, bias=b1_s[:, e:e + 1]
                                           ).then_inc(hid_ready, 1)
                        act.wait_ge(y_mm, i + 2)
                        act.wait_ge(y_stored, i * 16 + 16)
                        act.activation(y_out[:, :, :], ps_y, ACT.Copy).then_inc(y_ready, 1)

            act.wait_ge(lane_expo, 1)
            act.activation(lexp[:, :, :], lexp[:, :, :], ACT.Exp).then_inc(lane_exp, 1)
            act.wait_ge(mend_expo, 1)
            act.activation(mexp[:, :, :], mexp[:, :, :], ACT.Exp).then_inc(mend_exp, 1)

            out_v = out.rearrange("(k p) d -> p k d", p=P)
            with act.Fori(0, NB // TB // 2) as i:
                for s in range(2):
                    act.wait_ge(tail_var, i * 2 + (s + 1))
                    act.activation(red[:, 3, :], red[:, 2, :], ACT.Sqrt).then_inc(tail_std, 1)
                    act.wait_ge(tail_sub, i * 2 + (s + 1))
                    act.activation(gate[:, :, :], sc4[:, :, :], ACT.Exp, scale=1.0 / HD).then_inc(tail_exp, 1)
                    act.wait_ge(gate_ready, i * 2 + (s + 1))
                    act.wait_ge(y_loaded[s], i * 16 + 16)
                    for k in range(TB):
                        m = act.activation(gated[:, k, EX - 1, :], y_ring[:, s, k, (EX - 1) * D:EX * D], ACT.Copy,
                                           scale=gate[:, k, EX - 1:EX])
                    m.then_inc(last_gated, 1)
                    act.wait_ge(out_ready, i * 2 + (s + 1))
                    act.dma_start(out_v[:, bass.ds(i * (2 * TB) + s * TB, TB), :], o_ring[:, s, :, :]
                                  ).then_inc(out_stored[s], 16)
            for s in range(2):
                act.wait_ge(out_stored[s], 16 + NB // TB // 2 * 16)

        @block.vector
        def _(dve):
            V = nc.vector
            c = Chain(dve, prep)
            c.mark(V.memset(ids[:, NB:NB + 4], 0))
            dve.wait_ge(loaded, 16 * 6)
            c.mark(V.tensor_scalar(keep[:, 0:NB], ids[:, 0:NB], 0, None, ALU.not_equal))
            c.mark(V.memset(digit[:, EB // 2:EB // 2 + 4, :, :], 0.0))
            dve.wait_ge(edges_in, 16)
            c.step(V.tensor_scalar(digit_i, dst, 7, None, ALU.logical_shift_right))
            c.step(V.tensor_copy(digit[:, 0:EB // 2, 0, :], digit_i.rearrange("p (a b) -> p a b", b=2)))
            c.step(V.tensor_scalar(low_i, dst, P - 1, None, ALU.bitwise_and))
            c.step(V.tensor_copy(digit[:, 0:EB // 2, 1, :], low_i.rearrange("p (a b) -> p a b", b=2)))
            dve.wait_ge(consts, 6)
            V.tensor_copy(ps_iota, iota2[:, :, 0]).then_inc(iota_ready, 1)

            def one_hots(pair, to):
                units = to.shape[1]
                d = digit[:, bass.ds(pair, units // 2), :, :].rearrange("p a h b -> p (a h) b")
                return V.tensor_tensor(to,
                                       iota2[:, :, :].unsqueeze(1).broadcast_to([P, units, P, 2]),
                                       d.unsqueeze(2).broadcast_to([P, units, P, 2]), ALU.is_equal)

            with dve.Fori(0, EB // 64) as i:
                for j in range(4):
                    dve.wait_ge(hist_done, i * 4 + (j + 1))
                    own = HPAIR - CODED
                    one_hots(i * 32 + HPAIR * j, hot16[:, j % 2, 0:own].rearrange("p a h n b -> p (a h) n b"))
                    low = digit[:, bass.ds(i * 32 + (HPAIR * j + own), CODED), 1, :]
                    full = [P, CODED, P, 2]
                    V.tensor_tensor(hot16[:, j % 2, own:HPAIR, 1], iota2[:, :, :].unsqueeze(1).broadcast_to(full),
                                    low.unsqueeze(2).broadcast_to(full), ALU.is_equal).then_inc(hot_ready, 1)
            dve.wait_ge(hist_done, EB // 16 + 2)
            V.tensor_copy(code_sum[:, 0, :], ps_code[0]).then_inc(hot_ready, 1)
            dve.wait_ge(hist_done, EB // 16 + 3)
            c.step(V.tensor_copy(hist_even[:, :], ps_cnt[0]))
            c.step(V.tensor_tensor(hist[:, :], hist_even[:, :], ps_cnt[1], ALU.add))
            c.step(V.tensor_tensor_scan(incl[:, :], ones_f[:, :], hist[:, :], 0.0, ALU.mult, ALU.add))
            V.tensor_copy(rowsum[:, :], incl[:, P - 1:P]).then_inc(off_ready, 1)
            dve.wait_ge(off_ready, 1)
            c.step(V.tensor_tensor(incl[:, :], incl[:, :], flat_id[:, :], ALU.add))
            dve.wait_ge(off_mm, 1)
            c.step(V.tensor_copy(rowoff[:, :], ps_tr[:, 0:1]))
            c.step(V.tensor_scalar(end[:, :], incl[:, :], rowoff[:, 0:1], None, ALU.add))
            c.step(V.tensor_tensor(off[:, :], end[:, :], hist[:, :], ALU.subtract))
            c.step(V.tensor_scalar(off1[:, :], off[:, :], 1.0, None, ALU.add))
            V.tensor_tensor(off2[:, :], off1[:, :], hist_even[:, :], ALU.add).then_inc(off_ready, 1)
            dve.wait_ge(off_mm, 2)
            c.mark(V.tensor_copy(offT[:, :], ps_tr[:, 128:256]))
            c.mark(V.memset(endT[:, NB:NB + 32], 0))
            c.mark(V.tensor_copy(endT[:, 0:NB], ps_tr[:, 256:384]))
            c.mark(V.memset(tabt[:, :, :], 1.0))
            c.step(V.memset(X[:, NB:NB + 2, :], 0.0))

            def mask_same(grp, s):
                dve.wait_ge(same_mm, grp + 1)
                V.tensor_tensor(same[:, s, :, :], ps_same[:, :, :],
                                before[:, :].unsqueeze(1).broadcast_to([P, GRP, P]), ALU.mult
                                ).then_inc(same_ready, 1)

            one_hots(0, hot_ring[:, 0, :, :, :]).then_inc(oh_ready, 1)
            one_hots(2, hot_ring[:, 1, :, :, :]).then_inc(oh_ready, 1)
            mask_same(0, 0)
            V.memset(slotf[:, :, :], 0.0).then_inc(slot_ready, 2)
            V.memset(picked[:, :, :], 0.0).then_inc(sidx_ready, 1)
            dve.wait_ge(emb_kept, NB)
            dve.wait_ge(consts, 11)
            a = Chain(dve, dve_att)

            def layer_norm_stats(chain, n):
                chain.mark(V.bn_stats(stats[:, n, 0, :], xcur[:, 0, :]))
                lone_wait(dve, chain.s, chain.mark(V.bn_stats(stats[:, n, 1, :], xcur[:, 1, :])))
                chain.mark(V.bn_aggr(mv[:, n, 0, :], stats[:, n, 0, :]))
                chain.step(V.bn_aggr(mv[:, n, 1, :], stats[:, n, 1, :]))
                V.tensor_scalar(vare[:, n, :], mv[:, n, :, 1], LN_EPS, None, ALU.add).then_inc(var_ready, 1)

            def layer_norm(i, n, to):
                dve.wait_ge(std_ready, i * 2 + (n + 1))
                a.step(V.reciprocal(rstd[:, n, :], std[:, n, :]))
                for t in range(2):
                    m = V.tensor_scalar(to[:, t, :], xcur[:, t, :], mv[:, n, t, 0:1], rstd[:, n, t:t + 1],
                                        ALU.subtract, ALU.mult)
                m.then_inc(norm_ready, 1)

            def attend(i, t):
                if t == 1:
                    layer_norm(i, 0, xn)
                if t == 18:
                    dve.wait_ge(value_mm, i + 1)
                    a.step(V.tensor_tensor(xcur[:, :, :], xcur[:, :, :],
                                           ps_tr[:, 0:2 * D].rearrange("p (t d) -> p t d", t=2), ALU.add))
                    layer_norm_stats(a, 1)
                    a.mark(V.tensor_copy(X[:, bass.ds(i * 2, 2), :], xcur[:, :, :]))
                if t == 22:
                    layer_norm(i, 1, xn2)
                if t == 29:
                    dve.wait_ge(gat_mm, i + 1)
                    dve.wait_ge(table_stored, i * 16 + 16)
                    hv = ps_tr[:, 256:256 + 2 * HE].rearrange("p (t f) -> p t f", t=2)
                    a.mark(V.tensor_copy(tabt[:, :, 0:SUM_W].rearrange("p t (h e) -> p t h e", h=HD)[:, :, :, 0:EX],
                                         hv.rearrange("p t (h e) -> p t h e", h=HD)))
                    for n in range(2):
                        a.mark(V.tensor_tensor(hatt[:, n, :, :], hv,
                                               att_s[:, n, :].unsqueeze(1).broadcast_to([P, 2, HE]), ALU.mult))
                    dve.wait_ge(dve_att, a.at + (a.base + a.n))
                    for n in range(2):
                        m = V.tensor_reduce(tabt[:, :, SUM_W + n * HD:SUM_W + (n + 1) * HD],
                                            hatt[:, n, :, :].rearrange("p t (h e) -> p t h e", h=HD),
                                            AX.X, ALU.add)
                    m.then_inc(table_ready, 1)
                if t == 30:
                    a.step(V.tensor_copy(xcur[:, :, :], X[:, bass.ds(i * 2 + 2, 2), :]))
                    layer_norm_stats(a, 0)

            c.step(V.tensor_copy(xcur[:, :, :], X[:, 0:2, :]))
            layer_norm_stats(c, 0)
            with dve.Fori(0, BATCHES) as i:
                a.turn(i, 16)
                for g in range(STEPS):
                    s = g % 2
                    grp = i * STEPS + g
                    dve.wait_ge(slot_ready, grp * GRP + 2)
                    one_hots(grp * 2 + 4, hot_ring[:, (g + 2) % 4, :, :, :]).then_inc(oh_ready, 1)
                    if g == 0:
                        dve.wait_ge(sidx_ready, i * 2 + 1)
                    for b in range(GRP):
                        if b == 3:
                            mask_same(grp + 1, 1 - s)
                        dve.wait_ge(slot_mm, grp * GRP + (b + 2))
                        n = GRP * g + b
                        V.tensor_tensor_reduce(out=picked[:, b, :], in0=ps_slot[:, b % 2, 0, :], in1=hot(g % 4, b, 1),
                                               scale=1.0, scalar=0.0, op0=ALU.mult, op1=ALU.add,
                                               accum_out=slotf[:, n // HALF, n % HALF:n % HALF + 1]
                                               ).then_inc(slot_ready, 1)
                        attend(i, n)
                    if g % 4 == 3:
                        h = g // 4
                        dve.wait_ge(scattered[h], i * (HALF * 16) + 16)
                        V.tensor_copy(spay[:, h, :], src[:, bass.ds(i * (2 * HALF) + h * HALF, HALF)])
                        dve.wait_ge(slot_ready, (grp + 1) * GRP + 2)
                        V.tensor_copy(sidx[:, h, :], slotf[:, h, :]).then_inc(sidx_ready, 1)
                a.end_turn(BATCHES)

            pre = Chain(dve, prep2)
            dve.wait_ge(counted, EB + 2)
            for q in range(4):
                pre.step(V.tensor_tensor(cmp, offT[:, :].unsqueeze(1).broadcast_to([P, 32, P]),
                                        lane_start[:, 32 * q:32 * q + 32].unsqueeze(2).broadcast_to([P, 32, P]),
                                        ALU.is_lt))
                pre.step(V.tensor_reduce(cnt[:, 32 * q:32 * q + 32], cmp, AX.X, ALU.add))
            assert pre.n == PREP2
            dve.wait_ge(lane_mm, 1)
            pre.step(V.tensor_scalar(node[:, 1, CH:CH + 1], ps_tr[:, 0:1], -1.0, None, ALU.add))
            V.tensor_scalar(first_u[:, :], node[:, 1, CH:CH + 1], 0.0, None, ALU.max).then_inc(first_ready, 1)
            for s in range(2):
                pre.mark(V.memset(keep4[:, s, :, 0:1], 0.0))
                pre.mark(V.memset(neg4[:, s, :, 0:1], -BIG))
                pre.mark(V.memset(decay[:, s, :, 0:1], 0.0))
            pre.mark(V.memset(mx[:, 1, :, CH:CH + 1], -BIG))
            pre.mark(V.memset(run[:, 1, :, CH:CH + 1], 0.0))
            pre.step(V.memset(trow[:, 0, 0, 0:1], 0.0))
            dve.wait_ge(first_in, 16)
            pre.step(V.tensor_copy(ad[:, 1, :, CH], first_row[:, SUM_W + HD:SUM_W + 2 * HD]))

            def stream_index(chain, s, at):
                sv = srt_s[:, bass.ds(at, CH)]
                chain.mark(V.tensor_copy(start[:, s, 0:1], node[:, 1 - s, CH:CH + 1]))
                chain.step(V.tensor_scalar(start[:, s, 1:CH + 1], sv, FLAG, None, ALU.is_ge))
                chain.step(V.tensor_tensor_scan(node[:, s, :], ones_f[:, 0:CH + 1], start[:, s, :], 0.0,
                                                ALU.mult, ALU.add))
                chain.step(V.scalar_tensor_tensor(self_id[:, s, :], node[:, s, 1:CH + 1], -float(FLAG),
                                                  start[:, s, 1:CH + 1], ALU.add, ALU.mult))
                V.tensor_tensor(gidx[:, s, :], self_id[:, s, :], sv, ALU.add).then_inc(gidx_ready, 1)

            dve.wait_ge(sorted_in, 16)
            stream_index(pre, 0, 0)
            stream_index(pre, 1, CH)
            mending = Chain(dve, dve_mend)
            mending.step(V.tensor_scalar(key, srt_s[:, 0:LANE], float(FLAG), float(LANE), ALU.is_lt, ALU.mult))
            mending.step(V.tensor_tensor(key, key, col_no[:, :], ALU.add))
            mending.step(V.tensor_reduce(fstart[:, :], key, AX.X, ALU.min))
            mending.mark(V.tensor_scalar(lane_sum[:, 2, :], fstart[:, 0:1].broadcast_to([P, SUM_W]), float(LANE),
                                         None, ALU.is_lt))
            mending.step(V.tensor_tensor(mendq[:, 0:1], slot_base[:, :], fstart[:, :], ALU.add))
            mending.mark(V.tensor_tensor(mendq[:, 1:2], trash[:, :], mendq[:, 0:1], ALU.subtract))
            mending.step(V.tensor_scalar(mendq[:, 2:3], fstart[:, :], 0.0, None, ALU.is_equal))
            mending.mark(V.scalar_tensor_tensor(mendq[:, 3:4], mendq[:, 1:2], mendq[:, 2:3], mendq[:, 0:1],
                                           ALU.mult, ALU.add))
            mending.mark(V.tensor_scalar(mendu[:, 0:1], mendq[:, 0:1], 0.0, None, ALU.max))
            dve.wait_ge(dve_mend, mending.n)
            V.tensor_copy(mendu[:, 1:2], mendq[:, 3:4]).then_inc(mend_idx, 1)

            st = Chain(dve, dve_str)
            with dve.Fori(0, BATCHES) as i:
                st.turn(i, 36)
                for s in range(2):
                    r = 1 - s
                    at = i * (2 * CH) + s * CH
                    sv = srt_s[:, bass.ds(at, CH)].unsqueeze(1).broadcast_to([P, HD, CH])
                    dve.wait_ge(orow_ready, i * 2 + (s + 1))
                    st.mark(V.tensor_scalar(keep4[:, s, :, 1:CH + 1], sv, FLAG, None, ALU.is_lt))
                    st.mark(V.tensor_scalar(neg4[:, s, :, 1:CH + 1], sv, FLAG, -BIG, ALU.is_ge, ALU.mult))
                    st.mark(V.tensor_copy(ad_in[:, s, :, 0], ad[:, r, :, CH]))
                    st.mark(V.tensor_copy(e_in[:, s, :, 0], mx[:, r, :, CH]))
                    st.mark(V.tensor_copy(add[:, s, :, 0], run[:, r, :, CH]))
                    dve.wait_ge(gathered[s], i * (CH * 16) + CH * 16)
                    g_t = grow[:, s, :, :].rearrange("p t f -> p f t")
                    st.step(V.scalar_tensor_tensor(ad_in[:, s, :, 1:CH + 1], sv, FLAG,
                                                   g_t[:, SUM_W + HD:SUM_W + 2 * HD, :], ALU.is_ge, ALU.mult))
                    flat = lambda t: t[:, s, :, :].rearrange("p f t -> p (f t)")
                    st.step(V.tensor_tensor_scan(flat(ad), flat(keep4), flat(ad_in), 0.0, ALU.mult, ALU.add))
                    st.step(V.tensor_tensor(e_raw[:, s, :, :], g_t[:, SUM_W:SUM_W + HD, :], ad[:, s, :, 1:CH + 1],
                                            ALU.add))
                    st.step(V.scalar_tensor_tensor(e_in[:, s, :, 1:CH + 1], e_raw[:, s, :, :], SLOPE,
                                                   e_raw[:, s, :, :], ALU.mult, ALU.max))
                    st.step(V.tensor_tensor_scan(flat(mx), flat(neg4), flat(e_in), 0.0, ALU.add, ALU.max))
                    st.mark(V.tensor_tensor(expo[:, s, HD:2 * HD, :], e_in[:, s, :, 1:CH + 1],
                                            mx[:, s, :, 1:CH + 1], ALU.subtract))
                    st.step(V.tensor_tensor(expo[:, s, 0:HD, :], mx[:, s, :, 0:CH], mx[:, s, :, 1:CH + 1],
                                            ALU.subtract))
                    V.tensor_scalar(expo[:, s, 0:HD, :], expo[:, s, 0:HD, :], 0.0, None, ALU.min
                                    ).then_inc(expo_ready, 1)
                    dve.wait_ge(exp_ready, i * 2 + (s + 1))
                    fan = [P, HD, EX + 1, CH]
                    st.mark(V.tensor_tensor(decay[:, s, :, 1:CH + 1].rearrange("p (h e) t -> p h e t", h=HD),
                                            ex[:, s, 0:HD, :].unsqueeze(2).broadcast_to(fan),
                                            keep4[:, s, :, 1:CH + 1].unsqueeze(2).broadcast_to(fan), ALU.mult))
                    st.step(V.tensor_tensor(add[:, s, :, 1:CH + 1].rearrange("p (h e) t -> p h e t", h=HD),
                                            g_t[:, 0:SUM_W, :].rearrange("p (h e) t -> p h e t", h=HD),
                                            ex[:, s, HD:2 * HD, :].unsqueeze(2).broadcast_to(fan), ALU.mult))
                    stream_index(st, s, at + 2 * CH)
                    V.tensor_tensor_scan(flat(run), flat(decay), flat(add), 0.0, ALU.mult, ALU.add
                                         ).then_inc(run_ready, 1)
                    dve.wait_ge(run_ready, i * 2 + (s + 1))
                st.end_turn(BATCHES)

            V.tensor_copy(lane_sum[:, 1, :].rearrange("p (h e) -> p h e", h=HD),
                          mx[:, 1, :, CH:CH + 1].broadcast_to([P, HD, EX + 1]))
            V.tensor_copy(lane_sum[:, 0, :], run[:, 1, :, CH]).then_inc(lane_ends, 1)
            mending.mark(V.memset(lmax[:, 0:1], -BIG))
            mending.mark(V.memset(lsum[:, 0:1], 0.0))
            dve.wait_ge(lane_endsT, 1)
            mending.step(V.tensor_copy(laneT[:, :, :], ps_tr[0:SUM_W, 0:3 * P].rearrange("p (n l) -> p n l", n=3)))
            mending.step(V.tensor_scalar(lneg[:, :], laneT[:, 2, :], -BIG, None, ALU.mult))
            mending.step(V.tensor_tensor_scan(lmax[:, 1:P + 1], lneg[:, :], laneT[:, 1, :], -BIG, ALU.add, ALU.max))
            mending.mark(V.tensor_tensor(lexp[:, 1, :], laneT[:, 1, :], lmax[:, 1:P + 1], ALU.subtract))
            mending.step(V.tensor_tensor(lexp[:, 0, :], lmax[:, 0:P], lmax[:, 1:P + 1], ALU.subtract))
            V.tensor_scalar(lexp[:, 0, :], lexp[:, 0, :], 0.0, None, ALU.min).then_inc(lane_expo, 1)
            mending.step(V.tensor_scalar(lneg[:, :], laneT[:, 2, :], -1.0, 1.0, ALU.mult, ALU.add))
            dve.wait_ge(lane_exp, 1)
            mending.mark(V.tensor_tensor(lexp[:, 0, :], lexp[:, 0, :], lneg[:, :], ALU.mult))
            mending.step(V.tensor_tensor(lexp[:, 1, :], lexp[:, 1, :], laneT[:, 0, :], ALU.mult))
            V.tensor_tensor_scan(lsum[:, 1:P + 1], lexp[:, 0, :], lexp[:, 1, :], 0.0, ALU.mult, ALU.add
                                 ).then_inc(lane_carry, 1)
            dve.wait_ge(lane_carryT, 1)
            mending.step(V.tensor_copy(carry[:, :, :],
                                  ps_sc[:, 0, 0:64].rearrange("p (n f) -> p n f", n=2)[:, :, 0:SUM_W]))
            dve.wait_ge(mend_in, 16)
            cmax = carry[:, 1, :].rearrange("p (h e) -> p h e", h=HD)[:, :, 0]
            mending.step(V.tensor_tensor(mmax[:, :], cmax, mrow[:, SUM_W:ROW_W], ALU.max))
            V.tensor_copy(mout[:, SUM_W:ROW_W], mmax[:, :])
            V.tensor_tensor(mexp[:, 0, :], cmax, mmax[:, :], ALU.subtract)
            V.tensor_tensor(mexp[:, 1, :], mrow[:, SUM_W:ROW_W], mmax[:, :], ALU.subtract).then_inc(mend_expo, 1)
            dve.wait_ge(mend_exp, 1)
            for n, part in ((0, carry[:, 0, :]), (1, mrow[:, 0:SUM_W])):
                mending.mark(V.tensor_tensor(mtmp[:, n, :].rearrange("p (h e) -> p h e", h=HD),
                                        part.rearrange("p (h e) -> p h e", h=HD),
                                        mexp[:, n, :].unsqueeze(2).broadcast_to([P, HD, EX + 1]), ALU.mult))
            dve.wait_ge(dve_mend, mending.n)
            V.tensor_tensor(mout[:, 0:SUM_W], mtmp[:, 0, :], mtmp[:, 1, :], ALU.add).then_inc(mend_ready, 1)

            for s in range(2):
                V.tensor_copy(tidx[:, s, :], endT[:, s * TB:(s + 1) * TB]).then_inc(tidx_ready, 1)
            tail = Chain(dve, dve_tail)
            hs = lambda t: t.rearrange("p k (h e) -> p k h e", h=HD)
            with dve.Fori(0, NB // TB // 2) as i:
                tail.turn(i, 2 * TAIL)
                for s in range(2):
                    n0 = tail.n
                    dve.wait_ge(tail_rows[s], i * (TB * 16) + TB * 16)
                    sums = hs(trow[:, s, :, 0:SUM_W])
                    tail.step(V.tensor_scalar(den[:, :, :], sums[:, :, :, EX], DEN_EPS, None, ALU.add))
                    tail.step(V.reciprocal(den[:, :, :], den[:, :, :]))
                    tail.step(V.tensor_tensor(agg[:, :, :, :], sums[:, :, :, 0:EX],
                                            den[:, :, :].unsqueeze(3).broadcast_to([P, TB, HD, EX]), ALU.mult))
                    ag = agg[:, :, :, :].rearrange("p k h e -> p k (h e)")
                    over_k = lambda v: v.unsqueeze(1).broadcast_to([P, TB, HE])
                    over_f = lambda v: v.unsqueeze(2).broadcast_to([P, TB, HE])
                    tail.step(V.tensor_tensor(ag, ag, over_k(gate_p[:, 0, :]), ALU.add))
                    tail.step(V.tensor_reduce(red[:, 0, :], ag, AX.X, ALU.add))
                    tail.step(V.scalar_tensor_tensor(ag, over_f(red[:, 0, :]), -1.0 / HE, ag, ALU.mult, ALU.add))
                    tail.step(V.tensor_tensor(sq[:, :, :], ag, ag, ALU.mult))
                    tail.step(V.tensor_reduce(red[:, 0, :], sq[:, :, :], AX.X, ALU.add))
                    V.tensor_scalar(red[:, 2, :], red[:, 0, :], 1.0 / HE, LN_EPS, ALU.mult, ALU.add
                                    ).then_inc(tail_var, 1)
                    dve.wait_ge(tail_std, i * 2 + (s + 1))
                    tail.step(V.reciprocal(red[:, 4, :], red[:, 3, :]))
                    tail.step(V.tensor_tensor(ag, ag, over_f(red[:, 4, :]), ALU.mult))
                    tail.step(V.tensor_tensor(ag, ag, over_k(gate_p[:, 1, :]), ALU.mult))
                    tail.step(V.tensor_tensor(ag, ag, over_k(gate_p[:, 2, :]), ALU.add))
                    tail.step(V.tensor_reduce(sc4[:, :, :], agg[:, :, :, :].rearrange("p k h e -> p k e h"), AX.X, ALU.add))
                    pair = [P, TB, EX, EX]
                    other = sc4[:, :, :].unsqueeze(2).broadcast_to(pair)
                    own = sc4[:, :, :].unsqueeze(3).broadcast_to(pair)
                    tail.mark(V.tensor_tensor(dif[:, :, :, :], other, own, ALU.is_equal))
                    tail.step(V.tensor_reduce(red[:, 5, :], sc4[:, :, :], AX.X, ALU.max))
                    dif_f = dif[:, :, :, :].rearrange("p k e o -> p k (e o)")
                    tail.mark(V.tensor_tensor(dif_f, dif_f, over_k(tie[:, :, :].rearrange("p e o -> p (e o)")), ALU.mult))
                    tail.step(V.tensor_tensor(agg[:, :, :, :], other, own, ALU.is_gt))
                    V.tensor_tensor(sc4[:, :, :], sc4[:, :, :], red[:, 5, :].unsqueeze(2).broadcast_to([P, TB, EX]),
                                    ALU.subtract).then_inc(tail_sub, 1)
                    tail.step(V.tensor_tensor(dif_f, dif_f, ag, ALU.add))
                    tail.step(V.tensor_reduce(rank[:, :, :], dif[:, :, :, :], AX.X, ALU.add))
                    dve.wait_ge(tail_exp, i * 2 + (s + 1))
                    tail.step(V.scalar_tensor_tensor(gate[:, :, :], rank[:, :, :], 1.5, gate[:, :, :], ALU.is_lt, ALU.mult))
                    tail.step(V.tensor_reduce(red[:, 0, :], gate[:, :, :], AX.X, ALU.add))
                    tail.step(V.reciprocal(red[:, 1, :], red[:, 0, :]))
                    V.tensor_tensor(gate[:, :, :], gate[:, :, :],
                                    red[:, 1, :].unsqueeze(2).broadcast_to([P, TB, EX]), ALU.mult
                                    ).then_inc(gate_ready, 1)
                    dve.wait_ge(gate_ready, i * 2 + (s + 1))
                    dve.wait_ge(y_loaded[s], i * 16 + 16)
                    for e in range(EX - 1):
                        tail.mark(V.tensor_tensor(gated[:, :, e, :], y_ring[:, s, :, e * D:(e + 1) * D],
                                                gate[:, :, e:e + 1].broadcast_to([P, TB, D]), ALU.mult))
                    dve.wait_ge(dve_tail, tail.at + (tail.base + tail.n - 1))
                    dve.wait_ge(out_stored[s], i * 16 + 16)
                    tail.mark(V.tensor_tensor(o_half[:, 0, :, :], gated[:, :, 0, :], gated[:, :, 1, :], ALU.add))
                    dve.wait_ge(dve_tail, tail.at + (tail.base + tail.n - 1))
                    dve.wait_ge(last_gated, i * 2 + (s + 1))
                    V.tensor_copy(tidx[:, s, :], endT[:, bass.ds(i * (2 * TB) + (2 + s) * TB, TB)]).then_inc(tidx_ready, 1)
                    tail.step(V.tensor_tensor(o_half[:, 1, :, :], gated[:, :, 2, :], gated[:, :, 3, :], ALU.add))
                    tail.step(V.tensor_tensor(o_half[:, 0, :, :], o_half[:, 0, :, :], o_half[:, 1, :, :], ALU.add))
                    V.tensor_tensor(o_ring[:, s, :, :], o_half[:, 0, :, :],
                                    X[:, bass.ds(i * (2 * TB) + s * TB, TB), :], ALU.add).then_inc(out_ready, 1)
                    assert tail.n - n0 == TAIL, tail.n - n0
                tail.end_turn(NB // TB // 2)


NAMES = ["x", "L0_tok_W", "L0_attn_q_weight", "L0_ffn_W_gat", "L0_ffn_att_src", "L0_ffn_att_dst", "L0_ffn_b_gat",
         "L0_ffn_ln_gamma", "L0_ffn_ln_beta", "L0_ffn_W1", "L0_ffn_b1", "L0_ffn_W2", "L0_ffn_b2"]


def kernel(**inputs):
    import concourse.bacc as bacc
    from concourse.bass_utils import run_bass_kernel_spmd

    x, emb, qw, wgat, asrc, adst, bgat, gamma, beta, w1, b1, w2, b2 = (np.asarray(inputs[n]) for n in NAMES)
    edges = np.asarray(inputs["L0_ffn_edge_index"])
    he = wgat.shape[1]
    arrays = {
        "tok": x.reshape(-1, P).T,
        "emb": emb.T,
        "qw": qw,
        "wgat": wgat,
        "att_src": asrc.reshape(1, he),
        "att_dst": adst.reshape(1, he),
        "b_gat": bgat.reshape(1, he),
        "gamma": gamma.reshape(1, he),
        "beta": beta.reshape(1, he),
        "w1": w1.transpose(1, 0, 2),
        "b1": b1.T,
        "w2": w2.transpose(1, 0, 2),
        "b2": b2.reshape(1, -1),
        "esrc": edges[0].reshape(P, -1),
        "edst": edges[1].reshape(P, -1),
    }
    arrays = {k: np.ascontiguousarray(v) for k, v in arrays.items()}
    nc = bacc.Bacc("TRN2", target_bir_lowering=False, num_devices=1)
    args = [nc.dram_tensor("in_" + k, v.shape, mybir.dt.from_np(v.dtype), kind="ExternalInput").ap()
            for k, v in arrays.items()]
    shape = (x.size, emb.shape[0])
    args.append(nc.dram_tensor("result", shape, F32, kind="ExternalOutput").ap())
    build(nc, *args)
    r = run_bass_kernel_spmd(nc, [{"in_" + k: v for k, v in arrays.items()}], core_ids=[0])
    return r.results[0]["result"].reshape(*x.shape, emb.shape[0])
```
